# Optimizing a Trainium2 kernel written in Bass

```python
import numpy as np
import jax
import jax.numpy as jnp

def _softmax(x, axis=-1):
    return jax.nn.softmax(x, axis=axis)

def _gelu(x):
    return jax.nn.gelu(x, approximate=True)

def _silu(x):
    return jax.nn.silu(x)

def _sigmoid(x):
    return jax.nn.sigmoid(x)

def _layernorm(x, axis=-1, eps=1e-05):
    m = jnp.mean(x, axis=axis, keepdims=True)
    v = jnp.var(x, axis=axis, keepdims=True)
    return (x - m) / jnp.sqrt(v + eps)

def _scatter_add(tgt, idx, src, axis=0):
    return tgt.at[idx].add(src)

def _segment_sum(src, seg, n):
    return jax.ops.segment_sum(src, seg, n)
kernel_name = 'mk_flamingo_gated_d4_seqx_r4_dfb574'

def setup_inputs(seed: int=0):
    np.random.seed(seed)
    _w = jnp.asarray

    def _rec_inputs():
        import jax
        import jax.numpy as jnp
        _rk = jax.random.key(seed)
        x = -0.0002928 + 1 * jax.random.normal(jax.random.fold_in(_rk, 1), (16, 128, 256), jnp.float32)
        _lenS = 128 - jax.random.randint(jax.random.fold_in(_rk, 7), (16,), 0, max(1, 128 // 4) + 1, jnp.int32)
        _lenS2 = 128 - jax.random.randint(jax.random.fold_in(_rk, 8), (16,), 0, max(1, 128 // 4) + 1, jnp.int32)
        _ctx_1024P = jax.random.normal(jax.random.fold_in(_rk, 11), (16, 16, 256), jnp.float32)
        _ctx_1024c = jax.random.dirichlet(jax.random.fold_in(_rk, 511), 0.3 * jnp.ones((16,), jnp.float32), (16, 128))
        _ctx_1024t = jnp.einsum('bsk,bkd->bsd', _ctx_1024c, _ctx_1024P)
        _ctx_1024t = _ctx_1024t * jax.lax.rsqrt(jnp.mean(jnp.square(_ctx_1024t)) + 1e-12) * 0.953939
        ctx_1024 = -1.39393e-06 + 0.999914 * (_ctx_1024t + 0.3 * jax.random.normal(jax.random.fold_in(_rk, 611), (16, 128, 256), jnp.float32))
        _validS = jnp.arange(128)[None, :] < _lenS[:, None]
        _validS2 = jnp.arange(128)[None, :] < _lenS2[:, None]
        _causal = jnp.tril(jnp.ones((128, 128), dtype=bool))
        mask_Bx1x1xS2_ik0 = jnp.where(jnp.broadcast_to(_validS2[:, None, None, :], (16, 1, 1, 128)), 0, 1).astype(jnp.int32)
        mask_BxS_ff1 = jnp.where(jnp.ones((16, 128), dtype=bool), 1.0, 0.0).astype(jnp.float32)
        mask_BxS2_ik0 = jnp.where(jnp.broadcast_to(_validS2[:, :], (16, 128)), 0, 1).astype(jnp.int32)
        _g = jax.random.normal(jax.random.fold_in(_rk, 9001), (2, 4), jnp.float32)
        _g = jnp.sign(_g) * jnp.maximum(jnp.abs(_g), 1.0) + (_g == 0) * 1.0
        g_xattn = _g[0]
        g_ffn = _g[1]
        return (x, ctx_1024, mask_Bx1x1xS2_ik0, mask_BxS_ff1, mask_BxS2_ik0, g_xattn, g_ffn)
    x, ctx_1024, mask_Bx1x1xS2_ik0, mask_BxS_ff1, mask_BxS2_ik0, g_xattn, g_ffn = _rec_inputs()

    def _L0_xattn_setup():
        import jax, jax.numpy as jnp
        import numpy as np
        B, T, C = (2, 512, 256)
        NUM_HEADS, QK_LEN, V_LEN = (16, 64, 64)

        def _split_heads(x, n_heads, d):
            b, t, _ = x.shape
            return x.reshape(b, t, n_heads, d).transpose(0, 2, 1, 3)
        key = jax.random.key(seed)
        ks = jax.random.split(key, 11)
        s = 0.02
        return {'Q': jax.random.normal(ks[0], (B, T, C), jnp.float32), 'K': jax.random.normal(ks[1], (B, T, C), jnp.float32), 'V': jax.random.normal(ks[2], (B, T, C), jnp.float32), 'Wq': jax.random.normal(ks[3], (C, NUM_HEADS * QK_LEN), jnp.float32) * s, 'bq': jnp.zeros((NUM_HEADS * QK_LEN,), jnp.float32), 'Wk': jax.random.normal(ks[4], (C, NUM_HEADS * QK_LEN), jnp.float32) * s, 'bk': jnp.zeros((NUM_HEADS * QK_LEN,), jnp.float32), 'Wv': jax.random.normal(ks[5], (C, NUM_HEADS * V_LEN), jnp.float32) * s, 'bv': jnp.zeros((NUM_HEADS * V_LEN,), jnp.float32), 'Wo': jax.random.normal(ks[6], (NUM_HEADS * V_LEN, C), jnp.float32) * s, 'bo': jnp.zeros((C,), jnp.float32)}
    _L0_xattn_all = _L0_xattn_setup()
    _L0_xattn_in = {k: v for k, v in _L0_xattn_all.items() if k in ('Wq', 'bq', 'Wk', 'bk', 'Wv', 'bv', 'Wo', 'bo')}
    del _L0_xattn_all

    def _L0_ffn_setup():
        import jax, jax.numpy as jnp
        import numpy as np
        IN_F = 256
        OUT_F = 256
        B, S = (8, 1024)

        def _pack_ternary(tern):
            enc = (tern + 1.0).astype(jnp.int32).reshape(-1)
            return (enc[0::4] | enc[1::4] << 2 | enc[2::4] << 4 | enc[3::4] << 6).astype(jnp.int32)
        key = jax.random.key(seed)
        kx, kw = jax.random.split(key)
        x = jax.random.normal(kx, (B, S, IN_F), dtype=jnp.float32)
        w = jax.random.normal(kw, (OUT_F, IN_F), dtype=jnp.float32) * 0.02
        scale = jnp.maximum(jnp.mean(jnp.abs(w)), 1e-05)
        wn = w / scale
        tern = jnp.sign(wn) * (jnp.abs(wn) > 0.5).astype(jnp.float32)
        packed = _pack_ternary(tern)
        bias = jnp.zeros((OUT_F,), dtype=jnp.float32)
        return {'x': x, 'packed_weight': packed, 'weight_scale': scale.reshape(1), 'bias': bias}
    _L0_ffn_all = _L0_ffn_setup()
    _L0_ffn_in = {k: v for k, v in _L0_ffn_all.items() if k in ('packed_weight', 'weight_scale', 'bias')}
    del _L0_ffn_all

    def _L1_xattn_setup():
        import jax, jax.numpy as jnp
        import numpy as np
        BS, SEQ, D_MODEL, N_HEADS = (4, 512, 256, 16)
        D_HEAD = D_MODEL // N_HEADS

        def _split_heads(x):
            b, s, _ = x.shape
            return x.reshape(b, s, N_HEADS, D_HEAD).transpose(0, 2, 1, 3)
        key = jax.random.key(seed)
        ks = jax.random.split(key, 12)
        s = 1.0 / np.sqrt(D_MODEL)
        return {'Q': jax.random.normal(ks[0], (BS, SEQ, D_MODEL), jnp.float32), 'K': jax.random.normal(ks[1], (BS, SEQ, D_MODEL), jnp.float32), 'V': jax.random.normal(ks[2], (BS, SEQ, D_MODEL), jnp.float32), 'mask': jax.random.randint(ks[3], (BS, 1, 1, SEQ), 0, 2, jnp.int32), 'Wq': jax.random.normal(ks[4], (D_MODEL, D_MODEL), jnp.float32) * s, 'bq': jnp.zeros((D_MODEL,), jnp.float32), 'Wk': jax.random.normal(ks[5], (D_MODEL, D_MODEL), jnp.float32) * s, 'bk': jnp.zeros((D_MODEL,), jnp.float32), 'Wv': jax.random.normal(ks[6], (D_MODEL, D_MODEL), jnp.float32) * s, 'bv': jnp.zeros((D_MODEL,), jnp.float32), 'Wo': jax.random.normal(ks[7], (D_MODEL, D_MODEL), jnp.float32) * s, 'bo': jnp.zeros((D_MODEL,), jnp.float32)}
    _L1_xattn_all = _L1_xattn_setup()
    _L1_xattn_in = {k: v for k, v in _L1_xattn_all.items() if k in ('Wq', 'bq', 'Wk', 'bk', 'Wv', 'bv', 'Wo', 'bo')}
    del _L1_xattn_all

    def _L1_ffn_setup():
        import jax, jax.numpy as jnp
        import numpy as np
        E, D, F, GATE_DIM = (8, 256, 1024, 16)
        B, T = (2, 512)
        key = jax.random.key(seed)
        ks = jax.random.split(key, 7)
        s = 0.02
        return {'hidden_states': jax.random.normal(ks[0], (B, T, D), dtype=jnp.float32), 'w_red': jax.random.normal(ks[1], (D, GATE_DIM), dtype=jnp.float32) * s, 'wg': jax.random.normal(ks[2], (E, GATE_DIM), dtype=jnp.float32), 'w1': jax.random.normal(ks[3], (E, D, F), dtype=jnp.float32) * s, 'b1': jax.random.normal(ks[4], (E, F), dtype=jnp.float32) * s, 'w2': jax.random.normal(ks[5], (E, F, D), dtype=jnp.float32) * s, 'b2': jax.random.normal(ks[6], (E, D), dtype=jnp.float32) * s}
    _L1_ffn_all = _L1_ffn_setup()
    _L1_ffn_in = {k: v for k, v in _L1_ffn_all.items() if k in ('w_red', 'wg', 'w1', 'b1', 'w2', 'b2')}
    del _L1_ffn_all

    def _L2_xattn_setup():
        import jax, jax.numpy as jnp
        import numpy as np
        B, F, T, D = (8, 64, 32, 256)
        NEG = -1e+30
        key = jax.random.key(seed)
        ks = jax.random.split(key, 10)
        s = 1.0 / np.sqrt(D)
        return {'features': jax.random.normal(ks[0], (B, F, D), jnp.float32), 'masks': jnp.ones((B, F), jnp.float32), 'textual_features': jax.random.normal(ks[1], (B, T, D), jnp.float32), 'q_masks': jax.random.randint(ks[2], (B, T), 0, 2, jnp.int32), 'Ws': jax.random.normal(ks[3], (D, D), jnp.float32) * s, 'W': jax.random.normal(ks[4], (D, D), jnp.float32) * s, 'w': jax.random.normal(ks[5], (D, 1), jnp.float32) * s, 'b': jax.random.normal(ks[6], (1, D), jnp.float32) * s, 'Wcw': jax.random.normal(ks[7], (1, D), jnp.float32) * s, 'bcw': jnp.zeros((1,), jnp.float32), 'Wcb': jax.random.normal(ks[8], (1, D), jnp.float32) * s, 'bcb': jnp.zeros((1,), jnp.float32)}
    _L2_xattn_all = _L2_xattn_setup()
    _L2_xattn_in = {k: v for k, v in _L2_xattn_all.items() if k in ('Ws', 'W', 'w', 'b', 'Wcw', 'bcw', 'Wcb', 'bcb')}
    del _L2_xattn_all

    def _L2_ffn_setup():
        import jax, jax.numpy as jnp
        import numpy as np
        QB = 127.0
        EPS = 1e-05

        def _ste(x, q):
            return x + jax.lax.stop_gradient(q - x)

        def bitlinear(x, W, b):
            w_scale = jnp.clip(jnp.mean(jnp.abs(W)), EPS, None)
            Wq = _ste(W, jnp.clip(jnp.round(W / w_scale), -1.0, 1.0) * w_scale)
            x_scale = jnp.clip(jnp.max(jnp.abs(x), axis=-1, keepdims=True), EPS, None)
            xq = _ste(x, jnp.clip(jnp.round(x * (QB / x_scale)), -QB - 1.0, QB) * (x_scale / QB))
            return jnp.einsum('bnd,hd->bnh', xq, Wq) + b
        key = jax.random.key(seed)
        k0, k1, k2 = jax.random.split(key, 3)
        B, N, D = (8, 1024, 256)
        H = int(D * 4.0)
        x = jax.random.normal(k0, (B, N, D), dtype=jnp.float32)
        W1 = jax.random.normal(k1, (H, D), dtype=jnp.float32) * 0.02
        b1 = jnp.zeros((H,), dtype=jnp.float32)
        W2 = jax.random.normal(k2, (D, H), dtype=jnp.float32) * 0.02
        b2 = jnp.zeros((D,), dtype=jnp.float32)
        return {'x': x, 'W1': W1, 'b1': b1, 'W2': W2, 'b2': b2}
    _L2_ffn_all = _L2_ffn_setup()
    _L2_ffn_in = {k: v for k, v in _L2_ffn_all.items() if k in ('W1', 'b1', 'W2', 'b2')}
    del _L2_ffn_all

    def _L3_xattn_setup():
        import jax, jax.numpy as jnp
        import numpy as np
        H, DK, DV = (16, 64, 64)
        MEM = 128
        D_MODEL = 256
        OUT_DIM = 256
        key = jax.random.key(seed)
        ks = jax.random.split(key, 12)
        B, S = (2, 512)
        scale = 1.0 / np.sqrt(D_MODEL)
        inp = {'queries': jax.random.normal(ks[0], (B, S, D_MODEL), jnp.float32), 'keys': jax.random.normal(ks[1], (B, S, D_MODEL), jnp.float32), 'values': jax.random.normal(ks[2], (B, S, D_MODEL), jnp.float32), 'wq_w': jax.random.normal(ks[3], (D_MODEL, H * DK), jnp.float32) * scale, 'wq_b': jnp.zeros((H * DK,), jnp.float32), 'wk_w': jax.random.normal(ks[4], (D_MODEL, H * DK), jnp.float32) * scale, 'wk_b': jnp.zeros((H * DK,), jnp.float32), 'wv_w': jax.random.normal(ks[5], (D_MODEL, H * DV), jnp.float32) * scale, 'wv_b': jnp.zeros((H * DV,), jnp.float32), 'mk': jax.random.normal(ks[6], (1, MEM, H * DK), jnp.float32) * (0.1 / DK), 'mv': jax.random.normal(ks[7], (1, MEM, H * DV), jnp.float32) * (0.1 / MEM), 'wo_w': jax.random.normal(ks[8], (H * DV, OUT_DIM), jnp.float32) * (1.0 / np.sqrt(H * DV)), 'wo_b': jnp.zeros((OUT_DIM,), jnp.float32)}
        return inp
    _L3_xattn_all = _L3_xattn_setup()
    _L3_xattn_in = {k: v for k, v in _L3_xattn_all.items() if k in ('wq_w', 'wq_b', 'wk_w', 'wk_b', 'wv_w', 'wv_b', 'mk', 'mv', 'wo_w', 'wo_b')}
    del _L3_xattn_all

    def _L3_ffn_setup():
        import jax, jax.numpy as jnp
        import numpy as np
        TOP_K = 2
        key = jax.random.key(seed)
        ks = jax.random.split(key, 5)
        B, T, D, F, E = (4, 512, 256, 1024, 8)
        s = 0.02
        return {'x': jax.random.normal(ks[0], (B, T, D), jnp.float32), 'gate_w': jax.random.normal(ks[1], (D, E), jnp.float32) * s, 'w1': jax.random.normal(ks[2], (E, D, F), jnp.float32) * s, 'w3': jax.random.normal(ks[3], (E, D, F), jnp.float32) * s, 'w2': jax.random.normal(ks[4], (E, F, D), jnp.float32) * s}
    _L3_ffn_all = _L3_ffn_setup()
    _L3_ffn_in = {k: v for k, v in _L3_ffn_all.items() if k in ('gate_w', 'w1', 'w3', 'w2')}
    del _L3_ffn_all
    return {'x': x, 'ctx_1024': ctx_1024, 'mask_Bx1x1xS2_ik0': mask_Bx1x1xS2_ik0, 'mask_BxS_ff1': mask_BxS_ff1, 'mask_BxS2_ik0': mask_BxS2_ik0, 'g_xattn': g_xattn, 'g_ffn': g_ffn, 'L0_xattn_Wq': _L0_xattn_in['Wq'], 'L0_xattn_bq': _L0_xattn_in['bq'], 'L0_xattn_Wk': _L0_xattn_in['Wk'], 'L0_xattn_bk': _L0_xattn_in['bk'], 'L0_xattn_Wv': _L0_xattn_in['Wv'], 'L0_xattn_bv': _L0_xattn_in['bv'], 'L0_xattn_Wo': _L0_xattn_in['Wo'], 'L0_xattn_bo': _L0_xattn_in['bo'], 'L0_ffn_packed_weight': _L0_ffn_in['packed_weight'], 'L0_ffn_weight_scale': _L0_ffn_in['weight_scale'], 'L0_ffn_bias': _L0_ffn_in['bias'], 'L1_xattn_Wq': _L1_xattn_in['Wq'], 'L1_xattn_bq': _L1_xattn_in['bq'], 'L1_xattn_Wk': _L1_xattn_in['Wk'], 'L1_xattn_bk': _L1_xattn_in['bk'], 'L1_xattn_Wv': _L1_xattn_in['Wv'], 'L1_xattn_bv': _L1_xattn_in['bv'], 'L1_xattn_Wo': _L1_xattn_in['Wo'], 'L1_xattn_bo': _L1_xattn_in['bo'], 'L1_ffn_w_red': _L1_ffn_in['w_red'], 'L1_ffn_wg': _L1_ffn_in['wg'], 'L1_ffn_w1': _L1_ffn_in['w1'], 'L1_ffn_b1': _L1_ffn_in['b1'], 'L1_ffn_w2': _L1_ffn_in['w2'], 'L1_ffn_b2': _L1_ffn_in['b2'], 'L2_xattn_Ws': _L2_xattn_in['Ws'], 'L2_xattn_W': _L2_xattn_in['W'], 'L2_xattn_w': _L2_xattn_in['w'], 'L2_xattn_b': _L2_xattn_in['b'], 'L2_xattn_Wcw': _L2_xattn_in['Wcw'], 'L2_xattn_bcw': _L2_xattn_in['bcw'], 'L2_xattn_Wcb': _L2_xattn_in['Wcb'], 'L2_xattn_bcb': _L2_xattn_in['bcb'], 'L2_ffn_W1': _L2_ffn_in['W1'], 'L2_ffn_b1': _L2_ffn_in['b1'], 'L2_ffn_W2': _L2_ffn_in['W2'], 'L2_ffn_b2': _L2_ffn_in['b2'], 'L3_xattn_wq_w': _L3_xattn_in['wq_w'], 'L3_xattn_wq_b': _L3_xattn_in['wq_b'], 'L3_xattn_wk_w': _L3_xattn_in['wk_w'], 'L3_xattn_wk_b': _L3_xattn_in['wk_b'], 'L3_xattn_wv_w': _L3_xattn_in['wv_w'], 'L3_xattn_wv_b': _L3_xattn_in['wv_b'], 'L3_xattn_mk': _L3_xattn_in['mk'], 'L3_xattn_mv': _L3_xattn_in['mv'], 'L3_xattn_wo_w': _L3_xattn_in['wo_w'], 'L3_xattn_wo_b': _L3_xattn_in['wo_b'], 'L3_ffn_gate_w': _L3_ffn_in['gate_w'], 'L3_ffn_w1': _L3_ffn_in['w1'], 'L3_ffn_w3': _L3_ffn_in['w3'], 'L3_ffn_w2': _L3_ffn_in['w2']}

def reference(x, ctx_1024, mask_Bx1x1xS2_ik0, mask_BxS_ff1, mask_BxS2_ik0, g_xattn, g_ffn, L0_xattn_Wq, L0_xattn_bq, L0_xattn_Wk, L0_xattn_bk, L0_xattn_Wv, L0_xattn_bv, L0_xattn_Wo, L0_xattn_bo, L0_ffn_packed_weight, L0_ffn_weight_scale, L0_ffn_bias, L1_xattn_Wq, L1_xattn_bq, L1_xattn_Wk, L1_xattn_bk, L1_xattn_Wv, L1_xattn_bv, L1_xattn_Wo, L1_xattn_bo, L1_ffn_w_red, L1_ffn_wg, L1_ffn_w1, L1_ffn_b1, L1_ffn_w2, L1_ffn_b2, L2_xattn_Ws, L2_xattn_W, L2_xattn_w, L2_xattn_b, L2_xattn_Wcw, L2_xattn_bcw, L2_xattn_Wcb, L2_xattn_bcb, L2_ffn_W1, L2_ffn_b1, L2_ffn_W2, L2_ffn_b2, L3_xattn_wq_w, L3_xattn_wq_b, L3_xattn_wk_w, L3_xattn_wk_b, L3_xattn_wv_w, L3_xattn_wv_b, L3_xattn_mk, L3_xattn_mv, L3_xattn_wo_w, L3_xattn_wo_b, L3_ffn_gate_w, L3_ffn_w1, L3_ffn_w3, L3_ffn_w2):
    import jax
    import jax.numpy as jnp

    def _L0_xattn_ref(Q, K, V, Wq, bq, Wk, bk, Wv, bv, Wo, bo):
        import jax, jax.numpy as jnp
        import numpy as np
        B, T, C = (2, 512, 256)
        NUM_HEADS, QK_LEN, V_LEN = (16, 64, 64)

        def _split_heads(x, n_heads, d):
            b, t, _ = x.shape
            return x.reshape(b, t, n_heads, d).transpose(0, 2, 1, 3)
        q = _split_heads(Q @ Wq + bq, NUM_HEADS, QK_LEN)
        k = _split_heads(K @ Wk + bk, NUM_HEADS, QK_LEN)
        v = _split_heads(V @ Wv + bv, NUM_HEADS, V_LEN)
        scale = 1.0 / jnp.sqrt(jnp.asarray(QK_LEN, q.dtype))
        scores = jnp.einsum('bhqd,bhkd->bhqk', q, k) * scale
        attn = jax.nn.softmax(scores, axis=-1)
        out = jnp.einsum('bhqk,bhkd->bhqd', attn, v)
        out = out.transpose(0, 2, 1, 3).reshape(Q.shape[0], Q.shape[1], NUM_HEADS * V_LEN)
        return out @ Wo + bo

    def _L0_ffn_ref(x, packed_weight, weight_scale, bias):
        import jax, jax.numpy as jnp
        import numpy as np
        IN_F = 256
        OUT_F = 256
        B, S = (8, 1024)

        def _pack_ternary(tern):
            enc = (tern + 1.0).astype(jnp.int32).reshape(-1)
            return (enc[0::4] | enc[1::4] << 2 | enc[2::4] << 4 | enc[3::4] << 6).astype(jnp.int32)
        n = OUT_F * IN_F
        shifts = jnp.array([0, 2, 4, 6], dtype=jnp.int32)
        enc = (packed_weight[None, :] >> shifts[:, None] & 3).reshape(-1)[:n]
        w = (enc.astype(jnp.float32) - 1.0).reshape(OUT_F, IN_F) * weight_scale
        act_scale = 127.0 / jnp.maximum(jnp.max(jnp.abs(x), axis=-1, keepdims=True), 1e-05)
        x_dq = jnp.clip(jnp.round(x * act_scale), -128.0, 127.0) / act_scale
        return jnp.einsum('bsi,oi->bso', x_dq, w) + bias

    def _L1_xattn_ref(Q, K, V, mask, Wq, bq, Wk, bk, Wv, bv, Wo, bo):
        import jax, jax.numpy as jnp
        import numpy as np
        BS, SEQ, D_MODEL, N_HEADS = (4, 512, 256, 16)
        D_HEAD = D_MODEL // N_HEADS

        def _split_heads(x):
            b, s, _ = x.shape
            return x.reshape(b, s, N_HEADS, D_HEAD).transpose(0, 2, 1, 3)
        q = _split_heads(Q @ Wq.T + bq)
        k = _split_heads(K @ Wk.T + bk)
        v = _split_heads(V @ Wv.T + bv)
        scores = jnp.einsum('bhqd,bhkd->bhqk', q, k) / np.sqrt(D_HEAD).astype(np.float32)
        scores = jnp.where(mask == 0, jnp.float32(-1000000000.0), scores)
        attn = jax.nn.softmax(scores, axis=-1)
        ctx = jnp.einsum('bhqk,bhkd->bhqd', attn, v)
        b, h, s, d = ctx.shape
        ctx = ctx.transpose(0, 2, 1, 3).reshape(b, s, h * d)
        return ctx @ Wo.T + bo

    def _L1_ffn_ref(hidden_states, w_red, wg, w1, b1, w2, b2):
        import jax, jax.numpy as jnp
        import numpy as np
        E, D, F, GATE_DIM = (8, 256, 1024, 16)
        B, T = (2, 512)
        b, t, c = hidden_states.shape
        x = hidden_states.reshape(-1, c)
        red = x @ w_red
        wg_n = wg / jnp.maximum(jnp.linalg.norm(wg, axis=1, keepdims=True), 0.0001)
        logits = red @ wg_n.T
        gates = jax.nn.softmax(logits, axis=1)
        idx = jnp.argmax(gates, axis=1)
        scores = jnp.take_along_axis(gates, idx[:, None], axis=1)
        h = jax.nn.gelu(jnp.einsum('td,edf->etf', x, w1) + b1[:, None, :], approximate=False)
        y = jnp.einsum('etf,efd->etd', h, w2) + b2[:, None, :]
        out = jnp.take_along_axis(y, idx[None, :, None], axis=0)[0]
        out = out * scores
        return out.reshape(b, t, c)

    def _L2_xattn_ref(features, masks, textual_features, q_masks, Ws, W, w, b, Wcw, bcw, Wcb, bcb):
        import jax, jax.numpy as jnp
        import numpy as np
        B, F, T, D = (8, 64, 32, 256)
        NEG = -1e+30
        txt_proj = jnp.einsum('btd,de->bte', textual_features, Ws)
        feat_proj = jnp.einsum('bfd,de->bfe', features, W)
        h = jnp.tanh(txt_proj[:, None, :, :] + feat_proj[:, :, None, :] + b[None, None, :, :][..., 0, :])
        rho = jnp.einsum('bftd,d->bft', h, w[:, 0])
        qm = q_masks.astype(jnp.float32)
        rho = rho + (1.0 - qm)[:, None, :] * NEG
        att = jax.nn.softmax(rho, axis=-1)
        txt_h = jnp.einsum('bft,btd->bfd', att, textual_features)
        w_s = jnp.tanh(jnp.einsum('bfd,od->bfo', txt_h, Wcw) + bcw)
        b_s = jnp.tanh(jnp.einsum('bfd,od->bfo', txt_h, Wcb) + bcb)
        return w_s * features + b_s

    def _L2_ffn_ref(x, W1, b1, W2, b2):
        import jax, jax.numpy as jnp
        import numpy as np
        QB = 127.0
        EPS = 1e-05

        def _ste(x, q):
            return x + jax.lax.stop_gradient(q - x)

        def bitlinear(x, W, b):
            w_scale = jnp.clip(jnp.mean(jnp.abs(W)), EPS, None)
            Wq = _ste(W, jnp.clip(jnp.round(W / w_scale), -1.0, 1.0) * w_scale)
            x_scale = jnp.clip(jnp.max(jnp.abs(x), axis=-1, keepdims=True), EPS, None)
            xq = _ste(x, jnp.clip(jnp.round(x * (QB / x_scale)), -QB - 1.0, QB) * (x_scale / QB))
            return jnp.einsum('bnd,hd->bnh', xq, Wq) + b
        h = bitlinear(x, W1, b1)
        h = jax.nn.gelu(h, approximate=False)
        return bitlinear(h, W2, b2)

    def _L3_xattn_ref(queries, keys, values, wq_w, wq_b, wk_w, wk_b, wv_w, wv_b, mk, mv, wo_w, wo_b):
        import jax, jax.numpy as jnp
        import numpy as np
        H, DK, DV = (16, 64, 64)
        MEM = 128
        D_MODEL = 256
        OUT_DIM = 256
        B, S, _ = queries.shape
        q = (queries @ wq_w + wq_b).reshape(B, S, H, DK).transpose(0, 2, 1, 3)
        k_proj = keys @ wk_w + wk_b
        v_proj = values @ wv_w + wv_b
        k_ext = jnp.concatenate([k_proj, jnp.broadcast_to(mk, (B, MEM, H * DK))], axis=1)
        v_ext = jnp.concatenate([v_proj, jnp.broadcast_to(mv, (B, MEM, H * DV))], axis=1)
        T = S + MEM
        k = k_ext.reshape(B, T, H, DK).transpose(0, 2, 1, 3)
        v = v_ext.reshape(B, T, H, DV).transpose(0, 2, 1, 3)
        scores = jnp.einsum('bhsd,bhtd->bhst', q, k) / jnp.sqrt(jnp.float32(DK))
        attn = jax.nn.softmax(scores, axis=-1)
        out = jnp.einsum('bhst,bhtd->bhsd', attn, v)
        out = out.transpose(0, 2, 1, 3).reshape(B, S, H * DV)
        return out @ wo_w + wo_b

    def _L3_ffn_ref(x, gate_w, w1, w3, w2):
        import jax, jax.numpy as jnp
        import numpy as np
        TOP_K = 2
        logits = jnp.einsum('btd,de->bte', x, gate_w)
        probs = jax.nn.softmax(logits, axis=-1)
        expert_weights, expert_indices = jax.lax.top_k(probs, TOP_K)
        expert_weights = expert_weights / expert_weights.sum(-1, keepdims=True)
        E = w1.shape[0]
        out = jnp.zeros_like(x)
        for i in range(E):
            wi = jnp.where(expert_indices == i, expert_weights, 0.0).sum(-1)
            h = jax.nn.silu(jnp.einsum('btd,df->btf', x, w1[i])) * jnp.einsum('btd,df->btf', x, w3[i])
            out = out + jnp.einsum('btf,fd->btd', h, w2[i]) * wi[..., None]
        return out
    x = x + jnp.tanh(g_xattn[0]) * _L0_xattn_ref(_layernorm(x, axis=-1), ctx_1024, ctx_1024, L0_xattn_Wq, L0_xattn_bq, L0_xattn_Wk, L0_xattn_bk, L0_xattn_Wv, L0_xattn_bv, L0_xattn_Wo, L0_xattn_bo)
    x = x + jnp.tanh(g_ffn[0]) * _L0_ffn_ref(_layernorm(x, axis=-1), L0_ffn_packed_weight, L0_ffn_weight_scale, L0_ffn_bias)
    x = x + jnp.tanh(g_xattn[1]) * _L1_xattn_ref(_layernorm(x, axis=-1), ctx_1024, ctx_1024, mask_Bx1x1xS2_ik0, L1_xattn_Wq, L1_xattn_bq, L1_xattn_Wk, L1_xattn_bk, L1_xattn_Wv, L1_xattn_bv, L1_xattn_Wo, L1_xattn_bo)
    x = x + jnp.tanh(g_ffn[1]) * _L1_ffn_ref(_layernorm(x, axis=-1), L1_ffn_w_red, L1_ffn_wg, L1_ffn_w1, L1_ffn_b1, L1_ffn_w2, L1_ffn_b2)
    x = x + jnp.tanh(g_xattn[2]) * _L2_xattn_ref(_layernorm(x, axis=-1), mask_BxS_ff1, ctx_1024, mask_BxS2_ik0, L2_xattn_Ws, L2_xattn_W, L2_xattn_w, L2_xattn_b, L2_xattn_Wcw, L2_xattn_bcw, L2_xattn_Wcb, L2_xattn_bcb)
    x = x + jnp.tanh(g_ffn[2]) * _L2_ffn_ref(_layernorm(x, axis=-1), L2_ffn_W1, L2_ffn_b1, L2_ffn_W2, L2_ffn_b2)
    x = x + jnp.tanh(g_xattn[3]) * _L3_xattn_ref(_layernorm(x, axis=-1), ctx_1024, ctx_1024, L3_xattn_wq_w, L3_xattn_wq_b, L3_xattn_wk_w, L3_xattn_wk_b, L3_xattn_wv_w, L3_xattn_wv_b, L3_xattn_mk, L3_xattn_mv, L3_xattn_wo_w, L3_xattn_wo_b)
    x = x + jnp.tanh(g_ffn[3]) * _L3_ffn_ref(_layernorm(x, axis=-1), L3_ffn_gate_w, L3_ffn_w1, L3_ffn_w3, L3_ffn_w2)
    return x

_drawn_inputs = setup_inputs


def setup_inputs(seed=0):
    import zlib

    import numpy as np

    out = dict(_drawn_inputs(seed))
    spreads = {'L0_xattn_bq': (0.0, 0.8),
     'L0_xattn_bk': (0.0, 2.0),
     'L0_xattn_bv': (0.0, 0.1),
     'L0_xattn_bo': (0.0, 0.1),
     'L0_ffn_bias': (0.0, 0.1),
     'L1_xattn_bq': (0.0, 0.366),
     'L1_xattn_bk': (0.0, 2.0),
     'L1_xattn_bv': (0.0, 0.1),
     'L1_xattn_bo': (0.0, 0.1),
     'L2_ffn_b1': (0.0, 0.632),
     'L2_ffn_b2': (0.0, 0.1),
     'L3_xattn_wq_b': (0.0, 0.8),
     'L3_xattn_wk_b': (0.0, 0.8),
     'L3_xattn_wv_b': (0.0, 0.1),
     'L3_xattn_wo_b': (0.0, 0.1)}
    factors = {'g_ffn': 8.0,
     'L0_xattn_Wq': 8.0,
     'L0_xattn_Wk': 8.0,
     'L1_ffn_w_red': 3.796,
     'L1_ffn_wg': 3.809,
     'L1_ffn_w1': 3.765,
     'L1_ffn_b1': 8.0,
     'L1_ffn_w2': 3.651,
     'L1_ffn_b2': 8.0,
     'L2_xattn_b': 25.371,
     'L3_xattn_mk': 184.571,
     'L3_xattn_mv': 200.0,
     'L3_ffn_gate_w': 4.377,
     'L3_ffn_w1': 3.873,
     'L3_ffn_w3': 3.817,
     'L3_ffn_w2': 3.819}
    for name, (base, spread) in spreads.items():
        noise = np.random.default_rng([zlib.crc32(name.encode()), seed]).standard_normal(out[name].shape)
        drawn = base * np.exp(spread * noise) if base else spread * noise
        out[name] = jnp.asarray(drawn.astype(out[name].dtype))
    for name, factor in factors.items():
        out[name] = (out[name] * factor).astype(out[name].dtype)
    return out
```

```python
from contextlib import ExitStack

import concourse.bass as bass
from concourse import mybir

ALU = mybir.AluOpType
ACT = mybir.ActivationFunctionType
AX = mybir.AxisListType
F32 = mybir.dt.float32
BF16 = mybir.dt.bfloat16
I32 = mybir.dt.int32

P = 128
B = 16
D = 256
DK = D // P
G = 4
NG = B // G
GT = G * P
H = 16
E = 8
F = 1024
FC = F // P
LN_EPS = 1e-5
ROUND = 12582912.0
BIG = 1e9


def ds(i, n):
    return bass.ds(i, n)


def build(nc, t, out, layers=range(8)):
    outer = ExitStack()
    with outer:
        passing = []

        def sem(name, stack=outer):
            h = nc.alloc_semaphore(name=name)
            if stack is not outer:
                passing.append(h)
            return h

        def semaphores_cleared():
            nc.clear_and_free_semaphores(list(passing))
            passing.clear()
            nc.all_engine_barrier()

        def sb(name, shape, dt=F32, stack=outer):
            return stack.enter_context(nc.sbuf_tensor(name, shape, dt))

        def banks(stack, names):
            return {n: stack.enter_context(nc.psum_tensor(n, [P, 512], F32)) for n in names}

        x = sb("x", [P, B, D])
        xnT = sb("xnT", [P, DK, B * P])
        ctxT = sb("ctxT", [P, DK, B * P])
        ident = sb("ident", [P, P])
        identb = sb("identb", [P, P], BF16)
        ones = sb("ones", [P, 512])
        gate = sb("gate", [P, 8])
        nhalf = sb("nhalf", [P, B])
        stats = sb("stats", [P, B, 6])
        mom = sb("mom", [P, 5, B])
        mean = sb("mean", [P, B])
        veps = sb("veps", [P, B])
        rstd = sb("rstd", [P, B])
        cols = sb("cols", [P, 96])
        wq = sb("wq", [P, DK, 1024])
        wk = sb("wk", [P, DK, 1024])
        wv = sb("wv", [P, DK, 1024])
        wo = sb("wo", [P, 8, D])
        wq1 = sb("wq1", [P, DK, 512])
        wk1 = sb("wk1", [P, DK, 512])
        wv1 = sb("wv1", [P, DK, D])
        wo1 = sb("wo1", [P, DK, D])
        rows1 = sb("rows1", [2, 2, 512])
        mrow = sb("mrow", [2, B * P])
        tern0 = sb("tern0", [P, DK, D], BF16)
        tern1 = sb("tern1", [P, DK, F], BF16)
        tern2 = sb("tern2", [P, FC, D], BF16)
        wscale = sb("wscale", [P, 4])

        s_x = sem("x_loaded")
        s_w0 = sem("w0_loaded")
        s_out = sem("out_stored")

        def setup():
            st = ExitStack()
            with st:
                S = lambda n: sem(n, st)
                ctx_in = sb("ctx_in", [P, 2, G, D], F32, st)
                brow = sb("brow", [96, P], F32, st)
                win = sb("win", [P, 4, DK, D], F32, st)
                packed = sb("packed", [64, D], I32, st)
                code = sb("code", [64, 4, D], I32, st)
                ternp = sb("ternp", [64, 4, D], BF16, st)
                w1in = sb("w1in", [P, FC, D], F32, st)
                w2in = sb("w2in", [P, DK, F], F32, st)
                absw = sb("absw", [P, 2], F32, st)
                q1 = sb("q1", [P, FC, D], BF16, st)
                q2 = sb("q2", [P, DK, F], BF16, st)
                mint = sb("mint", [2, B * P], I32, st)
                g_in = sb("g_in", [P, 8], F32, st)
                ps = banks(st, [f"set{i}" for i in range(6)])
                pf = [ps[f"set{i}"] for i in range(6)]
                pb = [st.enter_context(nc.psum_tensor(f"setb{i}", [P, 1024], BF16)) for i in range(2)]
                s_ctx = [S("ctx_even_loaded"), S("ctx_odd_loaded")]
                s_ctxT, s_ctxE = S("ctx_turned"), S("ctx_evacuated")
                s_small, s_win, s_packed, s_w12, s_pad = S("small_loaded"), S("w1x_loaded"), S("packed_loaded"), S("w12_loaded"), S("pads_zero")
                s_id, s_dve, s_turn, s_evac = S("ident_ready"), S("dve_step"), S("weight_turned"), S("weight_evacuated")
                s_rows = S("rows_loaded")
                s_sum, s_g = S("abs_summed"), S("g_step")
                s_q = S("ternary_ready")

                with nc.Block() as block:
                    @block.sync
                    def _(sp):
                        cv = t["ctx_1024"].rearrange("(g a) s d -> g s a d", a=G)
                        sp.dma_start(ctx_in[:, 0, :, :], cv[0]).then_inc(s_ctx[0], 16)
                        sp.dma_start(ctx_in[:, 1, :, :], cv[1]).then_inc(s_ctx[1], 16)
                        sp.dma_start(x[:, :, :], t["x"].rearrange("b s d -> s b d")).then_inc(s_x, 16)
                        for n in range(2, NG):
                            sp.wait_ge(s_ctxT, 2 * (n - 2) + 2)
                            sp.dma_start(ctx_in[:, n % 2, :, :], cv[n]).then_inc(s_ctx[n % 2], 16)
                        sp.dma_start(wq[:, :, :], t["L0_xattn_Wq"].rearrange("(k p) n -> p k n", p=P)).then_inc(s_w0, 16)
                        sp.dma_start(wk[:, :, :], t["L0_xattn_Wk"].rearrange("(k p) n -> p k n", p=P)).then_inc(s_w0, 16)
                        sp.dma_start(wv[:, :, :], t["L0_xattn_Wv"].rearrange("(k p) n -> p k n", p=P)).then_inc(s_w0, 16)
                        sp.dma_start(wo[:, :, :], t["L0_xattn_Wo"].rearrange("(k p) n -> p k n", p=P)).then_inc(s_w0, 16)
                        sp.dma_start(w1in[:, :, :], t["L2_ffn_W1"].rearrange("(k p) n -> p k n", p=P)).then_inc(s_w12, 16)
                        sp.dma_start(w2in[:, :, :], t["L2_ffn_W2"].rearrange("(k p) n -> p k n", p=P)).then_inc(s_w12, 16)

                    @block.gpsimd
                    def _(pool):
                        pool.memset(ident[:, :], 0.0).then_inc(s_id, 1)
                        pool.memset(ones[:, :], 1.0).then_inc(s_id, 1)
                        pool.wait_ge(s_id, 2)
                        pool.affine_select(out=ident[:, :], in_=ident[:, :], compare_op=ALU.not_equal, fill=1.0,
                                           base=0, pattern=[[-1, P]], channel_multiplier=1).then_inc(s_id, 1)
                        pool.wait_ge(s_id, 3)
                        pool.tensor_copy(identb[:, :], ident[:, :]).then_inc(s_id, 1)
                        pool.memset(nhalf[:, :], -0.5).then_inc(s_id, 1)
                        pool.memset(wq1[:, :, :], 0.0).then_inc(s_pad, 1)
                        pool.memset(wk1[:, :, :], 0.0).then_inc(s_pad, 1)
                        pool.memset(rows1[:, :, :], 0.0).then_inc(s_pad, 1)
                        pool.wait_ge(s_pad, 3)
                        r1 = rows1[:, :, :].rearrange("r a (h c) -> r a h c", c=32)
                        pool.memset(r1[0:1, 0, :, 16], 1.0).then_inc(s_pad, 1)
                        pool.memset(r1[0:1, 1, :, 16], 4.0 * BIG).then_inc(s_pad, 1)

                    @block.scalar
                    def _(act):
                        row = lambda a: a.rearrange("(c p) -> c p", p=P)
                        act.dma_start(brow[0:8, :], row(t["L0_xattn_bq"])).then_inc(s_small, 16)
                        act.dma_start(brow[8:16, :], row(t["L0_xattn_bk"])).then_inc(s_small, 16)
                        act.dma_start(brow[16:24, :], row(t["L3_xattn_wq_b"])).then_inc(s_small, 16)
                        act.dma_start(brow[24:32, :], row(t["L3_xattn_wk_b"])).then_inc(s_small, 16)
                        act.dma_start(brow[32:96, :], t["L1_ffn_b1"].rearrange("e (c p) -> (e c) p", p=P)).then_inc(s_small, 16)
                        act.dma_start(g_in[:, 0:4], t["g_xattn"].rearrange("(a n) -> a n", a=1).to_broadcast([P, 4])).then_inc(s_small, 16)
                        act.dma_start(g_in[:, 4:8], t["g_ffn"].rearrange("(a n) -> a n", a=1).to_broadcast([P, 4])).then_inc(s_small, 16)
                        act.dma_start(mint[:, :], t["mask_Bx1x1xS2_ik0"].rearrange("b i j s -> (i j) (b s)").to_broadcast([2, B * P])).then_inc(s_small, 16)
                        for n, w in enumerate(("Wq", "Wk", "Wv", "Wo")):
                            act.dma_start(win[:, n, :, :], t["L1_xattn_" + w].rearrange("(k p) n -> p k n", p=P)).then_inc(s_win, 16)
                        act.dma_start(packed[:, :], t["L0_ffn_packed_weight"].rearrange("(p n) -> p n", n=D)).then_inc(s_packed, 16)
                        act.wait_ge(s_pad, 5)
                        r1 = rows1[:, :, :].rearrange("r a (h c) -> r a h c", c=32)
                        act.dma_start(r1[0:1, 0, :, 0:16], t["L1_xattn_bq"].rearrange("(a h c) -> a h c", a=1, c=16)).then_inc(s_rows, 16)
                        act.dma_start(r1[1:2, 1, :, 0:16], t["L1_xattn_bk"].rearrange("(a h c) -> a h c", a=1, c=16)).then_inc(s_rows, 16)
                        act.wait_ge(s_small, 16 * 8)
                        act.activation(gate[:, :], g_in[:, :], ACT.Tanh).then_inc(s_g, 1)
                        for n in range(NG):
                            for k in range(DK):
                                act.wait_ge(s_ctxT, 2 * n + k + 1)
                                act.activation(ctxT[:, k, n * GT:(n + 1) * GT], pf[(2 * n + k) % 4][:, :], ACT.Copy).then_inc(s_ctxE, 1)
                        act.wait_ge(s_rows, 32)

                    jobs = []
                    for n, w in enumerate((wq1, wk1)):
                        for k in range(DK):
                            jobs.append(("f", [win[:, n, o, k * P:(k + 1) * P] for o in range(DK)],
                                         w[:, k, :].rearrange("p (h c) -> p h c", c=32)[:, :, 0:16],
                                         lambda ap: ap[:, 0:256].rearrange("p (h c) -> p h c", c=16), "win"))
                    for n, w in ((2, wv1), (3, wo1)):
                        for k in range(DK):
                            jobs.append(("f", [win[:, n, o, k * P:(k + 1) * P] for o in range(DK)],
                                         w[:, k, :], lambda ap: ap[:, 0:256], "win"))
                    jobs.append(("f", [brow[:, :]], cols[:, :], lambda ap: ap[:, 0:96], "rows"))
                    for k in range(DK):
                        jobs.append(("b", [ternp[:, s, k * P:(k + 1) * P] for s in range(4)],
                                     tern0[:, k, :], lambda ap: ap[:, 0:256], "tern"))
                    for k in range(DK):
                        for half in range(2):
                            jobs.append(("b", [q1[:, 4 * half + o, k * P:(k + 1) * P] for o in range(4)],
                                         tern1[:, k, half * 512:(half + 1) * 512], lambda ap: ap[:, 0:512], "q1"))
                    for k in range(FC):
                        jobs.append(("b", [q2[:, o, k * P:(k + 1) * P] for o in range(DK)],
                                     tern2[:, k, :], lambda ap: ap[:, 0:256], "q2"))
                    READY = {"win": (s_win, 64), "rows": (s_small, 128), "tern": (s_q, 4), "q1": (s_q, 5), "q2": (s_q, 6)}

                    @block.tensor
                    def _(pe):
                        pe.wait_ge(s_id, 5)
                        for n in range(NG):
                            pe.wait_ge(s_ctx[n % 2], 16 * (n // 2 + 1))
                            for k in range(DK):
                                if n >= 2:
                                    pe.wait_ge(s_ctxE, 2 * (n - 2) + k + 1)
                                for a in range(G):
                                    m = pe.transpose(pf[(2 * n + k) % 4][:, a * P:(a + 1) * P], ctx_in[:, n % 2, a, k * P:(k + 1) * P], ident[:, :])
                                m.then_inc(s_ctxT, 1)

                        def turn(n, kind, srcs, what):
                            pe.wait_ge(*READY[what])
                            if n >= 2:
                                pe.wait_ge(s_evac, n - 1)
                            bank = (pf[4:6] if kind == "f" else pb)[n % 2]
                            at = 0
                            for src in srcs:
                                rows, width = src.shape[0], src.shape[1]
                                m = pe.transpose(bank[0:width, at:at + rows], src, (ident if kind == "f" else identb)[0:rows, 0:rows])
                                at += rows
                            m.then_inc(s_turn, 1)

                        for n, (kind, srcs, _, _, what) in enumerate(jobs[:11]):
                            turn(n, kind, srcs, what)
                        pe.wait_ge(s_sum, 2)
                        pe.wait_ge(s_ctxE, 2 * NG)
                        pe.matmul(pf[0][:, 0:2], ones[:, 0:P], absw[:, :], start=True, stop=True).then_inc(s_sum, 1)
                        for n, (kind, srcs, _, _, what) in enumerate(jobs[11:]):
                            turn(n + 11, kind, srcs, what)

                    @block.vector
                    def _(v):
                        v.wait_ge(s_packed, 16)
                        for s in range(4):
                            nc.vector.tensor_scalar(code[:, s, :], packed[:, :], 2 * s, 3, ALU.logical_shift_right, ALU.bitwise_and).then_inc(s_dve, 1)
                        for s in range(4):
                            v.wait_ge(s_dve, s + 1)
                            nc.vector.tensor_scalar(ternp[:, s, :], code[:, s, :], -1.0, None, ALU.add).then_inc(s_q, 1)
                        v.wait_ge(s_small, 128)
                        v.wait_ge(s_id, 5)
                        nc.vector.tensor_scalar(mrow[:, :], mint[:, :], 0.0, ident[0:2, 0:1], ALU.not_equal, ALU.subtract).then_inc(s_dve, 1)
                        v.wait_ge(s_pad, 5)

                        def evac(n):
                            kind, _, dst, view, _ = jobs[n]
                            v.wait_ge(s_turn, n + 1)
                            bank = (pf[4:6] if kind == "f" else pb)[n % 2]
                            nc.vector.tensor_copy(dst, view(bank)).then_inc(s_evac, 1)

                        for n in range(11):
                            evac(n)
                        v.wait_ge(s_w12, 32)
                        nc.vector.tensor_reduce(absw[:, 0:1], w1in[:, :, :], AX.XY, ALU.add, apply_absolute_value=True).then_inc(s_sum, 1)
                        nc.vector.tensor_reduce(absw[:, 1:2], w2in[:, :, :], AX.XY, ALU.add, apply_absolute_value=True).then_inc(s_sum, 1)
                        v.wait_ge(s_sum, 3)
                        nc.vector.tensor_scalar(wscale[:, 0:2], pf[0][:, 0:2], 1.0 / (D * F), 1e-5, ALU.mult, ALU.max).then_inc(s_dve, 1)
                        v.wait_ge(s_dve, 6)
                        nc.vector.reciprocal(wscale[:, 2:4], wscale[:, 0:2]).then_inc(s_dve, 1)
                        v.wait_ge(s_dve, 7)
                        for n, (w, q) in enumerate(((w1in, q1), (w2in, q2))):
                            nc.vector.tensor_scalar(w[:, :, :], w[:, :, :], wscale[:, 2 + n:3 + n], ROUND, ALU.mult, ALU.add).then_inc(s_dve, 1)
                        for n, (w, q) in enumerate(((w1in, q1), (w2in, q2))):
                            v.wait_ge(s_dve, 8 + n)
                            nc.vector.tensor_scalar(w[:, :, :], w[:, :, :], ROUND, -1.0, ALU.subtract, ALU.max).then_inc(s_dve, 1)
                        for n, (w, q) in enumerate(((w1in, q1), (w2in, q2))):
                            v.wait_ge(s_dve, 10 + n)
                            nc.vector.tensor_scalar(q[:, :, :], w[:, :, :], 1.0, None, ALU.min).then_inc(s_q, 1)
                        for n in range(11, len(jobs)):
                            evac(n)

        def moments_vector(v, s_st, s_mo, s_step, before=0):
            with v.Fori(0, B) as b:
                nc.vector.bn_stats(stats[:, ds(b, 1), :].rearrange("p a c -> p (a c)"),
                                   x[:, ds(b, 1), :].rearrange("p a c -> p (a c)")).then_inc(s_st, 1)
            v.wait_ge(s_st, B)
            me, ve, mo, vo = (stats[:, :, i] for i in (1, 2, 4, 5))
            nc.vector.tensor_tensor(mom[:, 0, :], me, mo, ALU.add).then_inc(s_step, 1)
            nc.vector.tensor_tensor(mom[:, 1, :], me, mo, ALU.subtract).then_inc(s_step, 1)
            nc.vector.tensor_tensor(mom[:, 2, :], ve, vo, ALU.add).then_inc(s_step, 1)
            v.wait_ge(s_step, before + 1)
            nc.vector.tensor_scalar(mean[:, :], mom[:, 0, :], 0.5, None, ALU.mult).then_inc(s_step, 1)
            v.wait_ge(s_step, before + 2)
            nc.vector.scalar_tensor_tensor(out=mom[:, 3, :], in0=mom[:, 1, :], scalar=0.25, in1=mom[:, 1, :],
                                           op0=ALU.mult, op1=ALU.mult).then_inc(s_step, 1)
            v.wait_ge(s_step, before + 3)
            nc.vector.tensor_scalar(mom[:, 4, :], mom[:, 2, :], 1.0 / D, LN_EPS, ALU.mult, ALU.add).then_inc(s_step, 1)
            v.wait_ge(s_step, before + 6)
            nc.vector.tensor_tensor(veps[:, :], mom[:, 4, :], mom[:, 3, :], ALU.add).then_inc(s_mo, 1)

        def root_pool(pool, s_mo, s_rs):
            pool.wait_ge(s_mo, 1)
            pool.tensor_tensor(rstd[:, :], veps[:, :], nhalf[:, :], ALU.pow).then_inc(s_rs, 1)

        def norm_transposed(block, st, tag, keep=None):
            S = lambda n: sem(n + tag, st)
            xn = sb("xn" + tag, [P, 2, G, D], F32, st)
            ps = banks(st, [f"xt{i}" + tag for i in range(4)])
            pt = [ps[f"xt{i}" + tag] for i in range(4)]
            s_st, s_mo, s_step, s_rs = S("stats_done"), S("moments_done"), S("moment_step"), S("rstd_done")
            s_xn, s_turn, s_ev = S("xn_ready"), S("xn_turned"), S("xn_evacuated")

            @block.gpsimd
            def _(pool):
                root_pool(pool, s_mo, s_rs)

            @block.vector
            def _(v):
                moments_vector(v, s_st, s_mo, s_step)
                v.wait_ge(s_rs, 1)
                with v.Fori(0, NG // 2) as r:
                    for j in range(2):
                        v.wait_ge(s_turn, r * 4 + 2 * j + 2)
                        for a in range(G):
                            b = r * 8 + (G * j + a)
                            if keep is not None:
                                nc.vector.tensor_scalar(keep[:, ds(b, 1), :].rearrange("p a c -> p (a c)"), x[:, ds(b, 1), :].rearrange("p a c -> p (a c)"),
                                                        mean[:, ds(b, 1)], rstd[:, ds(b, 1)], ALU.subtract, ALU.mult)
                            m = nc.vector.tensor_scalar(xn[:, j, a, :], x[:, ds(b, 1), :].rearrange("p a c -> p (a c)"),
                                                        mean[:, ds(b, 1)], rstd[:, ds(b, 1)], ALU.subtract, ALU.mult)
                        m.then_inc(s_xn, 1)

            @block.tensor
            def _(pe):
                pe.sem_inc(s_turn, 4)
                with pe.Fori(0, NG // 2) as r:
                    for j in range(2):
                        pe.wait_ge(s_xn, r * 2 + j + 1)
                        for k in range(DK):
                            pe.wait_ge(s_ev, r * 4 + 2 * j + k + 1)
                            for a in range(G):
                                m = pe.transpose(pt[2 * j + k][:, a * P:(a + 1) * P], xn[:, j, a, k * P:(k + 1) * P], ident[:, :])
                            m.then_inc(s_turn, 1)

            @block.scalar
            def _(act):
                act.sem_inc(s_ev, 4)
                with act.Fori(0, NG // 2) as r:
                    for j in range(2):
                        for k in range(DK):
                            act.wait_ge(s_turn, r * 4 + 2 * j + k + 5)
                            act.activation(xnT[:, k, ds(r * 2 * GT + j * GT, GT)], pt[2 * j + k][:, :], ACT.Copy).then_inc(s_ev, 1)

        def attention(layer, tag):
            HP, DV, KT = {0: (64, 64, 1), 1: (32, 16, 1), 3: (64, 64, 2)}[layer]
            HC = P // HP
            NC = H // HC
            HU = 4 // KT
            U = H // HU
            N = G * U
            HO = min(H, 512 // DV)
            UO = HO // HU
            OC = H * DV // P
            OB = (OC + 3) // 4
            VH = (H * DV + 511) // 512
            VW = H * DV // VH
            qscale = {0: 0.125, 1: 0.25, 3: 0.125}[layer]
            Wq, Wk, Wv, Wo = (wq1, wk1, wv1, wo1) if layer == 1 else (wq, wk, wv, wo)
            bcol = {0: 0, 3: 16}.get(layer)
            st0 = ExitStack()
            with st0:
                with nc.Block() as block:
                    norm_transposed(block, st0, tag)
            st = ExitStack()
            with st:
                S = lambda n: sem(n + tag, st)
                qT = sb("qT" + tag, [P, NC, GT], F32, st)
                kT = sb("kT" + tag, [P, NC, GT], F32, st)
                cg = sb("cg" + tag, [P, DK, GT], F32, st)
                vv = sb("vv" + tag, [P, 2, H * DV], F32, st)
                prob = sb("prob" + tag, [P, 2, 512], F32, st)
                probT = sb("probT" + tag, [P, 2, 512], F32, st)
                nmax = sb("nmax" + tag, [P, 2, HU], F32, st)
                sums = sb("sums" + tag, [P, 2, H], F32, st)
                rinv = sb("rinv" + tag, [P, H], F32, st)
                o = sb("o" + tag, [P, 2, H * DV], F32, st)
                oT = sb("oT" + tag, [P, OC, P], F32, st)
                bv = sb("bv" + tag, [P, H * DV], F32, st)
                bo = sb("bo" + tag, [1, D], F32, st)
                bqs = sb("bqs" + tag, [P, 8], F32, st)
                ps = banks(st, [n + tag for n in ("pp0", "pp1", "ps0", "ps1", "pt0", "pt1", "po", "pw")])
                pp = [ps["pp0" + tag], ps["pp1" + tag]]
                psc = [ps["ps0" + tag], ps["ps1" + tag]]
                ptr = [ps["pt0" + tag], ps["pt1" + tag]]
                po, pw = ps["po" + tag], ps["pw" + tag]
                s_bias, s_bq = S("bias_loaded"), S("bq_scaled")
                s_cg = S("group_context_ready")
                s_p, s_pf = S("proj_ready"), S("proj_evacuated")
                s_w, s_wf = S("work_ready"), S("work_evacuated")
                s_s, s_nm, s_e = S("scores_ready"), S("nmax_ready"), S("probs_ready")
                s_t, s_tf = S("probs_turned"), S("turned_evacuated")
                s_pv = S("values_summed")
                s_r, s_of = S("rinv_ready"), S("out_normed")
                pre = "L%d_xattn_" % layer
                bv_d, bo_d = (t[pre + "wv_b"], t[pre + "wo_b"]) if layer == 3 else (t[pre + "bv"], t[pre + "bo"])
                NP = 2 * NC
                NW = G * (VH + OB + 1)
                NO = G * H // HO

                def plan():
                    after = {n: [] for n in range(-1, N + 4)}
                    after[-1].append(("v", 0))
                    for a in range(G):
                        if a + 1 < G:
                            after[a * U + 2].append(("v", a + 1))
                        last = a * U + U - 1
                        after[last + 3].append(("turn", a))
                        after[last + 4].append(("out", a))
                    return after
                after = plan()

                if layer == 1:
                    msk = sb("msk", [P, GT], I32, st)
                    val = sb("val", [P, GT], F32, st)
                    cm = sb("cm", [P, DK, GT], F32, st)
                    s_msk, s_val, s_cm = S("mask_loaded"), S("valid_ready"), S("masked_ready")
                if layer == 3:
                    mkT = sb("mkT", [P, 8, P], F32, st)
                    mv = sb("mv", [P, 1024], F32, st)
                    s_mem, s_memT, s_memE = S("memory_loaded"), S("memory_turned"), S("memory_keys_ready")
                    mk_in = o[:, 0, :]

                def head(u, i):
                    return u // HC * HC * HU + u % HC + HC * i

                def key(h, a, kt):
                    p0, c = HP * (h % HC), h // HC
                    return mkT[p0:p0 + HP, c, :] if kt else kT[p0:p0 + HP, c, a * P:(a + 1) * P]

                with nc.Block() as block:
                    @block.sync
                    def _(sp):
                        sp.dma_start(bv[:, :], bv_d.rearrange("(a n) -> a n", a=1).to_broadcast([P, H * DV])).then_inc(s_bias, 16)
                        sp.dma_start(bo[:, :], bo_d.rearrange("(a n) -> a n", a=1)).then_inc(s_bias, 16)
                        if layer == 3:
                            sp.dma_start(mk_in, t["L3_xattn_mk"][0]).then_inc(s_mem, 16)
                            sp.dma_start(mv[:, :], t["L3_xattn_mv"][0]).then_inc(s_mem, 16)
                        if layer == 1:
                            md = t["mask_Bx1x1xS2_ik0"].rearrange("b i j s -> (i j) (b s)")
                            with sp.Fori(0, NG) as g:
                                sp.wait_ge(s_val, g)
                                sp.dma_start(msk[:, :], md[:, ds(g * GT, GT)].to_broadcast([P, GT])).then_inc(s_msk, 16)

                    @block.gpsimd
                    def _(pool):
                        def group(g, first):
                            src = ctxT[:, :, ds(g * GT, GT)]
                            if not first:
                                pool.wait_ge(s_w, (g - 1) * NW + wv_last + 1)
                            pool.tensor_copy(cg[:, :, :], src).then_inc(s_cg, 1)
                        order = [u for n in sorted(after) for u in after[n]]
                        at, pos = {}, 0
                        for kind, a in order:
                            pos += {"v": VH, "turn": OB, "out": 1}[kind]
                            at[(kind, a)] = pos
                        wv_last = at[("v", G - 1)] - 1
                        group(0, True)
                        with pool.Fori(1, NG) as g:
                            group(g, False)

                    @block.tensor
                    def _(pe):
                        pe.sem_inc(s_t, 2)
                        if layer == 3:
                            pe.wait_ge(s_mem, 32)
                            for half in range(2):
                                for c in range(4):
                                    m = pe.transpose(ptr[half][:, c * P:(c + 1) * P], mk_in[:, (4 * half + c) * P:(4 * half + c + 1) * P], ident[:, :])
                                m.then_inc(s_memT, 1)
                            pe.wait_ge(s_memE, 2)
                        pe.wait_ge(s_bias, 32)
                        with pe.Fori(0, NG) as g:
                            for i in range(NP):
                                c, isk = i % NC, i // NC
                                pe.wait_ge(s_pf, g * NP + i + 1)
                                W = Wk if isk else Wq
                                for k in range(DK):
                                    if isk and layer == 1:
                                        if c == 0 and k == 0:
                                            pe.wait_ge(s_cm, g * DK + DK)
                                        src = cm[:, k, :]
                                    elif isk:
                                        src = ctxT[:, k, ds(g * GT, GT)]
                                    else:
                                        src = xnT[:, k, ds(g * GT, GT)]
                                    m = pe.matmul(pp[i % 2][:, :], W[:, k, c * P:(c + 1) * P], src,
                                                  start=(k == 0), stop=(k == DK - 1 and layer != 1))
                                if layer == 1 and isk:
                                    m = pe.matmul(pp[i % 2][:, :], rows1[0:2, 1, c * P:(c + 1) * P], mrow[0:2, ds(g * GT, GT)], start=False, stop=True)
                                elif layer == 1:
                                    m = pe.matmul(pp[i % 2][:, :], rows1[0:1, 0, c * P:(c + 1) * P], ones[0:1, :], start=False, stop=True)
                                m.then_inc(s_p, 1)
                            pe.wait_ge(s_cg, g + 1)
                            w = [0]

                            def work(kind, a):
                                if kind == "v":
                                    for half in range(VH):
                                        pe.wait_ge(s_wf, g * NW + w[0] + 1)
                                        for k in range(DK):
                                            m = pe.matmul(pw[:, 0:VW], cg[:, k, a * P:(a + 1) * P], Wv[:, k, half * VW:(half + 1) * VW],
                                                          start=(k == 0), stop=(k == DK - 1))
                                        m.then_inc(s_w, 1)
                                        w[0] += 1
                                elif kind == "turn":
                                    pe.wait_ge(s_of, (g * NO) + (a + 1) * H // HO + 1)
                                    for ob in range(OB):
                                        pe.wait_ge(s_wf, g * NW + w[0] + 1)
                                        for c in range(4 * ob, min(4 * ob + 4, OC)):
                                            m = pe.transpose(pw[:, (c % 4) * P:(c % 4 + 1) * P], o[:, a % 2, c * P:(c + 1) * P], ident[:, :])
                                        m.then_inc(s_w, 1)
                                        w[0] += 1
                                else:
                                    pe.wait_ge(s_wf, g * NW + w[0] + 1)
                                    for c in range(OC):
                                        pe.matmul(pw[:, 0:D], oT[:, c, :], Wo[:, c, :], start=(c == 0), stop=False)
                                    pe.matmul(pw[:, 0:D], ones[0:1, 0:P], bo[0:1, :], start=False, stop=True).then_inc(s_w, 1)
                                    w[0] += 1

                            for kind, a in after[-1]:
                                work(kind, a)
                            pe.wait_ge(s_pf, g * NP + NP + 2)
                            for n in range(N + 4):
                                if n < N:
                                    a = n // U
                                    pe.wait_ge(s_e, g * N + n + 1)
                                    for i in range(HU):
                                        h = head(n % U, i)
                                        p0, c = HP * (h % HC), h // HC
                                        for kt in range(KT):
                                            at = (i * KT + kt) * P
                                            m = pe.matmul(psc[n % 2][:, at:at + P], qT[p0:p0 + HP, c, a * P:(a + 1) * P], key(h, a, kt),
                                                          start=True, stop=True)
                                    m.then_inc(s_s, 1)
                                if 1 <= n <= N:
                                    m1 = n - 1
                                    pe.wait_ge(s_e, g * N + m1 + 3)
                                    pe.wait_ge(s_tf, g * N + m1 + 1)
                                    for i in range(4):
                                        m = pe.transpose(ptr[m1 % 2][:, i * P:(i + 1) * P], prob[:, m1 % 2, i * P:(i + 1) * P], ident[:, :])
                                    m.then_inc(s_t, 1)
                                if 2 <= n <= N + 1:
                                    m2 = n - 2
                                    a, u = m2 // U, m2 % U
                                    pe.wait_ge(s_tf, g * N + m2 + 3)
                                    if m2 % U == 0:
                                        pe.wait_ge(s_wf, g * NW + w[0] + 1)
                                    if u % UO == 0:
                                        pe.wait_ge(s_of, g * NO + m2 // UO + 1)
                                    for i in range(HU):
                                        h = head(u, i)
                                        col = (h % HO) * DV
                                        for kt in range(KT):
                                            vals = mv[:, h * DV:(h + 1) * DV] if kt else vv[:, a % 2, h * DV:(h + 1) * DV]
                                            m = pe.matmul(po[:, col:col + DV], probT[:, m2 % 2, (i * KT + kt) * P:(i * KT + kt + 1) * P], vals,
                                                          start=(kt == 0), stop=(kt == KT - 1))
                                    m.then_inc(s_pv, 1)
                                for kind, a in after[n]:
                                    work(kind, a)
                            assert w[0] == NW

                    @block.scalar
                    def _(act):
                        act.sem_inc(s_pf, 2)
                        act.sem_inc(s_e, 2)
                        if bcol is not None:
                            act.activation(bqs[:, :], cols[:, bcol:bcol + 8], ACT.Copy, scale=qscale).then_inc(s_bq, 1)
                            act.wait_ge(s_bq, 1)
                        with act.Fori(0, NG) as g:
                            for i in range(NP):
                                c, isk = i % NC, i // NC
                                act.wait_ge(s_p, g * NP + i + 1)
                                dst = (kT if isk else qT)[:, c, :]
                                if layer == 1:
                                    m = act.activation(dst, pp[i % 2][:, :], ACT.Copy, scale=1.0 if isk else qscale)
                                elif isk:
                                    m = act.activation(dst, pp[i % 2][:, :], ACT.Identity, bias=cols[:, bcol + 8 + c:bcol + 9 + c])
                                else:
                                    m = act.activation(dst, pp[i % 2][:, :], ACT.Identity, bias=bqs[:, c:c + 1], scale=qscale)
                                m.then_inc(s_pf, 1)
                            for n in range(N):
                                a = n // U
                                act.wait_ge(s_nm, g * N + n + 1)
                                act.wait_ge(s_t, g * N + n + 1)
                                for i in range(HU):
                                    h = head(n % U, i)
                                    m = act.activation(prob[:, n % 2, i * KT * P:(i + 1) * KT * P], psc[n % 2][:, i * KT * P:(i + 1) * KT * P],
                                                       ACT.Exp, bias=nmax[:, n % 2, i:i + 1], accum_out=sums[:, a % 2, h:h + 1])
                                m.then_inc(s_e, 1)

                    @block.vector
                    def _(v):
                        v.sem_inc(s_wf, 1)
                        v.sem_inc(s_tf, 2)
                        v.sem_inc(s_of, 1)
                        if layer == 3:
                            for half in range(2):
                                v.wait_ge(s_memT, half + 1)
                                nc.vector.tensor_copy(mkT[:, 4 * half:4 * half + 4, :], ptr[half][:, :].rearrange("p (c n) -> p c n", n=P)).then_inc(s_memE, 1)
                        v.wait_ge(s_bias, 32)
                        with v.Fori(0, NG) as g:
                            if layer == 1:
                                v.wait_ge(s_msk, (g + 1) * 16)
                                v.wait_ge(s_cm, g * DK)
                                nc.vector.tensor_scalar(val[:, :], msk[:, :], 0.0, None, ALU.not_equal).then_inc(s_val, 1)
                                v.wait_ge(s_val, g + 1)
                                v.wait_ge(s_p, g * NP)
                                for k in range(DK):
                                    nc.vector.tensor_tensor(cm[:, k, :], ctxT[:, k, ds(g * GT, GT)], val[:, :], ALU.mult).then_inc(s_cm, 1)
                            w = [0]

                            def work(kind, a):
                                if kind == "v":
                                    for half in range(VH):
                                        v.wait_ge(s_w, g * NW + w[0] + 1)
                                        nc.vector.tensor_tensor(vv[:, a % 2, half * VW:(half + 1) * VW], pw[:, 0:VW], bv[:, half * VW:(half + 1) * VW], ALU.add).then_inc(s_wf, 1)
                                        w[0] += 1
                                elif kind == "turn":
                                    for ob in range(OB):
                                        v.wait_ge(s_w, g * NW + w[0] + 1)
                                        nch = min(4, OC - 4 * ob)
                                        nc.vector.tensor_copy(oT[:, 4 * ob:4 * ob + nch, :], pw[:, 0:nch * P].rearrange("p (c n) -> p c n", n=P)).then_inc(s_wf, 1)
                                        w[0] += 1
                                else:
                                    v.wait_ge(s_w, g * NW + w[0] + 1)
                                    xb = x[:, ds(g * G + a, 1), :].rearrange("p a c -> p (a c)")
                                    nc.vector.scalar_tensor_tensor(out=xb, in0=pw[:, 0:D], scalar=gate[:, layer:layer + 1], in1=xb,
                                                                   op0=ALU.mult, op1=ALU.add).then_inc(s_wf, 1)
                                    w[0] += 1

                            for kind, a in after[-1]:
                                work(kind, a)
                            for n in range(N + 4):
                                if n < N:
                                    v.wait_ge(s_s, g * N + n + 1)
                                    v.wait_ge(s_e, g * N + n + 1)
                                    nc.vector.tensor_reduce(nmax[:, n % 2, :], psc[n % 2][:, :].rearrange("p (h k) -> p h k", h=HU),
                                                            AX.X, ALU.max, negate=True).then_inc(s_nm, 1)
                                if 1 <= n <= N:
                                    m1 = n - 1
                                    v.wait_ge(s_t, g * N + m1 + 3)
                                    if m1 >= 2:
                                        v.wait_ge(s_pv, g * N + m1 - 1)
                                    else:
                                        pass
                                    nc.vector.tensor_copy(probT[:, m1 % 2, :], ptr[m1 % 2][:, :]).then_inc(s_tf, 1)
                                if 2 <= n <= N + 1 and (n - 2) % UO == UO - 1:
                                    m2 = n - 2
                                    a, ho = m2 // U, (m2 % U) // UO
                                    v.wait_ge(s_pv, g * N + m2 + 1)
                                    use = m2 // UO
                                    v.wait_ge(s_of, g * NO + use + 1)
                                    nc.vector.reciprocal(rinv[:, 0:HO], sums[:, a % 2, ho * HO:(ho + 1) * HO]).then_inc(s_r, 1)
                                    v.wait_ge(s_r, g * NO + use + 1)
                                    nc.vector.tensor_tensor(o[:, a % 2, ho * HO * DV:(ho + 1) * HO * DV].rearrange("p (h d) -> p h d", d=DV),
                                                            po[:, 0:HO * DV].rearrange("p (h d) -> p h d", d=DV),
                                                            rinv[:, 0:HO].unsqueeze(2).to_broadcast([P, HO, DV]), ALU.mult).then_inc(s_of, 1)
                                for kind, a in after[n]:
                                    work(kind, a)

        def bitlinear(layer, tag):
            two = layer == 2
            W1, N1 = (tern1, F) if two else (tern0, D)
            xnv = xnT[:, :, :].rearrange("p k n -> p (k n)").rearrange("p (b d) -> p b d", d=D)
            gcol = gate[:, 4 + layer:5 + layer]
            st = ExitStack()
            with st:
                S = lambda n: sem(n + tag, st)
                am = sb("am" + tag, [P, B], F32, st)
                am1 = sb("am1" + tag, [P, B], F32, st)
                up = sb("up" + tag, [P, B], F32, st)
                upr = sb("upr" + tag, [P, B], F32, st)
                down = sb("down" + tag, [P, B], F32, st)
                wsc = sb("wsc" + tag, [P, 2], F32, st)
                bias = sb("bias" + tag, [P, D], F32, st)
                gbias = sb("gbias" + tag, [P, D], F32, st)
                tmp = sb("tmp" + tag, [P, 2, D], F32, st)
                q = sb("q" + tag, [P, 2, D], BF16, st)
                qT = sb("qT" + tag, [P, 2, DK, P], BF16, st)
                s_st, s_mo, s_step, s_rs = S("stats_done"), S("moments_done"), S("moment_step"), S("rstd_done")
                s_b, s_n, s_am, s_x2 = S("bias_loaded"), S("xn_ready"), S("absmax_ready"), S("bias_added")
                s_d = S("dve_step")
                s_q, s_t, s_e = S("codes_ready"), S("codes_turned"), S("codes_evacuated")
                s_m, s_y = S("sums_ready"), S("tokens_done")
                pt = [st.enter_context(nc.psum_tensor(f"pt{i}{tag}", [P, 1024], BF16)) for i in range(2)]
                NY = 4 if two else 3
                if two:
                    b1 = sb("b1" + tag, [P, F], F32, st)
                    h = sb("h" + tag, [P, 2, F], F32, st)
                    tmp2 = sb("tmp2" + tag, [P, F], F32, st)
                    q2 = sb("q2" + tag, [P, 2, F], BF16, st)
                    q2T = sb("q2T" + tag, [P, 2, FC, P], BF16, st)
                    am2 = sb("am2" + tag, [P, 2, 5], F32, st)
                    ph = [st.enter_context(nc.psum_tensor(f"ph{i}{tag}", [P, 512], F32)) for i in range(2)]
                    pt2 = st.enter_context(nc.psum_tensor("pt2" + tag, [P, 1024], BF16))
                    s_h, s_gl, s_q2 = S("hidden_ready"), S("gelu_done"), S("codes2_ready")
                    s_m1, s_t2, s_e2 = S("sums1_ready"), S("codes2_turned"), S("codes2_evacuated")
                py = [st.enter_context(nc.psum_tensor(f"py{i}{tag}", [P, D], F32)) for i in range(2)]
                KD = (2 + 7) * G if two else 2 * G

                with nc.Block() as block:
                    @block.sync
                    def _(sp):
                        row = lambda a: a.rearrange("(a n) -> a n", a=1)
                        sp.dma_start(bias[:, :], row(t["L2_ffn_b2" if two else "L0_ffn_bias"]).to_broadcast([P, D])).then_inc(s_b, 16)
                        if two:
                            sp.dma_start(b1[:, :], row(t["L2_ffn_b1"]).to_broadcast([P, F])).then_inc(s_b, 16)
                        else:
                            sp.dma_start(wsc[:, 0:1], row(t["L0_ffn_weight_scale"]).to_broadcast([P, 1])).then_inc(s_b, 16)

                    @block.gpsimd
                    def _(pool):
                        root_pool(pool, s_mo, s_rs)
                        pool.wait_ge(s_n, B)
                        pool.wait_ge(s_b, 33)
                        pool.tensor_tensor(x[:, :, :], x[:, :, :], gbias[:, :].unsqueeze(1).to_broadcast([P, B, D]), ALU.add).then_inc(s_x2, 1)

                    @block.vector
                    def _(v):
                        v.wait_ge(s_b, 32)
                        nc.vector.tensor_scalar(gbias[:, :], bias[:, :], gcol, None, ALU.mult).then_inc(s_b, 1)
                        wlast = wscale[:, 1:2] if two else wsc[:, 0:1]
                        nc.vector.tensor_scalar(wsc[:, 1:2], wlast, gcol, 1.0 / 127.0, ALU.mult, ALU.mult).then_inc(s_step, 1)
                        moments_vector(v, s_st, s_mo, s_step, 1)
                        v.wait_ge(s_rs, 1)
                        with v.Fori(0, B) as b:
                            xb = x[:, ds(b, 1), :].rearrange("p a c -> p (a c)")
                            xnb = xnv[:, ds(b, 1), :].rearrange("p a c -> p (a c)")
                            nc.vector.tensor_scalar(xnb, xb, mean[:, ds(b, 1)], rstd[:, ds(b, 1)], ALU.subtract, ALU.mult).then_inc(s_n, 1)
                            v.wait_ge(s_n, b + 1)
                            nc.vector.tensor_reduce(am[:, ds(b, 1)], xnb, AX.X, ALU.max, apply_absolute_value=True).then_inc(s_am, 1)
                        v.wait_ge(s_am, B)
                        nc.vector.tensor_scalar(am1[:, :], am[:, :], 1e-5, None, ALU.max).then_inc(s_am, 1)
                        v.wait_ge(s_am, B + 1)
                        nc.vector.reciprocal(upr[:, :], am1[:, :]).then_inc(s_am, 1)
                        if two:
                            nc.vector.tensor_scalar(down[:, :], am1[:, :], wscale[:, 0:1], 1.0 / 127.0, ALU.mult, ALU.mult).then_inc(s_am, 1)
                        else:
                            nc.vector.tensor_scalar(down[:, :], am1[:, :], wsc[:, 1:2], None, ALU.mult).then_inc(s_am, 1)
                        v.wait_ge(s_am, B + 2)
                        nc.vector.tensor_scalar(up[:, :], upr[:, :], 127.0, None, ALU.mult).then_inc(s_am, 1)
                        v.wait_ge(s_am, B + 4)
                        v.wait_ge(s_x2, 1)

                        with v.Fori(0, NG) as g:
                            done = [0]

                            def step(ins):
                                ins.then_inc(s_d, 1)
                                done[0] += 1
                                v.wait_ge(s_d, g * KD + done[0])

                            def codes(dst, src, scratch, scale, s_ready):
                                step(nc.vector.tensor_scalar(scratch, src, scale, ROUND, ALU.mult, ALU.add))
                                step(nc.vector.tensor_scalar(scratch, scratch, ROUND, -128.0, ALU.subtract, ALU.max))
                                nc.vector.tensor_scalar(dst, scratch, 127.0, None, ALU.min).then_inc(s_ready, 1)

                            for n in range(G + NY - 1):
                                if n < G:
                                    b = g * G + n
                                    v.wait_ge(s_t, b + 1)
                                    codes(q[:, n % 2, :], xnv[:, ds(b, 1), :].rearrange("p a c -> p (a c)"), tmp[:, n % 2, :], up[:, ds(b, 1)], s_q)
                                if two and 1 <= n <= G:
                                    a = n - 1
                                    b = g * G + a
                                    v.wait_ge(s_m1, b + 1)
                                    for half in range(2):
                                        c = slice(half * 512, half * 512 + 512)
                                        nc.vector.scalar_tensor_tensor(out=h[:, a % 2, c], in0=ph[half][:, :], scalar=down[:, ds(b, 1)], in1=b1[:, c],
                                                                       op0=ALU.mult, op1=ALU.add).then_inc(s_h, 1)
                                if two and 2 <= n <= G + 1:
                                    a = n - 2
                                    b = g * G + a
                                    v.wait_ge(s_gl, b + 1)
                                    sc = am2[:, a % 2, :]
                                    hh = h[:, a % 2, :]
                                    step(nc.vector.tensor_reduce(sc[:, 0:1], hh, AX.X, ALU.max, apply_absolute_value=True))
                                    step(nc.vector.tensor_scalar(sc[:, 1:2], sc[:, 0:1], 1e-5, None, ALU.max))
                                    step(nc.vector.reciprocal(sc[:, 2:3], sc[:, 1:2]))
                                    step(nc.vector.tensor_scalar(sc[:, 3:4], sc[:, 2:3], 127.0, None, ALU.mult))
                                    step(nc.vector.tensor_scalar(sc[:, 4:5], sc[:, 1:2], wsc[:, 1:2], None, ALU.mult))
                                    v.wait_ge(s_t2, b + 1)
                                    codes(q2[:, a % 2, :], hh, tmp2[:, :], sc[:, 3:4], s_q2)
                                    v.wait_ge(s_q2, b + 1)
                                if NY - 1 <= n:
                                    a = n - NY + 1
                                    b = g * G + a
                                    v.wait_ge(s_m, b + 1)
                                    xb = x[:, ds(b, 1), :].rearrange("p a c -> p (a c)")
                                    nc.vector.scalar_tensor_tensor(out=xb, in0=py[a % 2][:, :], scalar=am2[:, a % 2, 4:5] if two else down[:, ds(b, 1)], in1=xb,
                                                                   op0=ALU.mult, op1=ALU.add).then_inc(s_y, 1)
                            assert done[0] == KD

                    @block.tensor
                    def _(pe):
                        pe.sem_inc(s_t, 2)
                        if two:
                            pe.sem_inc(s_t2, 2)
                        with pe.Fori(0, NG) as g:
                            for n in range(G + NY - 1):
                                if n < G:
                                    b = g * G + n
                                    pe.wait_ge(s_q, b + 1)
                                    pe.wait_ge(s_e, b + 1)
                                    for k in range(DK):
                                        m = pe.transpose(pt[n % 2][:, k * P:(k + 1) * P], q[:, n % 2, k * P:(k + 1) * P], identb[:, :])
                                    m.then_inc(s_t, 1)
                                if 1 <= n <= G:
                                    a = n - 1
                                    b = g * G + a
                                    pe.wait_ge(s_e, b + 3)
                                    if two:
                                        pe.wait_ge(s_h, 2 * b)
                                        for half in range(2):
                                            for k in range(DK):
                                                m = pe.matmul(ph[half][:, :], qT[:, a % 2, k, :], W1[:, k, half * 512:half * 512 + 512], start=(k == 0), stop=(k == DK - 1))
                                        m.then_inc(s_m1, 1)
                                    else:
                                        pe.wait_ge(s_y, b + 1)
                                        for k in range(DK):
                                            m = pe.matmul(py[a % 2][:, :], qT[:, a % 2, k, :], W1[:, k, :], start=(k == 0), stop=(k == DK - 1))
                                        m.then_inc(s_m, 1)
                                if two and 2 <= n <= G + 1:
                                    a = n - 2
                                    b = g * G + a
                                    pe.wait_ge(s_q2, b + 1)
                                    pe.wait_ge(s_e2, b + 1)
                                    for c in range(FC):
                                        m = pe.transpose(pt2[:, c * P:(c + 1) * P], q2[:, a % 2, c * P:(c + 1) * P], identb[:, :])
                                    m.then_inc(s_t2, 1)
                                if two and 3 <= n:
                                    a = n - 3
                                    b = g * G + a
                                    pe.wait_ge(s_e2, b + 2)
                                    pe.wait_ge(s_y, b + 1)
                                    for c in range(FC):
                                        m = pe.matmul(py[a % 2][:, :], q2T[:, a % 2, c, :], tern2[:, c, :], start=(c == 0), stop=(c == FC - 1))
                                    m.then_inc(s_m, 1)

                    @block.scalar
                    def _(act):
                        act.sem_inc(s_e, 2)
                        act.sem_inc(s_y, 2)
                        if two:
                            act.sem_inc(s_e2, 1)
                        with act.Fori(0, NG) as g:
                            for n in range(G + 2):
                                if n < G:
                                    b = g * G + n
                                    act.wait_ge(s_t, b + 3)
                                    if n < 2:
                                        act.wait_ge(s_m1 if two else s_m, g * G)
                                    else:
                                        act.wait_ge(s_m1 if two else s_m, g * G + n - 1)
                                    act.activation(qT[:, n % 2, :, :], pt[n % 2][:, 0:D].rearrange("p (k n) -> p k n", n=P), ACT.Copy).then_inc(s_e, 1)
                                if two and 1 <= n <= G:
                                    a = n - 1
                                    b = g * G + a
                                    act.wait_ge(s_h, 2 * b + 2)
                                    act.activation(h[:, a % 2, :], h[:, a % 2, :], ACT.Gelu).then_inc(s_gl, 1)
                                if two and 2 <= n:
                                    a = n - 2
                                    b = g * G + a
                                    act.wait_ge(s_t2, b + 3)
                                    if a < 2:
                                        act.wait_ge(s_m, g * G)
                                    else:
                                        act.wait_ge(s_m, g * G + a - 1)
                                    act.activation(q2T[:, a % 2, :, :], pt2[:, :].rearrange("p (k n) -> p k n", n=P), ACT.Copy).then_inc(s_e2, 1)

        def experts(layer, tag):
            top = 2 if layer == 3 else 1
            SLOTS = top * B + E - 1
            pre = "L%d_ffn_" % layer
            gcol = gate[:, 4 + layer:5 + layer]
            rows_in = nc.dram_tensor("rows_in" + tag, ((SLOTS + 1) * P, D), F32, kind="Internal").ap()
            rows_out = nc.dram_tensor("rows_out" + tag, (SLOTS * P, D), F32, kind="Internal").ap()
            whole = ExitStack()
            with whole:
                S = lambda n: sem(n + tag, whole)
                xtok = sb("xtok" + tag, [P, B, D], F32, whole)
                pos = sb("pos" + tag, [P, top, B], mybir.dt.uint32, whole)
                coef = sb("coef" + tag, [P, top, B], F32, whole)
                first = sb("first" + tag, [P, 16], I32, whole)
                s_zero, s_w = S("rows_zeroed"), [S("weights_even_loaded"), S("weights_odd_loaded")]
                w1 = sb("w1" + tag, [P, 2, DK, F], F32, whole)
                w3 = sb("w3" + tag, [P, 2, DK, F], F32, whole) if layer == 3 else None
                w2 = sb("w2" + tag, [P, 2, FC, D], F32, whole)
                w1d = t[pre + "w1"].rearrange("e (k p) n -> e p k n", p=P)
                w2d = t[pre + "w2"].rearrange("e (c p) n -> e p c n", p=P)
                w3d = t[pre + "w3"].rearrange("e (k p) n -> e p k n", p=P) if layer == 3 else None
                NW = 3 if layer == 3 else 2

                def load_weights(eng, e, j):
                    def of(d):
                        return d[ds(e, 1)].rearrange("a p k n -> (a p) k n")
                    eng.dma_start(w1[:, j, :, :], of(w1d)).then_inc(s_w[j], 16)
                    eng.dma_start(w2[:, j, :, :], of(w2d)).then_inc(s_w[j], 16)
                    if layer == 3:
                        eng.dma_start(w3[:, j, :, :], of(w3d)).then_inc(s_w[j], 16)

                st = ExitStack()
                with st:
                    zero = sb("zero" + tag, [P, D], F32, st)
                    s_zt = sem("zero_ready" + tag, st)
                    with nc.Block() as block:
                        norm_transposed(block, st, tag, xtok)

                        @block.gpsimd
                        def _(pool):
                            pool.memset(zero[:, :], 0.0).then_inc(s_zt, 1)

                        @block.sync
                        def _(sp):
                            load_weights(sp, 0, 0)
                            sp.wait_ge(s_zt, 1)
                            sp.dma_start(rows_in.rearrange("(n p) d -> p n d", p=P), zero[:, :].unsqueeze(1).to_broadcast([P, SLOTS + 1, D])).then_inc(s_zero, 16)
                            sp.dma_start(rows_out.rearrange("(n p) d -> p n d", p=P), zero[:, :].unsqueeze(1).to_broadcast([P, SLOTS, D])).then_inc(s_zero, 16)
                            sp.wait_ge(s_zero, 32)

                st = ExitStack()
                with st:
                    R = lambda n: sem(n + tag, st)
                    T = lambda n, shape, dt=F32: sb(n + tag, shape, dt, st)
                    gw = T("gw", [P, DK, E])
                    lgT = T("lgT", [E, B * P])
                    lg = T("lg", [P, B, E])
                    pr = T("pr", [P, B, E])
                    prs = T("prs", [P, top, B, E])
                    oh = T("oh", [P, top, B, E])
                    eq = T("eq", [P, B, E])
                    tok = T("tok", [P, 8, B])
                    pref = T("pref", [P, E])
                    low = T("low", [P, P])
                    chosen = T("chosen", [P, B, E])
                    cnt = T("cnt", [P, E, B])
                    run = T("run", [P, E, B])
                    full = T("full", [P, B, E])
                    ends = T("ends", [P, E + 1])
                    slot = T("slot", [P, 6, E])
                    firstf = T("firstf", [P, 16])
                    pos_f = T("pos_f", [P, top, B])
                    pl = [st.enter_context(nc.psum_tensor(f"pl{i}{tag}", [P, 512], F32)) for i in range(4)]
                    s_gw, s_c, s_l, s_le, s_lt, s_d, s_mx, s_ex, s_oh, s_rk, s_pos, s_sc = (
                        R(n) for n in ("gate_weights_loaded", "constants_ready", "logits_turned_ready", "logits_evacuated", "logits_ready",
                                       "dve_step", "max_subtracted", "exp_done", "choices_ready", "ranks_ready", "rows_known", "tokens_scattered"))
                    if layer == 1:
                        wred = T("wred", [P, DK, 16])
                        wredT = T("wredT", [16, DK, P])
                        wg = T("wg", [E, 16])
                        wgn = T("wgn", [E, 16])
                        wgs = T("wgs", [E, 8])
                        sq = T("sq", [E, 16])
                        wgT = T("wgT", [16, E])
                        s_g1, s_g2, s_g3 = R("gate_parts_turned"), R("gate_parts_ready"), R("norm_root")

                    with nc.Block() as block:
                        @block.sync
                        def _(sp):
                            if layer == 1:
                                sp.dma_start(wred[:, :, :], t[pre + "w_red"].rearrange("(k p) n -> p k n", p=P)).then_inc(s_gw, 16)
                                sp.dma_start(wg[:, :], t[pre + "wg"]).then_inc(s_gw, 16)
                            else:
                                sp.dma_start(gw[:, :, :], t[pre + "gate_w"].rearrange("(k p) n -> p k n", p=P)).then_inc(s_gw, 16)

                        @block.gpsimd
                        def _(pool):
                            pool.iota(pref[:, :], pattern=[[-1, E]], base=E, channel_multiplier=0, allow_small_or_imprecise_dtypes=True).then_inc(s_c, 1)
                            pool.affine_select(out=low[:, :], in_=ones[:, 0:P], compare_op=ALU.is_gt, fill=0.0, base=0,
                                               pattern=[[1, P]], channel_multiplier=-1).then_inc(s_c, 1)
                            pool.memset(ends[:, :], 0.0).then_inc(s_c, 1)
                            pool.memset(firstf[:, :], 0.0).then_inc(s_c, 1)
                            if layer == 1:
                                pool.wait_ge(s_g3, 1)
                                pool.tensor_tensor(wgs[:, 1:2], wgs[:, 0:1], wgs[:, 7:8], ALU.pow).then_inc(s_g3, 1)
                            pool.wait_ge(s_pos, 1)
                            for c in range(top):
                                for b in range(B):
                                    pool.indirect_dma_start(rows_in, bass.IndirectOffsetOnAxis(ap=pos[:, c, b:b + 1], axis=0),
                                                            xtok[:, b, :], None).then_inc(s_sc, 16)
                            pool.wait_ge(s_sc, 16 * top * B)

                        @block.tensor
                        def _(pe):
                            pe.wait_ge(s_c, 4)
                            if layer == 1:
                                pe.wait_ge(s_gw, 32)
                                for k in range(DK):
                                    pe.transpose(pl[0][0:16, k * P:(k + 1) * P], wred[:, k, :], ident[:, :])
                                pe.wait_ge(s_g3, 3)
                                pe.transpose(pl[1][0:16, 0:E], wgn[:, :], ident[0:E, 0:E]).then_inc(s_g1, 1)
                                pe.wait_ge(s_g2, 2)
                                for k in range(DK):
                                    m = pe.matmul(pl[2 + k][:, 0:E], wredT[:, k, :], wgT[:, :], start=True, stop=True)
                                m.then_inc(s_g1, 1)
                                pe.wait_ge(s_g2, 4)
                            else:
                                pe.wait_ge(s_gw, 16)
                            for g in range(NG):
                                if g >= 2:
                                    pe.wait_ge(s_le, g - 1)
                                for k in range(DK):
                                    m = pe.matmul(pl[g % 2][0:E, :], gw[:, k, :], xnT[:, k, g * GT:(g + 1) * GT], start=(k == 0), stop=(k == DK - 1))
                                m.then_inc(s_l, 1)
                            pe.wait_ge(s_le, NG)
                            for b in range(B):
                                m = pe.transpose(pl[2][:, b * E:(b + 1) * E], lgT[:, b * P:(b + 1) * P], ident[0:E, 0:E])
                            m.then_inc(s_lt, 1)
                            pe.wait_ge(s_oh, 1)
                            ch = chosen[:, :, :].rearrange("p b e -> p (b e)")
                            pe.matmul(pl[0][:, 0:P], low[:, :], ch, start=True, stop=True)
                            pe.matmul(pl[1][:, 0:P], ones[:, 0:P], ch, start=True, stop=True).then_inc(s_rk, 1)

                        @block.scalar
                        def _(act):
                            act.wait_ge(s_mx, 1)
                            act.activation(pr[:, :, :], lg[:, :, :], ACT.Exp).then_inc(s_ex, 1)

                        @block.vector
                        def _(v):
                            n = [0]

                            def step(ins):
                                ins.then_inc(s_d, 1)
                                n[0] += 1
                                v.wait_ge(s_d, n[0])

                            V = nc.vector
                            v.wait_ge(s_c, 4)
                            if layer == 1:
                                v.wait_ge(s_gw, 32)
                                step(V.tensor_tensor(sq[:, :], wg[:, :], wg[:, :], ALU.mult))
                                step(V.memset(wgs[:, 7:8], 0.5))
                                V.tensor_reduce(wgs[:, 0:1], sq[:, :], AX.X, ALU.add).then_inc(s_g3, 1)
                                v.wait_ge(s_g3, 2)
                                step(V.tensor_scalar(wgs[:, 2:3], wgs[:, 1:2], 1e-4, None, ALU.max))
                                step(V.reciprocal(wgs[:, 3:4], wgs[:, 2:3]))
                                V.tensor_scalar(wgn[:, :], wg[:, :], wgs[:, 3:4], None, ALU.mult).then_inc(s_g3, 1)
                                v.wait_ge(s_g1, 1)
                                V.tensor_copy(wredT[:, :, :], pl[0][0:16, 0:D].rearrange("p (k n) -> p k n", n=P)).then_inc(s_g2, 1)
                                V.tensor_copy(wgT[:, :], pl[1][0:16, 0:E]).then_inc(s_g2, 1)
                                v.wait_ge(s_g1, 2)
                                for k in range(DK):
                                    V.tensor_copy(gw[:, k, :], pl[2 + k][:, 0:E]).then_inc(s_g2, 1)
                            for g in range(NG):
                                v.wait_ge(s_l, g + 1)
                                V.tensor_copy(lgT[:, g * GT:(g + 1) * GT], pl[g % 2][0:E, :]).then_inc(s_le, 1)
                            v.wait_ge(s_lt, 1)

                            def per_token(ap):
                                return ap.unsqueeze(2).to_broadcast([P, B, E])

                            pl3 = pl[2][:, 0:B * E].rearrange("p (b e) -> p b e", e=E)
                            step(V.tensor_reduce(tok[:, 0, :], pl3, AX.X, ALU.max))
                            V.tensor_tensor(lg[:, :, :], pl3, per_token(tok[:, 0, :]), ALU.subtract).then_inc(s_mx, 1)
                            v.wait_ge(s_ex, 1)
                            step(V.tensor_reduce(tok[:, 1, :], pr[:, :, :], AX.X, ALU.add))
                            step(V.reciprocal(tok[:, 2, :], tok[:, 1, :]))
                            step(V.tensor_tensor(prs[:, 0, :, :], pr[:, :, :], per_token(tok[:, 2, :]), ALU.mult))
                            prefb = pref[:, :].unsqueeze(1).to_broadcast([P, B, E])
                            for c in range(top):
                                best, code = tok[:, 3 + c, :], tok[:, 5 + c, :]
                                if c:
                                    step(V.scalar_tensor_tensor(out=prs[:, 1, :, :], in0=oh[:, 0, :, :], scalar=-4.0, in1=prs[:, 0, :, :], op0=ALU.mult, op1=ALU.add))
                                step(V.tensor_reduce(best, prs[:, c, :, :], AX.X, ALU.max))
                                step(V.tensor_tensor(eq[:, :, :], prs[:, c, :, :], per_token(best), ALU.is_equal))
                                step(V.tensor_tensor(eq[:, :, :], eq[:, :, :], prefb, ALU.mult))
                                step(V.tensor_reduce(code, eq[:, :, :], AX.X, ALU.max))
                                step(V.tensor_tensor(oh[:, c, :, :], eq[:, :, :], per_token(code), ALU.is_equal))
                            if top == 2:
                                V.tensor_tensor(chosen[:, :, :], oh[:, 0, :, :], oh[:, 1, :, :], ALU.add).then_inc(s_oh, 1)
                                step(V.tensor_tensor(tok[:, 7, :], tok[:, 3, :], tok[:, 4, :], ALU.add))
                                step(V.reciprocal(tok[:, 0, :], tok[:, 7, :]))
                                for c in range(top):
                                    step(V.scalar_tensor_tensor(out=coef[:, c, :], in0=tok[:, 3 + c, :], scalar=gcol, in1=tok[:, 0, :], op0=ALU.mult, op1=ALU.mult))
                            else:
                                V.tensor_copy(chosen[:, :, :], oh[:, 0, :, :]).then_inc(s_oh, 1)
                                step(V.tensor_scalar(coef[:, 0, :], tok[:, 3, :], gcol, None, ALU.mult))
                            v.wait_ge(s_rk, 1)
                            counts = pl[1][:, 0:P].rearrange("p (b e) -> p e b", e=E)
                            step(V.tensor_copy(cnt[:, :, :], counts))
                            step(V.tensor_tensor_scan(run[:, :, :].rearrange("p e b -> p (e b)"), ones[:, 0:P], cnt[:, :, :].rearrange("p e b -> p (e b)"), 0.0, ALU.mult, ALU.add))
                            step(V.tensor_copy(ends[:, 1:E + 1], run[:, :, B - 1]))
                            step(V.tensor_tensor(slot[:, 0, :], ends[:, 1:E + 1], ends[:, 0:E], ALU.subtract))
                            step(V.tensor_scalar(slot[:, 1, :], slot[:, 0, :], 1.0 / P, 0.5 - 0.5 / P, ALU.mult, ALU.add))
                            step(V.tensor_scalar(slot[:, 2, :], slot[:, 1, :], ROUND, ROUND, ALU.add, ALU.subtract))
                            step(V.tensor_scalar(slot[:, 3, :], slot[:, 2, :], 1.0, None, ALU.max))
                            step(V.tensor_tensor_scan(firstf[:, 2:E + 2], ones[:, 0:E], slot[:, 3, :], 0.0, ALU.mult, ALU.add))
                            step(V.tensor_copy(first[:, :], firstf[:, :]))
                            step(V.scalar_tensor_tensor(out=slot[:, 4, :], in0=firstf[:, 1:E + 1], scalar=float(P), in1=ends[:, 0:E], op0=ALU.mult, op1=ALU.subtract))
                            step(V.tensor_tensor(run[:, :, :], run[:, :, :], cnt[:, :, :], ALU.subtract))
                            step(V.tensor_tensor(full[:, :, :], pl[0][:, 0:P].rearrange("p (b e) -> p b e", e=E), run[:, :, :].rearrange("p e b -> p b e"), ALU.add))
                            step(V.tensor_tensor(full[:, :, :], full[:, :, :], slot[:, 4, :].unsqueeze(1).to_broadcast([P, B, E]), ALU.add))
                            for c in range(top):
                                step(V.tensor_tensor(oh[:, c, :, :], oh[:, c, :, :], full[:, :, :], ALU.mult))
                                step(V.tensor_reduce(pos_f[:, c, :], oh[:, c, :, :], AX.X, ALU.add))
                            V.tensor_copy(pos[:, :, :], pos_f[:, :, :]).then_inc(s_pos, 1)

                st = ExitStack()
                with st:
                    R = lambda n: sem(n + tag, st)
                    T = lambda n, shape, dt=F32: sb(n + tag, shape, dt, st)
                    xg = T("xg", [P, D])
                    xgT = T("xgT", [P, DK, P])
                    hT = T("hT", [P, FC, P])
                    y = T("y", [P, D])
                    b1e = T("b1e", [P, 2, FC]) if layer == 1 else None
                    b2 = T("b2", [1, E, D]) if layer == 1 else None
                    b2e = T("b2e", [1, 2, D]) if layer == 1 else None
                    sg = T("sg", [P, 2, 512]) if layer == 3 else None
                    yg = T("yg", [P, 4, D])
                    pb = lambda n, w: st.enter_context(nc.psum_tensor(n + tag, [P, w], F32))
                    ph = [pb(f"ph{i}", 512) for i in range(2)]
                    ph3 = [pb(f"ph3{i}", 512) for i in range(2)] if layer == 3 else None
                    px, py = pb("px", D), pb("py", D)
                    s_xg, s_tn, s_xT = R("tokens_loaded"), R("tokens_turned"), R("turned_evacuated")
                    s_h, s_act, s_hT = R("hidden_sums"), R("activated"), R("hidden_ready")
                    s_y, s_ye, s_st = R("slot_done"), R("y_evacuated"), R("y_stored")
                    s_b, s_be = R("bias2_loaded"), R("bias_ready")
                    s_yg = [R(f"gathered{i}") for i in range(4)]
                    s_up = R("tokens_updated")

                    def slot_range(eng, e):
                        a = eng.value_load(first[0:1, ds(e + 1, 1)], min_val=0, max_val=SLOTS - 1)
                        b = eng.value_load(first[0:1, ds(e + 2, 1)], min_val=1, max_val=SLOTS)
                        return a, b

                    def total(eng):
                        return eng.value_load(first[0:1, E + 1:E + 2], min_val=E, max_val=SLOTS)

                    with nc.Block() as block:
                        @block.sync
                        def _(sp):
                            if layer == 1:
                                sp.dma_start(b2[:, :, :], t[pre + "b2"].rearrange("(a e) n -> a e n", a=1)).then_inc(s_b, 16)

                        @block.gpsimd
                        def _(pool):
                            pool.dma_start(xg[:, :], rows_in[0:P, :]).then_inc(s_xg, 16)
                            with pool.Fori(0, total(pool)) as s:
                                pool.wait_ge(s_tn, s + 1)
                                pool.dma_start(xg[:, :], rows_in[ds((s + 1) * P, P), :]).then_inc(s_xg, 16)
                                pool.wait_ge(s_ye, s + 1)
                                pool.dma_start(rows_out[ds(s * P, P), :], y[:, :]).then_inc(s_st, 16)
                            pool.wait_ge(s_st, total(pool) * 16)

                        @block.tensor
                        def _(pe):
                            def turn():
                                for k in range(DK):
                                    m = pe.transpose(px[:, k * P:(k + 1) * P], xg[:, k * P:(k + 1) * P], ident[:, :])
                                m.then_inc(s_tn, 1)

                            pe.wait_ge(s_xg, 16)
                            turn()

                            def expert(r, j):
                                a, b = slot_range(pe, r * 2 + j)
                                with pe.Fori(a, b) as s:
                                    pe.wait_ge(s_w[j], (r + 1) * (16 * NW))
                                    if layer == 1:
                                        pe.wait_ge(s_be, r * 2 + j + 1)
                                    pe.wait_ge(s_xT, s + 1)
                                    for half in range(2):
                                        for w, bank in ((w1, ph), (w3, ph3))[:layer // 2 + 1]:
                                            for c in range(4):
                                                f = (4 * half + c) * P
                                                for k in range(DK):
                                                    m = pe.matmul(bank[half][:, c * P:(c + 1) * P], w[:, j, k, f:f + P], xgT[:, k, :], start=(k == 0), stop=(k == DK - 1))
                                            m.then_inc(s_h, 1)
                                    pe.wait_ge(s_xg, s * 16 + 32)
                                    turn()
                                    pe.wait_ge(s_ye, s)
                                    for c in range(FC):
                                        if c % 4 == 0:
                                            pe.wait_ge(s_hT, s * 2 + c // 4 + 1)
                                        m = pe.matmul(py[:, :], hT[:, c, :], w2[:, j, c, :], start=(c == 0), stop=(c == FC - 1 and layer == 3))
                                    if layer == 1:
                                        m = pe.matmul(py[:, :], ones[0:1, 0:P], b2e[0:1, j, :], start=False, stop=True)
                                    m.then_inc(s_y, 1)

                            with pe.Fori(0, E // 2) as r:
                                for j in range(2):
                                    expert(r, j)

                        @block.scalar
                        def _(act):
                            if layer == 1:
                                act.wait_ge(s_b, 16)

                            def expert(r, j, load):
                                a, b = slot_range(act, r * 2 + j)
                                act.wait_ge(s_y, a)
                                if load:
                                    load_weights(act, r * 2 + j + 1, 1 - j)
                                if layer == 1:
                                    act.activation(b1e[:, j, :], cols[:, ds(r * 16 + (32 + FC * j), FC)], ACT.Copy).then_inc(s_b, 1)
                                    act.activation(b2e[:, j, :], b2[0:1, ds(r * 2 + j, 1), :].rearrange("a e n -> a (e n)"), ACT.Copy).then_inc(s_be, 1)
                                    act.wait_ge(s_b, r * 2 + (j + 17))
                                with act.Fori(a, b) as s:
                                    for half in range(2):
                                        if layer == 1:
                                            act.wait_ge(s_h, s * 2 + half + 1)
                                            for c in range(4):
                                                m = act.activation(hT[:, 4 * half + c, :], ph[half][:, c * P:(c + 1) * P], ACT.Gelu, bias=b1e[:, j, 4 * half + c:4 * half + c + 1])
                                            m.then_inc(s_hT, 1)
                                        else:
                                            act.wait_ge(s_h, s * 4 + 2 * half + 1)
                                            act.activation(sg[:, half, :], ph[half][:, :], ACT.Silu).then_inc(s_act, 1)

                            with act.Fori(0, E // 2 - 1) as r:
                                for j in range(2):
                                    expert(r, j, True)
                            for j in range(2):
                                expert(E // 2 - 1, j, j == 0)

                        @block.vector
                        def _(v):
                            def take_tokens(n):
                                v.wait_ge(s_tn, n)
                                nc.vector.tensor_copy(xgT[:, :, :], px[:, :].rearrange("p (k n) -> p k n", n=P)).then_inc(s_xT, 1)

                            take_tokens(1)
                            with v.Fori(0, total(v)) as s:
                                if layer == 3:
                                    for half in range(2):
                                        v.wait_ge(s_act, s * 2 + half + 1)
                                        v.wait_ge(s_h, s * 4 + 2 * half + 2)
                                        nc.vector.tensor_tensor(hT[:, 4 * half:4 * half + 4, :].rearrange("p c n -> p (c n)"), sg[:, half, :], ph3[half][:, :], ALU.mult).then_inc(s_hT, 1)
                                take_tokens(s + 2)
                                v.wait_ge(s_y, s + 1)
                                v.wait_ge(s_st, s * 16)
                                nc.vector.tensor_copy(y[:, :], py[:, :]).then_inc(s_ye, 1)

                    with nc.Block() as block:
                        @block.gpsimd
                        def _(pool):
                            for n in range(top * B):
                                c, b = n % top, n // top
                                if n >= 4:
                                    pool.wait_ge(s_up, n - 3)
                                pool.indirect_dma_start(yg[:, n % 4, :], None, rows_out,
                                                        bass.IndirectOffsetOnAxis(ap=pos[:, c, b:b + 1], axis=0)).then_inc(s_yg[n % 4], 16)

                        @block.vector
                        def _(v):
                            for n in range(top * B):
                                c, b = n % top, n // top
                                v.wait_ge(s_yg[n % 4], 16 * (n // 4 + 1))
                                if c:
                                    v.wait_ge(s_up, n)
                                nc.vector.scalar_tensor_tensor(out=x[:, b, :], in0=yg[:, n % 4, :], scalar=coef[:, c, b:b + 1], in1=x[:, b, :],
                                                               op0=ALU.mult, op1=ALU.add).then_inc(s_up, 1)

        def additive(tag):
            FB = 16
            UB = P // FB * DK
            RING = 4
            NEG = -1e30
            whole = ExitStack()
            with whole:
                S = lambda n: sem(n + tag, whole)
                T = lambda n, shape, dt=F32: sb(n + tag, shape, dt, whole)
                featT, txtT = T("featT", [P, DK, B * P]), T("txtT", [P, DK, B * P])
                Ws, W = T("Ws", [P, DK, D]), T("W", [P, DK, D])
                vrow = T("vrow", [4, P])
                vcol = T("vcol", [P, 4])
                wsel = T("wsel", [P, DK, UB // DK, 32])
                wcb = T("wcb", [P, 2, D])
                bc = T("bc", [P, 2])
                s_w, s_v, s_vt, s_vc = S("weights_loaded"), S("small_loaded"), S("small_turned"), S("small_ready")
                s_z = S("selector_zero")
                s_pj, s_pe = S("projected"), S("projection_evacuated")

                st = ExitStack()
                with st:
                    with nc.Block() as block:
                        norm_transposed(block, st, tag)

                        @block.sync
                        def _(sp):
                            row = lambda a: a.rearrange("(c p) a -> (a c) p", p=P)
                            sp.dma_start(W[:, :, :], t["L2_xattn_W"].rearrange("(k p) n -> p k n", p=P)).then_inc(s_w, 16)
                            sp.dma_start(Ws[:, :, :], t["L2_xattn_Ws"].rearrange("(k p) n -> p k n", p=P)).then_inc(s_w, 16)
                            sp.dma_start(vrow[0:2, :], row(t["L2_xattn_w"])).then_inc(s_v, 16)
                            sp.dma_start(vrow[2:4, :], t["L2_xattn_b"].rearrange("a (c p) -> (a c) p", p=P)).then_inc(s_v, 16)
                            sp.dma_start(wcb[:, 0, :], t["L2_xattn_Wcw"].to_broadcast([P, D])).then_inc(s_v, 16)
                            sp.dma_start(wcb[:, 1, :], t["L2_xattn_Wcb"].to_broadcast([P, D])).then_inc(s_v, 16)
                            one = lambda a: a.rearrange("(a n) -> a n", a=1).to_broadcast([P, 1])
                            sp.dma_start(bc[:, 0:1], one(t["L2_xattn_bcw"])).then_inc(s_v, 16)
                            sp.dma_start(bc[:, 1:2], one(t["L2_xattn_bcb"])).then_inc(s_v, 16)

                st = ExitStack()
                with st:
                    pv = st.enter_context(nc.psum_tensor("pv" + tag, [P, 512], F32))
                    pp = [st.enter_context(nc.psum_tensor(f"pp{i}{tag}", [P, 512], F32)) for i in range(4)]
                    with nc.Block() as block:
                        @block.tensor
                        def _(pe):
                            pe.wait_ge(s_v, 16 * 6)
                            pe.transpose(pv[:, 0:4], vrow[:, :], ident[0:4, 0:4]).then_inc(s_vt, 1)
                            pe.wait_ge(s_w, 32)
                            with pe.Fori(0, NG) as g:
                                for i, (w, src) in enumerate(((W, xnT), (Ws, ctxT))):
                                    for c in range(DK):
                                        pe.wait_ge(s_pe, g * 4 + (2 * i + c + 1))
                                        for k in range(DK):
                                            m = pe.matmul(pp[2 * i + c][:, :], w[:, k, c * P:(c + 1) * P], src[:, k, ds(g * GT, GT)], start=(k == 0), stop=(k == DK - 1))
                                        m.then_inc(s_pj, 1)

                        @block.vector
                        def _(v):
                            nc.vector.memset(wsel[:, :, :, :], 0.0).then_inc(s_z, 1)
                            v.wait_ge(s_vt, 1)
                            nc.vector.tensor_copy(vcol[:, :], pv[:, 0:4]).then_inc(s_vc, 1)
                            v.wait_ge(s_z, 1)
                            v.wait_ge(s_vc, 1)
                            for c in range(DK):
                                for u in range(UB // DK):
                                    m = nc.vector.tensor_copy(wsel[:, c, u, u:u + 1], vcol[:, c:c + 1])
                            m.then_inc(s_vc, 1)

                        @block.scalar
                        def _(act):
                            act.sem_inc(s_pe, 4)
                            act.wait_ge(s_vc, 2)
                            with act.Fori(0, NG) as g:
                                for i, dst in enumerate((featT, txtT)):
                                    for c in range(DK):
                                        act.wait_ge(s_pj, g * 4 + (2 * i + c + 1))
                                        d = dst[:, c, ds(g * GT, GT)]
                                        if i == 0:
                                            act.activation(d, pp[c][:, :], ACT.Identity, bias=vcol[:, 2 + c:3 + c]).then_inc(s_pe, 1)
                                        else:
                                            act.activation(d, pp[2 + c][:, :], ACT.Copy).then_inc(s_pe, 1)

                st = ExitStack()
                with st:
                    R = lambda n: sem(n + tag, st)
                    U = lambda n, shape, dt=F32: sb(n + tag, shape, dt, st)
                    th = [U(f"th{i}", [P, FB, P]) for i in range(RING)]
                    cx = U("cx", [P, D])
                    rv, rho = U("rv", [P, 512]), U("rho", [P, P])
                    qm = U("qm", [P, P], I32)
                    qn = U("qn", [P, P])
                    rs, pr, pT = U("rs", [P, P]), U("pr", [P, P]), U("pT", [P, P])
                    nmx, sm = U("nmx", [P, 1]), U("sm", [P, 1])
                    dot, rsm, pre, ws = U("dot", [P, 2]), U("rsm", [P, 1]), U("pre", [P, 2]), U("ws", [P, 2])
                    sc2 = U("sc2", [P, 2])
                    junk = U("junk", [P, 2, D])
                    upd = U("upd", [P, 2, D])
                    pbk = lambda n: st.enter_context(nc.psum_tensor(n + tag, [P, 512], F32))
                    prho, pt2, ptx = pbk("prho"), pbk("pt2"), pbk("ptx")
                    s_sum, s_th, s_use = R("sums_ready"), R("tanh_ready"), R("unit_used")
                    s_rv, s_rho, s_qm, s_qn, s_rs = R("rho_evacuated"), R("rho_sorted"), R("mask_loaded"), R("mask_read"), R("rho_masked")
                    s_nm, s_p, s_t2, s_pT = R("nmax_ready"), R("probs_ready"), R("probs_turned"), R("probsT_ready")
                    s_cx, s_tx, s_d, s_pre, s_ws, s_up = R("text_loaded"), R("text_mixed"), R("dot_step"), R("pre_ready"), R("ws_ready"), R("tile_step")

                    V_AT = {4: 0, 8: 1, 11: 2, 14: 3}
                    P_AT = {5: 0, 8: 1}
                    A_AT = {0: 0, 5: 1, 11: 2}

                    with nc.Block() as block:
                        @block.sync
                        def _(sp):
                            cd = t["ctx_1024"]
                            with sp.Fori(0, B) as b:
                                sp.wait_ge(s_qn, b)
                                sp.dma_start(qm[:, :], t["mask_BxS2_ik0"][ds(b, 1), :].to_broadcast([P, P])).then_inc(s_qm, 16)
                                sp.wait_ge(s_tx, b)
                                sp.dma_start(cx[:, :], cd[ds(b, 1)].rearrange("a s d -> (a s) d")).then_inc(s_cx, 16)
                                sp.wait_ge(s_rv, b + 1)
                                for j in range(4):
                                    sp.dma_start(rho[32 * j:32 * j + 32, :], rv[32 * j:32 * j + UB // DK, :].rearrange("u (i k) -> u i k", i=4)).then_inc(s_rho, 16)

                        @block.vector
                        def _(v):
                            V = nc.vector

                            def post(b, part):
                                if part == 0:
                                    v.wait_ge(s_qm, b * 16 + 16)
                                    V.tensor_scalar(qn[:, :], qm[:, :], -1.0, 1.0, ALU.mult, ALU.add).then_inc(s_qn, 1)
                                    v.wait_ge(s_qn, b + 1)
                                    v.wait_ge(s_rho, b * 64 + 64)
                                    V.scalar_tensor_tensor(out=rs[:, :], in0=qn[:, :], scalar=NEG, in1=rho[:, :], op0=ALU.mult, op1=ALU.add).then_inc(s_rs, 1)
                                    v.wait_ge(s_rs, b + 1)
                                    V.tensor_reduce(nmx[:, :], rs[:, :], AX.X, ALU.max, negate=True).then_inc(s_nm, 1)
                                elif part == 1:
                                    v.wait_ge(s_t2, b + 1)
                                    V.tensor_copy(pT[:, :], pt2[:, 0:P]).then_inc(s_pT, 1)
                                elif part == 2:
                                    v.wait_ge(s_tx, b + 1)
                                    for i in range(2):
                                        V.tensor_tensor_reduce(junk[:, i, :], ptx[:, 0:D], wcb[:, i, :], 1.0, 0.0, ALU.mult, ALU.add, dot[:, i:i + 1]).then_inc(s_d, 1)
                                    V.reciprocal(rsm[:, :], sm[:, :]).then_inc(s_d, 1)
                                    v.wait_ge(s_d, b * 4 + 3)
                                    V.tensor_scalar(sc2[:, :], dot[:, :], rsm[:, 0:1], None, ALU.mult).then_inc(s_d, 1)
                                    v.wait_ge(s_d, b * 4 + 4)
                                    V.tensor_tensor(pre[:, :], sc2[:, :], bc[:, :], ALU.add).then_inc(s_pre, 1)
                                else:
                                    v.wait_ge(s_ws, b + 1)
                                    xb = x[:, ds(b, 1), :].rearrange("p a c -> p (a c)")
                                    V.tensor_scalar(upd[:, 0, :], xb, mean[:, ds(b, 1)], rstd[:, ds(b, 1)], ALU.subtract, ALU.mult).then_inc(s_up, 1)
                                    v.wait_ge(s_up, b * 3 + 1)
                                    V.tensor_scalar(upd[:, 1, :], upd[:, 0, :], ws[:, 0:1], ws[:, 1:2], ALU.mult, ALU.add).then_inc(s_up, 1)
                                    v.wait_ge(s_up, b * 3 + 2)
                                    V.scalar_tensor_tensor(out=xb, in0=upd[:, 1, :], scalar=gate[:, 2:3], in1=xb, op0=ALU.mult, op1=ALU.add).then_inc(s_up, 1)

                            def batch(b, before):
                                for i in range(UB):
                                    u, c = i // DK, i % DK
                                    v.wait_ge(s_use, b * UB + (i + 1))
                                    V.tensor_tensor(th[i % RING][:, :, :].rearrange("p (j i) k -> p j i k", i=4),
                                                    featT[:, c, ds(b * P, P)].rearrange("p (j f) -> p j f", j=4)[:, :, 4 * u:4 * u + 4].unsqueeze(3).to_broadcast([P, 4, 4, P]),
                                                    txtT[:, c, ds(b * P, P)].unsqueeze(1).unsqueeze(1).to_broadcast([P, 4, 4, P]), ALU.add).then_inc(s_sum, 1)
                                    if before is not None and i in V_AT:
                                        post(before, V_AT[i])

                            batch(0, None)
                            with v.Fori(1, B) as b:
                                batch(b, b - 1)
                            for part in range(4):
                                post(B - 1, part)

                        @block.scalar
                        def _(act):
                            def post(b, part):
                                if part == 0:
                                    act.wait_ge(s_use, b * UB + (UB + RING))
                                    act.activation(rv[:, :], prho[:, :], ACT.Copy).then_inc(s_rv, 1)
                                elif part == 1:
                                    act.wait_ge(s_nm, b + 1)
                                    act.activation(pr[:, :], rs[:, :], ACT.Exp, bias=nmx[:, 0:1], accum_out=sm[:, 0:1]).then_inc(s_p, 1)
                                else:
                                    act.wait_ge(s_pre, b + 1)
                                    act.activation(ws[:, :], pre[:, :], ACT.Tanh).then_inc(s_ws, 1)

                            def batch(b, before):
                                for i in range(UB):
                                    act.wait_ge(s_sum, b * UB + (i + 1))
                                    act.activation(th[i % RING][:, :, :], th[i % RING][:, :, :], ACT.Tanh).then_inc(s_th, 1)
                                    if before is not None and i in A_AT:
                                        post(before, A_AT[i])

                            batch(0, None)
                            with act.Fori(1, B) as b:
                                batch(b, b - 1)
                            for part in range(3):
                                post(B - 1, part)

                        @block.tensor
                        def _(pe):
                            pe.sem_inc(s_use, RING)

                            def post(b, part):
                                if part == 0:
                                    pe.wait_ge(s_p, b + 1)
                                    pe.transpose(pt2[:, 0:P], pr[:, :], ident[:, :]).then_inc(s_t2, 1)
                                else:
                                    pe.wait_ge(s_pT, b + 1)
                                    pe.wait_ge(s_cx, b * 16 + 16)
                                    pe.matmul(ptx[:, 0:D], pT[:, :], cx[:, :], start=True, stop=True).then_inc(s_tx, 1)

                            def batch(b, before):
                                if before is not None:
                                    pe.wait_ge(s_rv, b)
                                for i in range(UB):
                                    u, c = i // DK, i % DK
                                    pe.wait_ge(s_th, b * UB + (i + 1))
                                    for j in range(4):
                                        m = pe.matmul(prho[32 * j:32 * j + 32, :], wsel[:, c, u, :], th[i % RING][:, 4 * j:4 * j + 4, :],
                                                      start=(i == 0), stop=(i == UB - 1))
                                    m.then_inc(s_use, 1)
                                    if before is not None and i in P_AT:
                                        post(before, P_AT[i])

                            batch(0, None)
                            with pe.Fori(1, B) as b:
                                batch(b, b - 1)
                            for part in range(2):
                                post(B - 1, part)

        def store():
            with nc.Block() as block:
                @block.sync
                def _(sp):
                    sp.dma_start(out.rearrange("b s d -> s b d"), x[:, :, :]).then_inc(s_out, 16)
                    sp.wait_ge(s_out, 16)

        def weights3():
            s_w3 = sem("w3_loaded")
            with nc.Block() as block:
                @block.sync
                def _(sp):
                    for w, name in ((wq, "wq_w"), (wk, "wk_w"), (wv, "wv_w"), (wo, "wo_w")):
                        sp.dma_start(w[:, :, :], t["L3_xattn_" + name].rearrange("(k p) n -> p k n", p=P)).then_inc(s_w3, 16)
                    sp.wait_ge(s_w3, 64)

        setup()
        with nc.Block() as block:
            @block.vector
            def _(v):
                v.wait_ge(s_x, 16)

            @block.tensor
            def _(pe):
                pe.wait_ge(s_w0, 64)
        if 0 in layers:
            attention(0, "_a0")
            semaphores_cleared()
        if 1 in layers:
            bitlinear(0, "_f0")
            semaphores_cleared()
        if 2 in layers:
            attention(1, "_a1")
            semaphores_cleared()
        if 3 in layers:
            experts(1, "_f1")
            semaphores_cleared()
        if 4 in layers:
            additive("_a2")
            semaphores_cleared()
        if 5 in layers:
            bitlinear(2, "_f2")
            semaphores_cleared()
        if 6 in layers:
            weights3()
            attention(3, "_a3")
            semaphores_cleared()
        if 7 in layers:
            experts(3, "_f3")
        store()


_SKIP = ("mask_BxS_ff1",)


def kernel(**inputs):
    import numpy as _np
    import concourse.bacc as _bacc
    from concourse.bass_utils import run_bass_kernel_spmd as _run

    nc = _bacc.Bacc("TRN2", target_bir_lowering=False, num_devices=1)
    arrays, aps = {}, {}
    for name, value in inputs.items():
        if name in _SKIP:
            continue
        a = _np.ascontiguousarray(value)
        arrays[f"in_{name}"] = a
        aps[name] = nc.dram_tensor(f"in_{name}", a.shape, mybir.dt.from_np(a.dtype), kind="ExternalInput").ap()
    out = nc.dram_tensor("out", (B, P, D), F32, kind="ExternalOutput").ap()
    build(nc, aps, out)
    r = _run(nc, [arrays], core_ids=[0])
    return r.results[0]["out"]
```

```python
from contextlib import ExitStack

import concourse.bass as bass
from concourse import mybir

ALU = mybir.AluOpType
ACT = mybir.ActivationFunctionType
AX = mybir.AxisListType
F32 = mybir.dt.float32
BF16 = mybir.dt.bfloat16
I32 = mybir.dt.int32

P = 128
B = 16
D = 256
DK = D // P
G = 4
NG = B // G
GT = G * P
H = 16
E = 8
F = 1024
FC = F // P
LN_EPS = 1e-5
ROUND = 12582912.0
BIG = 1e9


def ds(i, n):
    return bass.ds(i, n)


def build(nc, t, out, layers=range(8)):
    outer = ExitStack()
    with outer:
        passing = []

        def sem(name, stack=outer):
            h = nc.alloc_semaphore(name=name)
            if stack is not outer:
                passing.append(h)
            return h

        def semaphores_cleared():
            nc.clear_and_free_semaphores(list(passing))
            passing.clear()
            nc.all_engine_barrier()

        def sb(name, shape, dt=F32, stack=outer):
            return stack.enter_context(nc.sbuf_tensor(name, shape, dt))

        def banks(stack, names):
            return {n: stack.enter_context(nc.psum_tensor(n, [P, 512], F32)) for n in names}

        x = sb("x", [P, B, D])
        xnT = sb("xnT", [P, DK, B * P])
        ctxT = sb("ctxT", [P, DK, B * P])
        ident = sb("ident", [P, P])
        identb = sb("identb", [P, P], BF16)
        ones = sb("ones", [P, 512])
        gate = sb("gate", [P, 8])
        nhalf = sb("nhalf", [P, B])
        stats = sb("stats", [P, B, 6])
        mom = sb("mom", [P, 5, B])
        mean = sb("mean", [P, B])
        veps = sb("veps", [P, B])
        rstd = sb("rstd", [P, B])
        cols = sb("cols", [P, 96])
        wq = sb("wq", [P, DK, 1024])
        wk = sb("wk", [P, DK, 1024])
        wv = sb("wv", [P, DK, 1024])
        wo = sb("wo", [P, 8, D])
        wq1 = sb("wq1", [P, DK, 512])
        wk1 = sb("wk1", [P, DK, 512])
        wv1 = sb("wv1", [P, DK, D])
        wo1 = sb("wo1", [P, 4, D])
        rows1 = sb("rows1", [2, 2, 512])
        mrow = sb("mrow", [2, B * P])
        tern0 = sb("tern0", [P, DK, D], BF16)
        tern1 = sb("tern1", [P, DK, F], BF16)
        tern2 = sb("tern2", [P, FC, D], BF16)
        wscale = sb("wscale", [P, 4])

        s_x = sem("x_loaded")
        s_w0 = sem("w0_loaded")
        s_w3 = sem("w3_loaded")
        s_out = sem("out_stored")

        def setup():
            st = ExitStack()
            with st:
                S = lambda n: sem(n, st)
                ctx_in = sb("ctx_in", [P, 2, G, D], F32, st)
                brow = sb("brow", [96, P], F32, st)
                win = sb("win", [P, 4, DK, D], F32, st)
                wop = sb("wop", [P, DK, 512], F32, st)
                packed = sb("packed", [64, D], I32, st)
                code = sb("code", [64, 4, D], I32, st)
                ternp = sb("ternp", [64, 4, D], BF16, st)
                w1in = sb("w1in", [P, FC, D], F32, st)
                w2in = sb("w2in", [P, DK, F], F32, st)
                absw = sb("absw", [P, 2], F32, st)
                q1 = sb("q1", [P, FC, D], BF16, st)
                q2 = sb("q2", [P, DK, F], BF16, st)
                mint = sb("mint", [2, B * P], I32, st)
                g_in = sb("g_in", [P, 8], F32, st)
                ps = banks(st, [f"set{i}" for i in range(6)])
                pf = [ps[f"set{i}"] for i in range(6)]
                pb = [st.enter_context(nc.psum_tensor(f"setb{i}", [P, 1024], BF16)) for i in range(2)]
                s_ctx = [S("ctx_even_loaded"), S("ctx_odd_loaded")]
                s_ctxT, s_ctxE = S("ctx_turned"), S("ctx_evacuated")
                s_small, s_win, s_packed, s_w12, s_pad = S("small_loaded"), S("w1x_loaded"), S("packed_loaded"), S("w12_loaded"), S("pads_zero")
                s_id, s_dve, s_turn, s_evac = S("ident_ready"), S("dve_step"), S("weight_turned"), S("weight_evacuated")
                s_rows, s_wop = S("rows_loaded"), S("wo1_padded")
                s_sum, s_g = S("abs_summed"), S("g_step")
                s_q = S("ternary_ready")

                with nc.Block() as block:
                    @block.sync
                    def _(sp):
                        cv = t["ctx_1024"].rearrange("(g a) s d -> g s a d", a=G)
                        sp.dma_start(ctx_in[:, 0, :, :], cv[0]).then_inc(s_ctx[0], 16)
                        sp.dma_start(ctx_in[:, 1, :, :], cv[1]).then_inc(s_ctx[1], 16)
                        sp.dma_start(x[:, :, :], t["x"].rearrange("b s d -> s b d")).then_inc(s_x, 16)
                        for n in range(2, NG):
                            sp.wait_ge(s_ctxT, 2 * (n - 2) + 2)
                            sp.dma_start(ctx_in[:, n % 2, :, :], cv[n]).then_inc(s_ctx[n % 2], 16)
                        sp.dma_start(wq[:, :, :], t["L0_xattn_Wq"].rearrange("(k p) n -> p k n", p=P)).then_inc(s_w0, 16)
                        sp.dma_start(wk[:, :, :], t["L0_xattn_Wk"].rearrange("(k p) n -> p k n", p=P)).then_inc(s_w0, 16)
                        sp.dma_start(wv[:, :, :], t["L0_xattn_Wv"].rearrange("(k p) n -> p k n", p=P)).then_inc(s_w0, 16)
                        sp.dma_start(wo[:, :, :], t["L0_xattn_Wo"].rearrange("(k p) n -> p k n", p=P)).then_inc(s_w0, 16)
                        sp.dma_start(w1in[:, :, :], t["L2_ffn_W1"].rearrange("(k p) n -> p k n", p=P)).then_inc(s_w12, 16)
                        sp.dma_start(w2in[:, :, :], t["L2_ffn_W2"].rearrange("(k p) n -> p k n", p=P)).then_inc(s_w12, 16)

                    @block.gpsimd
                    def _(pool):
                        pool.memset(ident[:, :], 0.0).then_inc(s_id, 1)
                        pool.memset(ones[:, :], 1.0).then_inc(s_id, 1)
                        pool.wait_ge(s_id, 2)
                        pool.affine_select(out=ident[:, :], in_=ident[:, :], compare_op=ALU.not_equal, fill=1.0,
                                           base=0, pattern=[[-1, P]], channel_multiplier=1).then_inc(s_id, 1)
                        pool.wait_ge(s_id, 3)
                        pool.tensor_copy(identb[:, :], ident[:, :]).then_inc(s_id, 1)
                        pool.memset(nhalf[:, :], -0.5).then_inc(s_id, 1)
                        pool.memset(wq1[:, :, :], 0.0).then_inc(s_pad, 1)
                        pool.memset(wk1[:, :, :], 0.0).then_inc(s_pad, 1)
                        pool.memset(rows1[:, :, :], 0.0).then_inc(s_pad, 1)
                        pool.memset(wop[:, :, :], 0.0).then_inc(s_pad, 1)
                        pool.wait_ge(s_pad, 4)
                        r1 = rows1[:, :, :].rearrange("r a (h c) -> r a h c", c=32)
                        pool.memset(r1[0:1, 0, :, 16], 1.0).then_inc(s_pad, 1)
                        pool.memset(r1[0:1, 1, :, 16], 4.0 * BIG).then_inc(s_pad, 1)
                        pool.wait_ge(s_win, 64)
                        pool.tensor_copy(wop[:, :, :].rearrange("p o (h c) -> p o h c", c=32)[:, :, :, 0:16],
                                         win[:, 3, :, :].rearrange("p o (h c) -> p o h c", c=16)).then_inc(s_wop, 1)

                    @block.scalar
                    def _(act):
                        row = lambda a: a.rearrange("(c p) -> c p", p=P)
                        act.dma_start(brow[0:8, :], row(t["L0_xattn_bq"])).then_inc(s_small, 16)
                        act.dma_start(brow[8:16, :], row(t["L0_xattn_bk"])).then_inc(s_small, 16)
                        act.dma_start(brow[16:24, :], row(t["L3_xattn_wq_b"])).then_inc(s_small, 16)
                        act.dma_start(brow[24:32, :], row(t["L3_xattn_wk_b"])).then_inc(s_small, 16)
                        act.dma_start(brow[32:96, :], t["L1_ffn_b1"].rearrange("e (c p) -> (e c) p", p=P)).then_inc(s_small, 16)
                        act.dma_start(g_in[:, 0:4], t["g_xattn"].rearrange("(a n) -> a n", a=1).to_broadcast([P, 4])).then_inc(s_small, 16)
                        act.dma_start(g_in[:, 4:8], t["g_ffn"].rearrange("(a n) -> a n", a=1).to_broadcast([P, 4])).then_inc(s_small, 16)
                        act.dma_start(mint[:, :], t["mask_Bx1x1xS2_ik0"].rearrange("b i j s -> (i j) (b s)").to_broadcast([2, B * P])).then_inc(s_small, 16)
                        for n, w in enumerate(("Wq", "Wk", "Wv", "Wo")):
                            act.dma_start(win[:, n, :, :], t["L1_xattn_" + w].rearrange("(k p) n -> p k n", p=P)).then_inc(s_win, 16)
                        act.dma_start(packed[:, :], t["L0_ffn_packed_weight"].rearrange("(p n) -> p n", n=D)).then_inc(s_packed, 16)
                        act.wait_ge(s_pad, 6)
                        r1 = rows1[:, :, :].rearrange("r a (h c) -> r a h c", c=32)
                        act.dma_start(r1[0:1, 0, :, 0:16], t["L1_xattn_bq"].rearrange("(a h c) -> a h c", a=1, c=16)).then_inc(s_rows, 16)
                        act.dma_start(r1[1:2, 1, :, 0:16], t["L1_xattn_bk"].rearrange("(a h c) -> a h c", a=1, c=16)).then_inc(s_rows, 16)
                        act.wait_ge(s_small, 16 * 8)
                        act.activation(gate[:, :], g_in[:, :], ACT.Tanh).then_inc(s_g, 1)
                        for n in range(NG):
                            for k in range(DK):
                                act.wait_ge(s_ctxT, 2 * n + k + 1)
                                act.activation(ctxT[:, k, n * GT:(n + 1) * GT], pf[(2 * n + k) % 4][:, :], ACT.Copy).then_inc(s_ctxE, 1)
                        act.wait_ge(s_rows, 32)

                    jobs = []
                    for n, w in enumerate((wq1, wk1)):
                        for k in range(DK):
                            jobs.append(("f", [win[:, n, o, k * P:(k + 1) * P] for o in range(DK)],
                                         w[:, k, :].rearrange("p (h c) -> p h c", c=32)[:, :, 0:16],
                                         lambda ap: ap[:, 0:256].rearrange("p (h c) -> p h c", c=16), "win"))
                    for k in range(DK):
                        jobs.append(("f", [win[:, 2, o, k * P:(k + 1) * P] for o in range(DK)],
                                     wv1[:, k, :], lambda ap: ap[:, 0:256], "win"))
                    for k in range(4):
                        jobs.append(("f", [wop[:, o, k * P:(k + 1) * P] for o in range(DK)],
                                     wo1[:, k, :], lambda ap: ap[:, 0:256], "wop"))
                    jobs.append(("f", [brow[:, :]], cols[:, :], lambda ap: ap[:, 0:96], "rows"))
                    for k in range(DK):
                        jobs.append(("b", [ternp[:, s, k * P:(k + 1) * P] for s in range(4)],
                                     tern0[:, k, :], lambda ap: ap[:, 0:256], "tern"))
                    for k in range(DK):
                        for half in range(2):
                            jobs.append(("b", [q1[:, 4 * half + o, k * P:(k + 1) * P] for o in range(4)],
                                         tern1[:, k, half * 512:(half + 1) * 512], lambda ap: ap[:, 0:512], "q1"))
                    for k in range(FC):
                        jobs.append(("b", [q2[:, o, k * P:(k + 1) * P] for o in range(DK)],
                                     tern2[:, k, :], lambda ap: ap[:, 0:256], "q2"))
                    EARLY = 13
                    READY = {"win": (s_win, 64), "wop": (s_wop, 1), "rows": (s_small, 128), "tern": (s_q, 4), "q1": (s_q, 5), "q2": (s_q, 6)}

                    @block.tensor
                    def _(pe):
                        pe.wait_ge(s_id, 5)
                        for n in range(NG):
                            pe.wait_ge(s_ctx[n % 2], 16 * (n // 2 + 1))
                            for k in range(DK):
                                if n >= 2:
                                    pe.wait_ge(s_ctxE, 2 * (n - 2) + k + 1)
                                for a in range(G):
                                    m = pe.transpose(pf[(2 * n + k) % 4][:, a * P:(a + 1) * P], ctx_in[:, n % 2, a, k * P:(k + 1) * P], ident[:, :])
                                m.then_inc(s_ctxT, 1)

                        def turn(n, kind, srcs, what):
                            pe.wait_ge(*READY[what])
                            if n >= 2:
                                pe.wait_ge(s_evac, n - 1)
                            bank = (pf[4:6] if kind == "f" else pb)[n % 2]
                            at = 0
                            for src in srcs:
                                rows, width = src.shape[0], src.shape[1]
                                m = pe.transpose(bank[0:width, at:at + rows], src, (ident if kind == "f" else identb)[0:rows, 0:rows])
                                at += rows
                            m.then_inc(s_turn, 1)

                        for n, (kind, srcs, _, _, what) in enumerate(jobs[:EARLY]):
                            turn(n, kind, srcs, what)
                        pe.wait_ge(s_sum, 2)
                        pe.wait_ge(s_ctxE, 2 * NG)
                        pe.matmul(pf[0][:, 0:2], ones[:, 0:P], absw[:, :], start=True, stop=True).then_inc(s_sum, 1)
                        for n, (kind, srcs, _, _, what) in enumerate(jobs[EARLY:]):
                            turn(n + EARLY, kind, srcs, what)

                    @block.vector
                    def _(v):
                        v.wait_ge(s_packed, 16)
                        for s in range(4):
                            nc.vector.tensor_scalar(code[:, s, :], packed[:, :], 2 * s, 3, ALU.logical_shift_right, ALU.bitwise_and).then_inc(s_dve, 1)
                        for s in range(4):
                            v.wait_ge(s_dve, s + 1)
                            nc.vector.tensor_scalar(ternp[:, s, :], code[:, s, :], -1.0, None, ALU.add).then_inc(s_q, 1)
                        v.wait_ge(s_small, 128)
                        v.wait_ge(s_id, 5)
                        nc.vector.tensor_scalar(mrow[:, :], mint[:, :], 0.0, ident[0:2, 0:1], ALU.not_equal, ALU.subtract).then_inc(s_dve, 1)
                        v.wait_ge(s_pad, 6)

                        def evac(n):
                            kind, _, dst, view, _ = jobs[n]
                            v.wait_ge(s_turn, n + 1)
                            bank = (pf[4:6] if kind == "f" else pb)[n % 2]
                            nc.vector.tensor_copy(dst, view(bank)).then_inc(s_evac, 1)

                        for n in range(EARLY):
                            evac(n)
                        v.wait_ge(s_w12, 32)
                        nc.vector.tensor_reduce(absw[:, 0:1], w1in[:, :, :], AX.XY, ALU.add, apply_absolute_value=True).then_inc(s_sum, 1)
                        nc.vector.tensor_reduce(absw[:, 1:2], w2in[:, :, :], AX.XY, ALU.add, apply_absolute_value=True).then_inc(s_sum, 1)
                        v.wait_ge(s_sum, 3)
                        nc.vector.tensor_scalar(wscale[:, 0:2], pf[0][:, 0:2], 1.0 / (D * F), 1e-5, ALU.mult, ALU.max).then_inc(s_dve, 1)
                        v.wait_ge(s_dve, 6)
                        nc.vector.reciprocal(wscale[:, 2:4], wscale[:, 0:2]).then_inc(s_dve, 1)
                        v.wait_ge(s_dve, 7)
                        for n, (w, q) in enumerate(((w1in, q1), (w2in, q2))):
                            nc.vector.tensor_scalar(w[:, :, :], w[:, :, :], wscale[:, 2 + n:3 + n], ROUND, ALU.mult, ALU.add).then_inc(s_dve, 1)
                        for n, (w, q) in enumerate(((w1in, q1), (w2in, q2))):
                            v.wait_ge(s_dve, 8 + n)
                            nc.vector.tensor_scalar(w[:, :, :], w[:, :, :], ROUND, -1.0, ALU.subtract, ALU.max).then_inc(s_dve, 1)
                        for n, (w, q) in enumerate(((w1in, q1), (w2in, q2))):
                            v.wait_ge(s_dve, 10 + n)
                            nc.vector.tensor_scalar(q[:, :, :], w[:, :, :], 1.0, None, ALU.min).then_inc(s_q, 1)
                        for n in range(EARLY, len(jobs)):
                            evac(n)

        def weights3(sp):
            for w, name in ((wk, "wk_w"), (wq, "wq_w"), (wv, "wv_w"), (wo, "wo_w")):
                sp.dma_start(w[:, :, :], t["L3_xattn_" + name].rearrange("(k p) n -> p k n", p=P)).then_inc(s_w3, 16)

        def moments_vector(v, s_st, s_mo, s_step, before=0):
            with v.Fori(0, B) as b:
                nc.vector.bn_stats(stats[:, ds(b, 1), :].rearrange("p a c -> p (a c)"),
                                   x[:, ds(b, 1), :].rearrange("p a c -> p (a c)")).then_inc(s_st, 1)
            v.wait_ge(s_st, B)
            me, ve, mo, vo = (stats[:, :, i] for i in (1, 2, 4, 5))
            nc.vector.tensor_tensor(mom[:, 0, :], me, mo, ALU.add).then_inc(s_step, 1)
            nc.vector.tensor_tensor(mom[:, 1, :], me, mo, ALU.subtract).then_inc(s_step, 1)
            nc.vector.tensor_tensor(mom[:, 2, :], ve, vo, ALU.add).then_inc(s_step, 1)
            v.wait_ge(s_step, before + 1)
            nc.vector.tensor_scalar(mean[:, :], mom[:, 0, :], 0.5, None, ALU.mult).then_inc(s_step, 1)
            v.wait_ge(s_step, before + 2)
            nc.vector.scalar_tensor_tensor(out=mom[:, 3, :], in0=mom[:, 1, :], scalar=0.25, in1=mom[:, 1, :],
                                           op0=ALU.mult, op1=ALU.mult).then_inc(s_step, 1)
            v.wait_ge(s_step, before + 3)
            nc.vector.tensor_scalar(mom[:, 4, :], mom[:, 2, :], 1.0 / D, LN_EPS, ALU.mult, ALU.add).then_inc(s_step, 1)
            v.wait_ge(s_step, before + 6)
            nc.vector.tensor_tensor(veps[:, :], mom[:, 4, :], mom[:, 3, :], ALU.add).then_inc(s_mo, 1)

        def root_pool(pool, s_mo, s_rs):
            pool.wait_ge(s_mo, 1)
            pool.tensor_tensor(rstd[:, :], veps[:, :], nhalf[:, :], ALU.pow).then_inc(s_rs, 1)

        def norm_transposed(block, st, tag, keep=None):
            S = lambda n: sem(n + tag, st)
            xn = sb("xn" + tag, [P, 2, G, D], F32, st)
            ps = banks(st, [f"xt{i}" + tag for i in range(4)])
            pt = [ps[f"xt{i}" + tag] for i in range(4)]
            s_st, s_mo, s_step, s_rs = S("stats_done"), S("moments_done"), S("moment_step"), S("rstd_done")
            s_xn, s_turn, s_ev = S("xn_ready"), S("xn_turned"), S("xn_evacuated")

            @block.gpsimd
            def _(pool):
                root_pool(pool, s_mo, s_rs)

            @block.vector
            def _(v):
                moments_vector(v, s_st, s_mo, s_step)
                v.wait_ge(s_rs, 1)
                with v.Fori(0, NG // 2) as r:
                    for j in range(2):
                        v.wait_ge(s_turn, r * 4 + 2 * j + 2)
                        for a in range(G):
                            b = r * 8 + (G * j + a)
                            if keep is not None:
                                nc.vector.tensor_scalar(keep[:, ds(b, 1), :].rearrange("p a c -> p (a c)"), x[:, ds(b, 1), :].rearrange("p a c -> p (a c)"),
                                                        mean[:, ds(b, 1)], rstd[:, ds(b, 1)], ALU.subtract, ALU.mult)
                            m = nc.vector.tensor_scalar(xn[:, j, a, :], x[:, ds(b, 1), :].rearrange("p a c -> p (a c)"),
                                                        mean[:, ds(b, 1)], rstd[:, ds(b, 1)], ALU.subtract, ALU.mult)
                        m.then_inc(s_xn, 1)

            @block.tensor
            def _(pe):
                pe.sem_inc(s_turn, 4)
                with pe.Fori(0, NG // 2) as r:
                    for j in range(2):
                        pe.wait_ge(s_xn, r * 2 + j + 1)
                        for k in range(DK):
                            pe.wait_ge(s_ev, r * 4 + 2 * j + k + 1)
                            for a in range(G):
                                m = pe.transpose(pt[2 * j + k][:, a * P:(a + 1) * P], xn[:, j, a, k * P:(k + 1) * P], ident[:, :])
                            m.then_inc(s_turn, 1)

            @block.scalar
            def _(act):
                act.sem_inc(s_ev, 4)
                with act.Fori(0, NG // 2) as r:
                    for j in range(2):
                        for k in range(DK):
                            act.wait_ge(s_turn, r * 4 + 2 * j + k + 5)
                            act.activation(xnT[:, k, ds(r * 2 * GT + j * GT, GT)], pt[2 * j + k][:, :], ACT.Copy).then_inc(s_ev, 1)

        def attention(layer, tag):
            HP, DV, KT = {0: (64, 64, 1), 1: (32, 16, 1), 3: (64, 64, 2)}[layer]
            HC = P // HP
            NC = H // HC
            HU = 4 // KT
            CU = HU // HC
            U = H // HU
            N = G * U
            OB = NC // 4
            UO = U // OB
            VH = (H * DV + 511) // 512
            VW = H * DV // VH
            qscale = {0: 0.125, 1: 0.25, 3: 0.125}[layer]
            Wq, Wk, Wv, Wo = (wq1, wk1, wv1, wo1) if layer == 1 else (wq, wk, wv, wo)
            bcol = {0: 0, 3: 16}.get(layer)
            st = ExitStack()
            with st:
                S = lambda n: sem(n + tag, st)
                qT = sb("qT" + tag, [P, NC, GT], F32, st)
                kd = sb("kd" + tag, [P, NC, HC, GT], F32, st)
                cg = sb("cg" + tag, [P, DK, GT], F32, st)
                vv = sb("vv" + tag, [P, 2, H, HP], F32, st)
                prob = sb("prob" + tag, [P, 4, 512], F32, st)
                probT = sb("probT" + tag, [P, 2, 512], F32, st)
                nmax = sb("nmax" + tag, [P, 2, HU], F32, st)
                sums = sb("sums" + tag, [P, 4, HU], F32, st)
                rinv = sb("rinv" + tag, [P, 2, HU], F32, st)
                oT = sb("oT" + tag, [P, 2, NC, P], F32, st)
                bv = sb("bv" + tag, [P, H * DV], F32, st)
                bo = sb("bo" + tag, [1, D], F32, st)
                bqs = sb("bqs" + tag, [P, 8], F32, st)
                ps = banks(st, [n + tag for n in ("pp0", "pp1", "ps0", "ps1", "pt0", "pt1", "po", "pw")])
                pp = [ps["pp0" + tag], ps["pp1" + tag]]
                psc = [ps["ps0" + tag], ps["ps1" + tag]]
                ptr = [ps["pt0" + tag], ps["pt1" + tag]]
                po, pw = ps["po" + tag], ps["pw" + tag]
                s_bias, s_bq, s_pads = S("bias_loaded"), S("bq_scaled"), S("pads_cleared")
                s_cg = S("group_context_ready")
                s_st, s_mo, s_step, s_rs = S("stats_done"), S("moments_done"), S("moment_step"), S("rstd_done")
                s_xn, s_xt, s_xe = S("xn_ready"), S("xn_turned"), S("xn_evacuated")
                xgT = xnT[:, :, 0:GT]
                xn = xnT[:, 0, GT:GT + G * D].rearrange("p (a d) -> p a d", d=D)
                s_p, s_pf = S("proj_ready"), S("proj_evacuated")
                s_w, s_wf = S("work_ready"), S("work_evacuated")
                s_s, s_nm, s_e = S("scores_ready"), S("nmax_ready"), S("probs_ready")
                s_r, s_x = S("rinv_ready"), S("probs_scaled")
                s_t, s_tf = S("probs_turned"), S("turned_evacuated")
                s_pv, s_of = S("values_summed"), S("out_evacuated")
                pre = "L%d_xattn_" % layer
                bv_d, bo_d = (t[pre + "wv_b"], t[pre + "wo_b"]) if layer == 3 else (t[pre + "bv"], t[pre + "bo"])
                NP = 2 * NC
                TAIL = range(N + 2 if layer == 1 else N, N + 5)
                NW = G * (VH + 1)
                NO = G * OB

                after = {n: [] for n in range(N + 5)}
                for half in range(VH):
                    after[half].append((half, 0))
                for a in range(1, G):
                    after[a * U - U + 3].append((0, a))
                    if VH == 2:
                        after[a * U - U + 5].append((1, a))
                for a in range(G):
                    after[a * U + U + 4].append(("out", a))
                order = [use for n in range(N + 5) for use in after[n]]
                wv_last = order.index((VH - 1, G - 1))

                if layer == 1:
                    msk = sb("msk", [P, GT], I32, st)
                    val = sb("val", [P, GT], F32, st)
                    cm = sb("cm", [P, DK, GT], F32, st)
                    s_msk, s_val, s_cm = S("mask_loaded"), S("valid_ready"), S("masked_ready")
                if layer == 3:
                    md3 = [w[:, :, :].rearrange("p k n -> p (k n)").rearrange("p (c n) -> p c n", n=P) for w in (wq1, wk1)]
                    mv = wo1[:, :, :].rearrange("p k n -> p (k n)").rearrange("p (h d) -> p h d", d=HP)
                    s_mem, s_memT, s_memE = S("memory_loaded"), S("memory_turned"), S("memory_keys_ready")
                    mk_in = vv[:, 1, :, :].rearrange("p h d -> p (h d)")

                def tiles(bank):
                    return bank.rearrange("p (h t k) -> p h t k", h=HU, t=KT)

                with nc.Block() as block:
                    @block.sync
                    def _(sp):
                        sp.dma_start(bv[:, :], bv_d.rearrange("(a n) -> a n", a=1).to_broadcast([P, H * DV])).then_inc(s_bias, 16)
                        sp.dma_start(bo[:, :], bo_d.rearrange("(a n) -> a n", a=1)).then_inc(s_bias, 16)
                        if layer == 3:
                            sp.dma_start(mk_in, t["L3_xattn_mk"][0]).then_inc(s_mem, 16)
                            sp.dma_start(mv.rearrange("p h d -> p (h d)"), t["L3_xattn_mv"][0]).then_inc(s_mem, 16)
                        if layer == 1:
                            md = t["mask_Bx1x1xS2_ik0"].rearrange("b i j s -> (i j) (b s)")
                            with sp.Fori(0, NG) as g:
                                sp.wait_ge(s_val, g + 1)
                                sp.dma_start(msk[:, :], md[:, ds(g * GT, GT)].to_broadcast([P, GT])).then_inc(s_msk, 16)

                    @block.gpsimd
                    def _(pool):
                        pool.memset(kd[:, :, :, :], 0.0).then_inc(s_pads, 1)
                        if layer == 1:
                            pool.memset(vv[:, :, :, :], 0.0).then_inc(s_pads, 1)
                        if layer == 3:
                            for j in range(HC):
                                pool.memset(md3[j], 0.0).then_inc(s_pads, 1)
                        pool.sem_inc(s_x, 2)
                        root_pool(pool, s_mo, s_rs)

                        def group(g, first):
                            if not first:
                                pool.wait_ge(s_w, (g - 1) * NW + wv_last + 1)
                            pool.tensor_copy(cg[:, :, :], ctxT[:, :, ds(g * GT, GT)]).then_inc(s_cg, 1)
                            for n in range(N):
                                pool.wait_ge(s_r, g * N + n + 1)
                                pb = prob[:, n % 4, :].rearrange("p (h k) -> p h k", h=HU)
                                pool.tensor_tensor(pb, pb, rinv[:, n % 2, :].unsqueeze(2).to_broadcast([P, HU, KT * P]), ALU.mult).then_inc(s_x, 1)
                        group(0, True)
                        with pool.Fori(1, NG) as g:
                            group(g, False)

                    @block.tensor
                    def _(pe):
                        pe.sem_inc(s_t, 4)
                        if layer == 3:
                            pe.wait_ge(s_w3, 64)
                            pe.wait_ge(s_mem, 32)
                            for half in range(2):
                                for c in range(4):
                                    m = pe.transpose(ptr[half][:, c * P:(c + 1) * P], mk_in[:, (4 * half + c) * P:(4 * half + c + 1) * P], ident[:, :])
                                m.then_inc(s_memT, 1)
                            pe.wait_ge(s_memE, 4)
                        pe.wait_ge(s_bias, 32)
                        def project(g, i):
                            c, isk = i % NC, i < NC
                            if c == 0 and not isk:
                                pe.wait_ge(s_xn, g * G + G)
                                pe.wait_ge(s_e, g * N + 2)
                                for k in range(DK):
                                    for a in range(G):
                                        m = pe.transpose(psc[k][:, a * P:(a + 1) * P], xn[:, a, k * P:(k + 1) * P], ident[:, :])
                                    m.then_inc(s_xt, 1)
                                pe.wait_ge(s_xe, g * DK + DK)
                            pe.wait_ge(s_pf, g * NP + i + 1)
                            W = Wk if isk else Wq
                            for k in range(DK):
                                if isk and layer == 1:
                                    if c == 0 and k == 0:
                                        pe.wait_ge(s_cm, g * DK + DK)
                                    src = cm[:, k, :]
                                elif isk:
                                    src = ctxT[:, k, ds(g * GT, GT)]
                                else:
                                    src = xgT[:, k, :]
                                m = pe.matmul(pp[i % 2][:, :], W[:, k, c * P:(c + 1) * P], src,
                                              start=(k == 0), stop=(k == DK - 1 and layer != 1))
                            if layer == 1 and isk:
                                m = pe.matmul(pp[i % 2][:, :], rows1[0:2, 1, c * P:(c + 1) * P], mrow[0:2, ds(g * GT, GT)], start=False, stop=True)
                            elif layer == 1:
                                m = pe.matmul(pp[i % 2][:, :], rows1[0:1, 0, c * P:(c + 1) * P], ones[0:1, :], start=False, stop=True)
                            m.then_inc(s_p, 1)

                        def group(g, last):
                            pe.wait_ge(s_cg, g + 1)
                            w = [0]

                            def work(kind, a):
                                if kind != "out":
                                    pe.wait_ge(s_wf, g * NW + w[0] + 1)
                                    for k in range(DK):
                                        m = pe.matmul(pw[:, 0:VW], cg[:, k, a * P:(a + 1) * P], Wv[:, k, kind * VW:(kind + 1) * VW],
                                                      start=(k == 0), stop=(k == DK - 1))
                                    m.then_inc(s_w, 1)
                                    w[0] += 1
                                else:
                                    pe.wait_ge(s_of, g * NO + (a + 1) * OB + 1)
                                    pe.wait_ge(s_wf, g * NW + w[0] + 1)
                                    for c in range(NC):
                                        pe.matmul(pw[:, 0:D], oT[:, a % 2, c, :], Wo[:, c, :], start=(c == 0), stop=False)
                                    pe.matmul(pw[:, 0:D], ones[0:1, 0:P], bo[0:1, :], start=False, stop=True).then_inc(s_w, 1)
                                    w[0] += 1

                            pe.wait_ge(s_pf, g * NP + NP + 2)
                            for n in range(N + 5):
                                if n < N:
                                    a, u = n // U, n % U
                                    pe.wait_ge(s_e, g * N + n + 1)
                                    for i in range(CU):
                                        c = u * CU + i
                                        queries = qT[:, c, a * P:(a + 1) * P]
                                        scores = tiles(psc[n % 2][:, :])[:, i * HC:(i + 1) * HC]
                                        m = pe.matmul(scores[:, :, 0, :], queries, kd[:, c, :, a * P:(a + 1) * P], start=True, stop=True)
                                        if layer == 3:
                                            for j in range(HC):
                                                m = pe.matmul(scores[:, j, 1, :], queries, md3[j][:, c, :], start=True, stop=True)
                                    m.then_inc(s_s, 1)
                                if 2 <= n <= N + 1:
                                    m1 = n - 2
                                    pe.wait_ge(s_x, g * N + m1 + 3)
                                    pe.wait_ge(s_tf, g * N + m1 + 1)
                                    for i in range(4):
                                        m = pe.transpose(ptr[m1 % 2][:, i * P:(i + 1) * P], prob[:, m1 % 4, i * P:(i + 1) * P], ident[:, :])
                                    m.then_inc(s_t, 1)
                                if 3 <= n <= N + 2:
                                    m2 = n - 3
                                    a, u = m2 // U, m2 % U
                                    pe.wait_ge(s_tf, g * N + m2 + 3)
                                    if u == 0:
                                        pe.wait_ge(s_wf, g * NW + w[0] + 1)
                                    if u % UO == 0:
                                        pe.wait_ge(s_of, g * NO + m2 // UO + 1)
                                    for i in range(HU):
                                        h = u * HU + i
                                        p0, at = HP * (h % HC), (h // HC) % 4 * P
                                        for kt in range(KT):
                                            vals = mv[:, h, :] if kt else vv[:, a % 2, h, :]
                                            m = pe.matmul(po[p0:p0 + HP, at:at + P], vals, tiles(probT[:, m2 % 2, :])[:, i, kt, :],
                                                          start=(kt == 0), stop=(kt == KT - 1))
                                    m.then_inc(s_pv, 1)
                                for kind, a in after[n]:
                                    work(kind, a)
                                if n in TAIL and not last:
                                    project(g + 1, n - TAIL[0])
                            assert w[0] == NW
                            if not last:
                                for i in range(len(TAIL), NP):
                                    project(g + 1, i)

                        for i in range(NP):
                            project(0, i)
                        with pe.Fori(0, NG - 1) as g:
                            group(g, False)
                        group(NG - 1, True)

                    @block.scalar
                    def _(act):
                        act.sem_inc(s_pf, 2)
                        act.sem_inc(s_e, 2)
                        if bcol is not None:
                            act.activation(bqs[:, :], cols[:, bcol:bcol + 8], ACT.Copy, scale=qscale).then_inc(s_bq, 1)
                            act.wait_ge(s_bq, 1)
                        act.wait_ge(s_pads, 1)
                        def evacuate(g):
                            for i in range(NP):
                                c, isk = i % NC, i < NC
                                act.wait_ge(s_p, g * NP + i + 1)
                                src = pp[i % 2]
                                if not isk and layer == 1:
                                    m = act.activation(qT[:, c, :], src[:, :], ACT.Copy, scale=qscale)
                                elif not isk:
                                    m = act.activation(qT[:, c, :], src[:, :], ACT.Identity, bias=bqs[:, c:c + 1], scale=qscale)
                                else:
                                    for j in range(HC):
                                        own = slice(HP * j, HP * (j + 1))
                                        if layer == 1:
                                            m = act.activation(kd[own, c, j, :], src[own, :], ACT.Copy)
                                        else:
                                            m = act.activation(kd[own, c, j, :], src[own, :], ACT.Identity, bias=cols[own, bcol + 8 + c:bcol + 9 + c])
                                m.then_inc(s_pf, 1)

                        def group(g):
                            for n in range(N):
                                act.wait_ge(s_nm, g * N + n + 1)
                                act.wait_ge(s_t, g * N + n + 1)
                                for i in range(HU):
                                    m = act.activation(prob[:, n % 4, i * KT * P:(i + 1) * KT * P], psc[n % 2][:, i * KT * P:(i + 1) * KT * P],
                                                       ACT.Exp, bias=nmax[:, n % 2, i:i + 1], accum_out=sums[:, n % 4, i:i + 1])
                                m.then_inc(s_e, 1)

                        evacuate(0)
                        with act.Fori(0, NG - 1) as g:
                            group(g)
                            evacuate(g + 1)
                        group(NG - 1)

                    @block.vector
                    def _(v):
                        v.sem_inc(s_wf, 1)
                        v.sem_inc(s_tf, 2)
                        v.sem_inc(s_of, 1)
                        if layer == 1:
                            v.sem_inc(s_val, 1)
                            v.wait_ge(s_pads, 2)
                        if layer == 3:
                            v.wait_ge(s_pads, 1 + HC)
                            for half in range(2):
                                v.wait_ge(s_memT, half + 1)
                                for j in range(HC):
                                    own = slice(HP * j, HP * (j + 1))
                                    nc.vector.tensor_copy(md3[j][own, 4 * half:4 * half + 4, :], ptr[half][own, :].rearrange("p (c n) -> p c n", n=P)).then_inc(s_memE, 1)
                        moments_vector(v, s_st, s_mo, s_step)
                        v.wait_ge(s_bias, 32)
                        v.wait_ge(s_rs, 1)
                        def sources(g):
                            if layer == 1:
                                v.wait_ge(s_msk, (g + 1) * 16)
                                nc.vector.tensor_scalar(val[:, :], msk[:, :], 0.0, None, ALU.not_equal).then_inc(s_val, 1)
                                v.wait_ge(s_val, g + 2)
                                for k in range(DK):
                                    nc.vector.tensor_tensor(cm[:, k, :], ctxT[:, k, ds(g * GT, GT)], val[:, :], ALU.mult).then_inc(s_cm, 1)
                            for a in range(G):
                                b = g * G + a
                                nc.vector.tensor_scalar(xn[:, a, :], x[:, ds(b, 1), :].rearrange("p a c -> p (a c)"),
                                                        mean[:, ds(b, 1)], rstd[:, ds(b, 1)], ALU.subtract, ALU.mult).then_inc(s_xn, 1)

                        def turned_tokens(g):
                            for k in range(DK):
                                v.wait_ge(s_xt, g * DK + (k + 1))
                                nc.vector.tensor_copy(xgT[:, k, :], psc[k][:, :]).then_inc(s_xe, 1)

                        def group(g, last):
                            w = [0]

                            def work(kind, a):
                                v.wait_ge(s_w, g * NW + w[0] + 1)
                                if kind != "out":
                                    hh = H // VH
                                    as_heads = lambda ap: ap.rearrange("p (h d) -> p h d", d=DV)
                                    nc.vector.tensor_tensor(vv[:, a % 2, kind * hh:(kind + 1) * hh, 0:DV], as_heads(pw[:, 0:VW]),
                                                            as_heads(bv[:, kind * VW:(kind + 1) * VW]), ALU.add).then_inc(s_wf, 1)
                                    w[0] += 1
                                else:
                                    xb = x[:, ds(g * G + a, 1), :].rearrange("p a c -> p (a c)")
                                    nc.vector.scalar_tensor_tensor(out=xb, in0=pw[:, 0:D], scalar=gate[:, layer:layer + 1], in1=xb,
                                                                   op0=ALU.mult, op1=ALU.add).then_inc(s_wf, 1)
                                    w[0] += 1

                            for n in range(N + 5):
                                if 1 <= n <= N:
                                    m0 = n - 1
                                    v.wait_ge(s_e, g * N + m0 + 3)
                                    v.wait_ge(s_x, g * N + m0 + 1)
                                    nc.vector.reciprocal(rinv[:, m0 % 2, :], sums[:, m0 % 4, :]).then_inc(s_r, 1)
                                if n < N:
                                    v.wait_ge(s_s, g * N + n + 1)
                                    v.wait_ge(s_e, g * N + n + 1)
                                    nc.vector.tensor_reduce(nmax[:, n % 2, :], psc[n % 2][:, :].rearrange("p (h k) -> p h k", h=HU),
                                                            AX.X, ALU.max, negate=True).then_inc(s_nm, 1)
                                if 2 <= n <= N + 1:
                                    m1 = n - 2
                                    v.wait_ge(s_t, g * N + m1 + 5)
                                    if m1 >= 2:
                                        v.wait_ge(s_pv, g * N + m1 - 1)
                                    nc.vector.tensor_copy(probT[:, m1 % 2, :], ptr[m1 % 2][:, :]).then_inc(s_tf, 1)
                                if 3 <= n <= N + 2 and (n - 3) % UO == UO - 1:
                                    m2 = n - 3
                                    a, ob = m2 // U, m2 % U // UO
                                    v.wait_ge(s_pv, g * N + m2 + 1)
                                    nc.vector.tensor_copy(oT[:, a % 2, 4 * ob:4 * ob + 4, :], po[:, :].rearrange("p (c n) -> p c n", n=P)).then_inc(s_of, 1)
                                for kind, a in after[n]:
                                    work(kind, a)
                                if n == N + 1 and not last:
                                    sources(g + 1)
                            if not last:
                                turned_tokens(g + 1)

                        sources(0)
                        turned_tokens(0)
                        with v.Fori(0, NG - 1) as g:
                            group(g, False)
                        group(NG - 1, True)

        def bitlinear(layer, tag):
            two = layer == 2
            W1, N1 = (tern1, F) if two else (tern0, D)
            xnv = xnT[:, :, :].rearrange("p k n -> p (k n)").rearrange("p (b d) -> p b d", d=D)
            gcol = gate[:, 4 + layer:5 + layer]
            st = ExitStack()
            with st:
                S = lambda n: sem(n + tag, st)
                am = sb("am" + tag, [P, B], F32, st)
                am1 = sb("am1" + tag, [P, B], F32, st)
                up = sb("up" + tag, [P, B], F32, st)
                upr = sb("upr" + tag, [P, B], F32, st)
                down = sb("down" + tag, [P, B], F32, st)
                wsc = sb("wsc" + tag, [P, 2], F32, st)
                bias = sb("bias" + tag, [P, D], F32, st)
                gbias = sb("gbias" + tag, [P, D], F32, st)
                tmp = sb("tmp" + tag, [P, 2, D], F32, st)
                q = sb("q" + tag, [P, 2, D], BF16, st)
                qT = sb("qT" + tag, [P, 2, DK, P], BF16, st)
                s_st, s_mo, s_step, s_rs = S("stats_done"), S("moments_done"), S("moment_step"), S("rstd_done")
                s_b, s_n, s_am, s_x2 = S("bias_loaded"), S("xn_ready"), S("absmax_ready"), S("bias_added")
                s_d = S("dve_step")
                s_q, s_t, s_e = S("codes_ready"), S("codes_turned"), S("codes_evacuated")
                s_m, s_y = S("sums_ready"), S("tokens_done")
                pt = [st.enter_context(nc.psum_tensor(f"pt{i}{tag}", [P, 1024], BF16)) for i in range(2)]
                NY = 4 if two else 3
                if two:
                    b1 = sb("b1" + tag, [P, F], F32, st)
                    h = sb("h" + tag, [P, 2, F], F32, st)
                    tmp2 = sb("tmp2" + tag, [P, F], F32, st)
                    q2 = sb("q2" + tag, [P, 2, F], BF16, st)
                    q2T = sb("q2T" + tag, [P, 2, FC, P], BF16, st)
                    am2 = sb("am2" + tag, [P, 2, 5], F32, st)
                    ph = [st.enter_context(nc.psum_tensor(f"ph{i}{tag}", [P, 512], F32)) for i in range(2)]
                    pt2 = st.enter_context(nc.psum_tensor("pt2" + tag, [P, 1024], BF16))
                    s_h, s_gl, s_q2 = S("hidden_ready"), S("gelu_done"), S("codes2_ready")
                    s_m1, s_t2, s_e2 = S("sums1_ready"), S("codes2_turned"), S("codes2_evacuated")
                py = [st.enter_context(nc.psum_tensor(f"py{i}{tag}", [P, D], F32)) for i in range(2)]
                KD = (2 + 7) * G if two else 2 * G

                with nc.Block() as block:
                    @block.sync
                    def _(sp):
                        row = lambda a: a.rearrange("(a n) -> a n", a=1)
                        sp.dma_start(bias[:, :], row(t["L2_ffn_b2" if two else "L0_ffn_bias"]).to_broadcast([P, D])).then_inc(s_b, 16)
                        if two:
                            sp.dma_start(b1[:, :], row(t["L2_ffn_b1"]).to_broadcast([P, F])).then_inc(s_b, 16)
                            weights3(sp)
                        else:
                            sp.dma_start(wsc[:, 0:1], row(t["L0_ffn_weight_scale"]).to_broadcast([P, 1])).then_inc(s_b, 16)

                    @block.gpsimd
                    def _(pool):
                        root_pool(pool, s_mo, s_rs)
                        pool.wait_ge(s_n, B)
                        pool.wait_ge(s_b, 33)
                        pool.tensor_tensor(x[:, :, :], x[:, :, :], gbias[:, :].unsqueeze(1).to_broadcast([P, B, D]), ALU.add).then_inc(s_x2, 1)

                    @block.vector
                    def _(v):
                        v.wait_ge(s_b, 32)
                        nc.vector.tensor_scalar(gbias[:, :], bias[:, :], gcol, None, ALU.mult).then_inc(s_b, 1)
                        wlast = wscale[:, 1:2] if two else wsc[:, 0:1]
                        nc.vector.tensor_scalar(wsc[:, 1:2], wlast, gcol, 1.0 / 127.0, ALU.mult, ALU.mult).then_inc(s_step, 1)
                        moments_vector(v, s_st, s_mo, s_step, 1)
                        v.wait_ge(s_rs, 1)
                        with v.Fori(0, NG) as g:
                            for a in range(G):
                                b = g * G + a
                                nc.vector.tensor_scalar(xnv[:, ds(b, 1), :].rearrange("p a c -> p (a c)"), x[:, ds(b, 1), :].rearrange("p a c -> p (a c)"),
                                                        mean[:, ds(b, 1)], rstd[:, ds(b, 1)], ALU.subtract, ALU.mult).then_inc(s_n, 1)
                            v.wait_ge(s_n, g * G + G)
                            nc.vector.tensor_reduce(am[:, ds(g * G, G)], xnv[:, ds(g * G, G), :], AX.X, ALU.max, apply_absolute_value=True).then_inc(s_am, 1)
                        v.wait_ge(s_am, NG)
                        nc.vector.tensor_scalar(am1[:, :], am[:, :], 1e-5, None, ALU.max).then_inc(s_am, 1)
                        v.wait_ge(s_am, NG + 1)
                        nc.vector.reciprocal(upr[:, :], am1[:, :]).then_inc(s_am, 1)
                        if two:
                            nc.vector.tensor_scalar(down[:, :], am1[:, :], wscale[:, 0:1], 1.0 / 127.0, ALU.mult, ALU.mult).then_inc(s_am, 1)
                        else:
                            nc.vector.tensor_scalar(down[:, :], am1[:, :], wsc[:, 1:2], None, ALU.mult).then_inc(s_am, 1)
                        v.wait_ge(s_am, NG + 2)
                        nc.vector.tensor_scalar(up[:, :], upr[:, :], 127.0, None, ALU.mult).then_inc(s_am, 1)
                        v.wait_ge(s_am, NG + 4)

                        if two:
                            v.sem_inc(s_h, 1)
                        with v.Fori(0, NG) as g:
                            done = [0]

                            def step(ins):
                                ins.then_inc(s_d, 1)
                                done[0] += 1
                                v.wait_ge(s_d, g * KD + done[0])

                            def codes(dst, src, scratch, scale, s_ready):
                                step(nc.vector.tensor_scalar(scratch, src, scale, ROUND, ALU.mult, ALU.add))
                                step(nc.vector.tensor_scalar(scratch, scratch, ROUND, -128.0, ALU.subtract, ALU.max))
                                nc.vector.tensor_scalar(dst, scratch, 127.0, None, ALU.min).then_inc(s_ready, 1)

                            for n in range(G + NY - 1):
                                if n < G:
                                    b = g * G + n
                                    v.wait_ge(s_t, b + 1)
                                    codes(q[:, n % 2, :], xnv[:, ds(b, 1), :].rearrange("p a c -> p (a c)"), tmp[:, n % 2, :], up[:, ds(b, 1)], s_q)
                                if two and 2 <= n <= G + 1:
                                    a = n - 2
                                    b = g * G + a
                                    v.wait_ge(s_gl, b + 1)
                                    sc = am2[:, a % 2, :]
                                    hh = h[:, a % 2, :]
                                    step(nc.vector.tensor_reduce(sc[:, 0:1], hh, AX.X, ALU.max, apply_absolute_value=True))
                                    step(nc.vector.tensor_scalar(sc[:, 1:2], sc[:, 0:1], 1e-5, None, ALU.max))
                                    step(nc.vector.reciprocal(sc[:, 2:3], sc[:, 1:2]))
                                    step(nc.vector.tensor_scalar(sc[:, 3:4], sc[:, 2:3], 127.0, None, ALU.mult))
                                    step(nc.vector.tensor_scalar(sc[:, 4:5], sc[:, 1:2], wsc[:, 1:2], None, ALU.mult))
                                    v.wait_ge(s_t2, b + 1)
                                    codes(q2[:, a % 2, :], hh, tmp2[:, :], sc[:, 3:4], s_q2)
                                    v.wait_ge(s_q2, b + 1)
                                if two and 1 <= n <= G:
                                    a = n - 1
                                    b = g * G + a
                                    v.wait_ge(s_m1, b + 3)
                                    for half in range(2):
                                        c = slice(half * 512, half * 512 + 512)
                                        nc.vector.scalar_tensor_tensor(out=h[:, a % 2, c], in0=ph[half][:, :], scalar=down[:, ds(b, 1)], in1=b1[:, c],
                                                                       op0=ALU.mult, op1=ALU.add).then_inc(s_h, 1)
                                if NY - 1 <= n:
                                    a = n - NY + 1
                                    b = g * G + a
                                    v.wait_ge(s_m, b + 3)
                                    if a == 0:
                                        v.wait_ge(s_x2, 1)
                                    xb = x[:, ds(b, 1), :].rearrange("p a c -> p (a c)")
                                    nc.vector.scalar_tensor_tensor(out=xb, in0=py[a % 2][:, :], scalar=am2[:, a % 2, 4:5] if two else down[:, ds(b, 1)], in1=xb,
                                                                   op0=ALU.mult, op1=ALU.add).then_inc(s_y, 1)
                            assert done[0] == KD

                    @block.tensor
                    def _(pe):
                        pe.sem_inc(s_t, 2)
                        pe.sem_inc(s_m, 2)
                        if two:
                            pe.sem_inc(s_t2, 2)
                            pe.sem_inc(s_m1, 2)
                        with pe.Fori(0, NG) as g:
                            for n in range(G + NY - 1):
                                if 1 <= n <= G:
                                    a = n - 1
                                    b = g * G + a
                                    pe.wait_ge(s_e, b + 3)
                                    if two:
                                        pe.wait_ge(s_h, 2 * b + 1)
                                        for half in range(2):
                                            for k in range(DK):
                                                m = pe.matmul(ph[half][:, :], qT[:, a % 2, k, :], W1[:, k, half * 512:half * 512 + 512], start=(k == 0), stop=(k == DK - 1))
                                        m.then_inc(s_m1, 1)
                                    else:
                                        pe.wait_ge(s_y, b + 1)
                                        for k in range(DK):
                                            m = pe.matmul(py[a % 2][:, :], qT[:, a % 2, k, :], W1[:, k, :], start=(k == 0), stop=(k == DK - 1))
                                        m.then_inc(s_m, 1)
                                if n < G:
                                    b = g * G + n
                                    pe.wait_ge(s_q, b + 1)
                                    pe.wait_ge(s_e, b + 1)
                                    for k in range(DK):
                                        m = pe.transpose(pt[n % 2][:, k * P:(k + 1) * P], q[:, n % 2, k * P:(k + 1) * P], identb[:, :])
                                    m.then_inc(s_t, 1)
                                if two and 2 <= n <= G + 1:
                                    a = n - 2
                                    b = g * G + a
                                    pe.wait_ge(s_q2, b + 1)
                                    pe.wait_ge(s_e2, b + 1)
                                    for c in range(FC):
                                        m = pe.transpose(pt2[:, c * P:(c + 1) * P], q2[:, a % 2, c * P:(c + 1) * P], identb[:, :])
                                    m.then_inc(s_t2, 1)
                                if two and 3 <= n:
                                    a = n - 3
                                    b = g * G + a
                                    pe.wait_ge(s_e2, b + 2)
                                    pe.wait_ge(s_y, b + 1)
                                    for c in range(FC):
                                        m = pe.matmul(py[a % 2][:, :], q2T[:, a % 2, c, :], tern2[:, c, :], start=(c == 0), stop=(c == FC - 1))
                                    m.then_inc(s_m, 1)

                    @block.scalar
                    def _(act):
                        act.sem_inc(s_e, 2)
                        act.sem_inc(s_y, 2)
                        if two:
                            act.sem_inc(s_e2, 1)
                        with act.Fori(0, NG) as g:
                            for n in range(G + 2):
                                if n < G:
                                    b = g * G + n
                                    act.wait_ge(s_t, b + 3)
                                    act.wait_ge(s_m1 if two else s_m, b + 1)
                                    act.activation(qT[:, n % 2, :, :], pt[n % 2][:, 0:D].rearrange("p (k n) -> p k n", n=P), ACT.Copy).then_inc(s_e, 1)
                                if two and 1 <= n <= G:
                                    a = n - 1
                                    b = g * G + a
                                    act.wait_ge(s_h, 2 * b + 3)
                                    act.activation(h[:, a % 2, :], h[:, a % 2, :], ACT.Gelu).then_inc(s_gl, 1)
                                if two and 2 <= n:
                                    a = n - 2
                                    b = g * G + a
                                    act.wait_ge(s_t2, b + 3)
                                    act.wait_ge(s_m, b + 1)
                                    act.activation(q2T[:, a % 2, :, :], pt2[:, :].rearrange("p (k n) -> p k n", n=P), ACT.Copy).then_inc(s_e2, 1)

        def experts(layer, tag):
            top = 2 if layer == 3 else 1
            SLOTS = top * B + E - 1
            pre = "L%d_ffn_" % layer
            gcol = gate[:, 4 + layer:5 + layer]
            rows_in = nc.dram_tensor("rows_in" + tag, ((SLOTS + 1) * P, D), F32, kind="Internal").ap()
            rows_out = nc.dram_tensor("rows_out" + tag, (SLOTS * P, D), F32, kind="Internal").ap()
            whole = ExitStack()
            with whole:
                S = lambda n: sem(n + tag, whole)
                xtok = sb("xtok" + tag, [P, B, D], F32, whole)
                pos = sb("pos" + tag, [P, top, B], mybir.dt.uint32, whole)
                coef = sb("coef" + tag, [P, top, B], F32, whole)
                first = sb("first" + tag, [P, 16], I32, whole)
                s_zero, s_w = S("rows_zeroed"), [S("weights_even_loaded"), S("weights_odd_loaded")]
                w1 = sb("w1" + tag, [P, 2, DK, F], F32, whole)
                w3 = sb("w3" + tag, [P, 2, DK, F], F32, whole) if layer == 3 else None
                w2 = sb("w2" + tag, [P, 2, FC, D], F32, whole)
                w1d = t[pre + "w1"].rearrange("e (k p) n -> e p k n", p=P)
                w2d = t[pre + "w2"].rearrange("e (c p) n -> e p c n", p=P)
                w3d = t[pre + "w3"].rearrange("e (k p) n -> e p k n", p=P) if layer == 3 else None
                NW = 3 if layer == 3 else 2

                def load_weights(eng, e, j):
                    def of(d):
                        return d[ds(e, 1)].rearrange("a p k n -> (a p) k n")
                    eng.dma_start(w1[:, j, :, :], of(w1d)).then_inc(s_w[j], 16)
                    eng.dma_start(w2[:, j, :, :], of(w2d)).then_inc(s_w[j], 16)
                    if layer == 3:
                        eng.dma_start(w3[:, j, :, :], of(w3d)).then_inc(s_w[j], 16)

                st = ExitStack()
                with st:
                    zero = sb("zero" + tag, [P, D], F32, st)
                    s_zt = sem("zero_ready" + tag, st)
                    with nc.Block() as block:
                        norm_transposed(block, st, tag, xtok)

                        @block.gpsimd
                        def _(pool):
                            pool.memset(zero[:, :], 0.0).then_inc(s_zt, 1)

                        @block.sync
                        def _(sp):
                            load_weights(sp, 0, 0)
                            sp.wait_ge(s_zt, 1)
                            sp.dma_start(rows_in.rearrange("(n p) d -> p n d", p=P), zero[:, :].unsqueeze(1).to_broadcast([P, SLOTS + 1, D])).then_inc(s_zero, 16)
                            sp.dma_start(rows_out.rearrange("(n p) d -> p n d", p=P), zero[:, :].unsqueeze(1).to_broadcast([P, SLOTS, D])).then_inc(s_zero, 16)
                            sp.wait_ge(s_zero, 32)

                st = ExitStack()
                with st:
                    R = lambda n: sem(n + tag, st)
                    T = lambda n, shape, dt=F32: sb(n + tag, shape, dt, st)
                    gw = T("gw", [P, DK, E])
                    lgT = T("lgT", [E, B * P])
                    lg = T("lg", [P, B, E])
                    pr = T("pr", [P, B, E])
                    prs = T("prs", [P, top, B, E])
                    oh = T("oh", [P, top, B, E])
                    eq = T("eq", [P, B, E])
                    tok = T("tok", [P, 8, B])
                    pref = T("pref", [P, E])
                    low = T("low", [P, P])
                    chosen = T("chosen", [P, B, E])
                    cnt = T("cnt", [P, E, B])
                    run = T("run", [P, E, B])
                    full = T("full", [P, B, E])
                    ends = T("ends", [P, E + 1])
                    slot = T("slot", [P, 6, E])
                    firstf = T("firstf", [P, 16])
                    pos_f = T("pos_f", [P, top, B])
                    pl = [st.enter_context(nc.psum_tensor(f"pl{i}{tag}", [P, 512], F32)) for i in range(4)]
                    s_gw, s_c, s_l, s_le, s_lt, s_d, s_mx, s_ex, s_oh, s_rk, s_pos, s_sc = (
                        R(n) for n in ("gate_weights_loaded", "constants_ready", "logits_turned_ready", "logits_evacuated", "logits_ready",
                                       "dve_step", "max_subtracted", "exp_done", "choices_ready", "ranks_ready", "rows_known", "tokens_scattered"))
                    if layer == 1:
                        wred = T("wred", [P, DK, 16])
                        wredT = T("wredT", [16, DK, P])
                        wg = T("wg", [E, 16])
                        wgn = T("wgn", [E, 16])
                        wgs = T("wgs", [E, 8])
                        sq = T("sq", [E, 16])
                        wgT = T("wgT", [16, E])
                        s_g1, s_g2, s_g3 = R("gate_parts_turned"), R("gate_parts_ready"), R("norm_root")

                    with nc.Block() as block:
                        @block.sync
                        def _(sp):
                            if layer == 1:
                                sp.dma_start(wred[:, :, :], t[pre + "w_red"].rearrange("(k p) n -> p k n", p=P)).then_inc(s_gw, 16)
                                sp.dma_start(wg[:, :], t[pre + "wg"]).then_inc(s_gw, 16)
                            else:
                                sp.dma_start(gw[:, :, :], t[pre + "gate_w"].rearrange("(k p) n -> p k n", p=P)).then_inc(s_gw, 16)

                        @block.gpsimd
                        def _(pool):
                            pool.iota(pref[:, :], pattern=[[-1, E]], base=E, channel_multiplier=0, allow_small_or_imprecise_dtypes=True).then_inc(s_c, 1)
                            pool.affine_select(out=low[:, :], in_=ones[:, 0:P], compare_op=ALU.is_gt, fill=0.0, base=0,
                                               pattern=[[1, P]], channel_multiplier=-1).then_inc(s_c, 1)
                            pool.memset(ends[:, :], 0.0).then_inc(s_c, 1)
                            pool.memset(firstf[:, :], 0.0).then_inc(s_c, 1)
                            if layer == 1:
                                pool.wait_ge(s_g3, 1)
                                pool.tensor_tensor(wgs[:, 1:2], wgs[:, 0:1], wgs[:, 7:8], ALU.pow).then_inc(s_g3, 1)
                            pool.wait_ge(s_pos, 1)
                            for c in range(top):
                                for b in range(B):
                                    pool.indirect_dma_start(rows_in, bass.IndirectOffsetOnAxis(ap=pos[:, c, b:b + 1], axis=0),
                                                            xtok[:, b, :], None).then_inc(s_sc, 16)
                            pool.wait_ge(s_sc, 16 * top * B)

                        @block.tensor
                        def _(pe):
                            pe.wait_ge(s_c, 4)
                            if layer == 1:
                                pe.wait_ge(s_gw, 32)
                                for k in range(DK):
                                    pe.transpose(pl[0][0:16, k * P:(k + 1) * P], wred[:, k, :], ident[:, :])
                                pe.wait_ge(s_g3, 3)
                                pe.transpose(pl[1][0:16, 0:E], wgn[:, :], ident[0:E, 0:E]).then_inc(s_g1, 1)
                                pe.wait_ge(s_g2, 2)
                                for k in range(DK):
                                    m = pe.matmul(pl[2 + k][:, 0:E], wredT[:, k, :], wgT[:, :], start=True, stop=True)
                                m.then_inc(s_g1, 1)
                                pe.wait_ge(s_g2, 4)
                            else:
                                pe.wait_ge(s_gw, 16)
                            for g in range(NG):
                                if g >= 2:
                                    pe.wait_ge(s_le, g - 1)
                                for k in range(DK):
                                    m = pe.matmul(pl[g % 2][0:E, :], gw[:, k, :], xnT[:, k, g * GT:(g + 1) * GT], start=(k == 0), stop=(k == DK - 1))
                                m.then_inc(s_l, 1)
                            pe.wait_ge(s_le, NG)
                            for b in range(B):
                                m = pe.transpose(pl[2][:, b * E:(b + 1) * E], lgT[:, b * P:(b + 1) * P], ident[0:E, 0:E])
                            m.then_inc(s_lt, 1)
                            pe.wait_ge(s_oh, 1)
                            ch = chosen[:, :, :].rearrange("p b e -> p (b e)")
                            pe.matmul(pl[0][:, 0:P], low[:, :], ch, start=True, stop=True)
                            pe.matmul(pl[1][:, 0:P], ones[:, 0:P], ch, start=True, stop=True).then_inc(s_rk, 1)

                        @block.scalar
                        def _(act):
                            act.wait_ge(s_mx, 1)
                            act.activation(pr[:, :, :], lg[:, :, :], ACT.Exp).then_inc(s_ex, 1)

                        @block.vector
                        def _(v):
                            n = [0]

                            def step(ins):
                                ins.then_inc(s_d, 1)
                                n[0] += 1
                                v.wait_ge(s_d, n[0])

                            V = nc.vector
                            v.wait_ge(s_c, 4)
                            if layer == 1:
                                v.wait_ge(s_gw, 32)
                                step(V.tensor_tensor(sq[:, :], wg[:, :], wg[:, :], ALU.mult))
                                step(V.memset(wgs[:, 7:8], 0.5))
                                V.tensor_reduce(wgs[:, 0:1], sq[:, :], AX.X, ALU.add).then_inc(s_g3, 1)
                                v.wait_ge(s_g3, 2)
                                step(V.tensor_scalar(wgs[:, 2:3], wgs[:, 1:2], 1e-4, None, ALU.max))
                                step(V.reciprocal(wgs[:, 3:4], wgs[:, 2:3]))
                                V.tensor_scalar(wgn[:, :], wg[:, :], wgs[:, 3:4], None, ALU.mult).then_inc(s_g3, 1)
                                v.wait_ge(s_g1, 1)
                                V.tensor_copy(wredT[:, :, :], pl[0][0:16, 0:D].rearrange("p (k n) -> p k n", n=P)).then_inc(s_g2, 1)
                                V.tensor_copy(wgT[:, :], pl[1][0:16, 0:E]).then_inc(s_g2, 1)
                                v.wait_ge(s_g1, 2)
                                for k in range(DK):
                                    V.tensor_copy(gw[:, k, :], pl[2 + k][:, 0:E]).then_inc(s_g2, 1)
                            for g in range(NG):
                                v.wait_ge(s_l, g + 1)
                                V.tensor_copy(lgT[:, g * GT:(g + 1) * GT], pl[g % 2][0:E, :]).then_inc(s_le, 1)
                            v.wait_ge(s_lt, 1)

                            def per_token(ap):
                                return ap.unsqueeze(2).to_broadcast([P, B, E])

                            pl3 = pl[2][:, 0:B * E].rearrange("p (b e) -> p b e", e=E)
                            step(V.tensor_reduce(tok[:, 0, :], pl3, AX.X, ALU.max))
                            V.tensor_tensor(lg[:, :, :], pl3, per_token(tok[:, 0, :]), ALU.subtract).then_inc(s_mx, 1)
                            v.wait_ge(s_ex, 1)
                            step(V.tensor_reduce(tok[:, 1, :], pr[:, :, :], AX.X, ALU.add))
                            step(V.reciprocal(tok[:, 2, :], tok[:, 1, :]))
                            step(V.tensor_tensor(prs[:, 0, :, :], pr[:, :, :], per_token(tok[:, 2, :]), ALU.mult))
                            prefb = pref[:, :].unsqueeze(1).to_broadcast([P, B, E])
                            for c in range(top):
                                best, code = tok[:, 3 + c, :], tok[:, 5 + c, :]
                                if c:
                                    step(V.scalar_tensor_tensor(out=prs[:, 1, :, :], in0=oh[:, 0, :, :], scalar=-4.0, in1=prs[:, 0, :, :], op0=ALU.mult, op1=ALU.add))
                                step(V.tensor_reduce(best, prs[:, c, :, :], AX.X, ALU.max))
                                step(V.tensor_tensor(eq[:, :, :], prs[:, c, :, :], per_token(best), ALU.is_equal))
                                step(V.tensor_tensor(eq[:, :, :], eq[:, :, :], prefb, ALU.mult))
                                step(V.tensor_reduce(code, eq[:, :, :], AX.X, ALU.max))
                                step(V.tensor_tensor(oh[:, c, :, :], eq[:, :, :], per_token(code), ALU.is_equal))
                            if top == 2:
                                V.tensor_tensor(chosen[:, :, :], oh[:, 0, :, :], oh[:, 1, :, :], ALU.add).then_inc(s_oh, 1)
                                step(V.tensor_tensor(tok[:, 7, :], tok[:, 3, :], tok[:, 4, :], ALU.add))
                                step(V.reciprocal(tok[:, 0, :], tok[:, 7, :]))
                                for c in range(top):
                                    step(V.scalar_tensor_tensor(out=coef[:, c, :], in0=tok[:, 3 + c, :], scalar=gcol, in1=tok[:, 0, :], op0=ALU.mult, op1=ALU.mult))
                            else:
                                V.tensor_copy(chosen[:, :, :], oh[:, 0, :, :]).then_inc(s_oh, 1)
                                step(V.tensor_scalar(coef[:, 0, :], tok[:, 3, :], gcol, None, ALU.mult))
                            v.wait_ge(s_rk, 1)
                            counts = pl[1][:, 0:P].rearrange("p (b e) -> p e b", e=E)
                            step(V.tensor_copy(cnt[:, :, :], counts))
                            step(V.tensor_tensor_scan(run[:, :, :].rearrange("p e b -> p (e b)"), ones[:, 0:P], cnt[:, :, :].rearrange("p e b -> p (e b)"), 0.0, ALU.mult, ALU.add))
                            step(V.tensor_copy(ends[:, 1:E + 1], run[:, :, B - 1]))
                            step(V.tensor_tensor(slot[:, 0, :], ends[:, 1:E + 1], ends[:, 0:E], ALU.subtract))
                            step(V.tensor_scalar(slot[:, 1, :], slot[:, 0, :], 1.0 / P, 0.5 - 0.5 / P, ALU.mult, ALU.add))
                            step(V.tensor_scalar(slot[:, 2, :], slot[:, 1, :], ROUND, ROUND, ALU.add, ALU.subtract))
                            step(V.tensor_scalar(slot[:, 3, :], slot[:, 2, :], 1.0, None, ALU.max))
                            step(V.tensor_tensor_scan(firstf[:, 2:E + 2], ones[:, 0:E], slot[:, 3, :], 0.0, ALU.mult, ALU.add))
                            step(V.tensor_copy(first[:, :], firstf[:, :]))
                            step(V.scalar_tensor_tensor(out=slot[:, 4, :], in0=firstf[:, 1:E + 1], scalar=float(P), in1=ends[:, 0:E], op0=ALU.mult, op1=ALU.subtract))
                            step(V.tensor_tensor(run[:, :, :], run[:, :, :], cnt[:, :, :], ALU.subtract))
                            step(V.tensor_tensor(full[:, :, :], pl[0][:, 0:P].rearrange("p (b e) -> p b e", e=E), run[:, :, :].rearrange("p e b -> p b e"), ALU.add))
                            step(V.tensor_tensor(full[:, :, :], full[:, :, :], slot[:, 4, :].unsqueeze(1).to_broadcast([P, B, E]), ALU.add))
                            for c in range(top):
                                step(V.tensor_tensor(oh[:, c, :, :], oh[:, c, :, :], full[:, :, :], ALU.mult))
                                step(V.tensor_reduce(pos_f[:, c, :], oh[:, c, :, :], AX.X, ALU.add))
                            V.tensor_copy(pos[:, :, :], pos_f[:, :, :]).then_inc(s_pos, 1)

                st = ExitStack()
                with st:
                    R = lambda n: sem(n + tag, st)
                    T = lambda n, shape, dt=F32: sb(n + tag, shape, dt, st)
                    xg = T("xg", [P, D])
                    xgT = T("xgT", [P, DK, P])
                    hT = T("hT", [P, FC, P])
                    y = T("y", [P, D])
                    b1e = T("b1e", [P, 2, FC]) if layer == 1 else None
                    b2 = T("b2", [1, E, D]) if layer == 1 else None
                    b2e = T("b2e", [1, 2, D]) if layer == 1 else None
                    sg = T("sg", [P, 2, 512]) if layer == 3 else None
                    yg = T("yg", [P, 4, D])
                    pb = lambda n, w: st.enter_context(nc.psum_tensor(n + tag, [P, w], F32))
                    ph = [pb(f"ph{i}", 512) for i in range(2)]
                    ph3 = [pb(f"ph3{i}", 512) for i in range(2)] if layer == 3 else None
                    px, py = pb("px", D), pb("py", D)
                    s_xg, s_tn, s_xT = R("tokens_loaded"), R("tokens_turned"), R("turned_evacuated")
                    s_h, s_act, s_hT = R("hidden_sums"), R("activated"), R("hidden_ready")
                    s_y, s_ye, s_st, s_yf = R("slot_done"), R("y_evacuated"), R("y_stored"), R("y_free")
                    s_b, s_be = R("bias2_loaded"), R("bias_ready")
                    s_yg = [R(f"gathered{i}") for i in range(4)]
                    s_up = R("tokens_updated")

                    def slot_range(eng, e):
                        a = eng.value_load(first[0:1, ds(e + 1, 1)], min_val=0, max_val=SLOTS - 1)
                        b = eng.value_load(first[0:1, ds(e + 2, 1)], min_val=1, max_val=SLOTS)
                        return a, b

                    def total(eng):
                        return eng.value_load(first[0:1, E + 1:E + 2], min_val=E, max_val=SLOTS)

                    with nc.Block() as block:
                        @block.sync
                        def _(sp):
                            if layer == 1:
                                sp.dma_start(b2[:, :, :], t[pre + "b2"].rearrange("(a e) n -> a e n", a=1)).then_inc(s_b, 16)

                        @block.gpsimd
                        def _(pool):
                            pool.sem_inc(s_yf, 1)
                            pool.dma_start(xg[:, :], rows_in[0:P, :]).then_inc(s_xg, 16)
                            pool.wait_ge(s_tn, 1)
                            pool.dma_start(xg[:, :], rows_in[P:2 * P, :]).then_inc(s_xg, 16)
                            slots = total(pool)
                            with pool.Fori(1, slots) as s:
                                pool.wait_ge(s_tn, s + 1)
                                pool.dma_start(xg[:, :], rows_in[ds((s + 1) * P, P), :]).then_inc(s_xg, 16)
                                pool.wait_ge(s_ye, s + 1)
                                pool.dma_start(rows_out[ds((s - 1) * P, P), :], y[:, :]).then_inc(s_st, 16)
                                pool.wait_ge(s_st, s * 16)
                                pool.sem_inc(s_yf, 1)
                            pool.wait_ge(s_ye, slots + 1)
                            pool.dma_start(rows_out[ds((slots - 1) * P, P), :], y[:, :]).then_inc(s_st, 16)
                            pool.wait_ge(s_st, slots * 16)

                        @block.tensor
                        def _(pe):
                            def turn():
                                for k in range(DK):
                                    m = pe.transpose(px[:, k * P:(k + 1) * P], xg[:, k * P:(k + 1) * P], ident[:, :])
                                m.then_inc(s_tn, 1)

                            pe.sem_inc(s_y, 1)
                            pe.wait_ge(s_xg, 16)
                            turn()

                            def expert(r, j):
                                a, b = slot_range(pe, r * 2 + j)
                                with pe.Fori(a, b) as s:
                                    pe.wait_ge(s_w[j], (r + 1) * (16 * NW))
                                    if layer == 1:
                                        pe.wait_ge(s_be, r * 2 + j + 1)
                                    pe.wait_ge(s_xT, s + 1)
                                    for half in range(2):
                                        for w, bank in ((w1, ph), (w3, ph3))[:layer // 2 + 1]:
                                            for c in range(4):
                                                f = (4 * half + c) * P
                                                for k in range(DK):
                                                    m = pe.matmul(bank[half][:, c * P:(c + 1) * P], w[:, j, k, f:f + P], xgT[:, k, :], start=(k == 0), stop=(k == DK - 1))
                                            m.then_inc(s_h, 1)
                                    pe.wait_ge(s_xg, s * 16 + 32)
                                    turn()
                                    pe.wait_ge(s_ye, s + 1)
                                    for c in range(FC):
                                        if c % 4 == 0:
                                            pe.wait_ge(s_hT, s * 2 + c // 4 + 1)
                                        m = pe.matmul(py[:, :], hT[:, c, :], w2[:, j, c, :], start=(c == 0), stop=(c == FC - 1 and layer == 3))
                                    if layer == 1:
                                        m = pe.matmul(py[:, :], ones[0:1, 0:P], b2e[0:1, j, :], start=False, stop=True)
                                    m.then_inc(s_y, 1)

                            with pe.Fori(0, E // 2) as r:
                                for j in range(2):
                                    expert(r, j)

                        @block.scalar
                        def _(act):
                            if layer == 1:
                                act.wait_ge(s_b, 16)

                            def expert(r, j, load):
                                a, b = slot_range(act, r * 2 + j)
                                act.wait_ge(s_y, a + 1)
                                if load:
                                    load_weights(act, r * 2 + j + 1, 1 - j)
                                if layer == 1:
                                    act.activation(b1e[:, j, :], cols[:, ds(r * 16 + (32 + FC * j), FC)], ACT.Copy).then_inc(s_b, 1)
                                    act.activation(b2e[:, j, :], b2[0:1, ds(r * 2 + j, 1), :].rearrange("a e n -> a (e n)"), ACT.Copy).then_inc(s_be, 1)
                                    act.wait_ge(s_b, r * 2 + (j + 17))
                                with act.Fori(a, b) as s:
                                    for half in range(2):
                                        if layer == 1:
                                            act.wait_ge(s_h, s * 2 + half + 1)
                                            for c in range(4):
                                                m = act.activation(hT[:, 4 * half + c, :], ph[half][:, c * P:(c + 1) * P], ACT.Gelu, bias=b1e[:, j, 4 * half + c:4 * half + c + 1])
                                            m.then_inc(s_hT, 1)
                                        else:
                                            act.wait_ge(s_h, s * 4 + 2 * half + 1)
                                            act.activation(sg[:, half, :], ph[half][:, :], ACT.Silu).then_inc(s_act, 1)

                            with act.Fori(0, E // 2 - 1) as r:
                                for j in range(2):
                                    expert(r, j, True)
                            for j in range(2):
                                expert(E // 2 - 1, j, j == 0)

                        @block.vector
                        def _(v):
                            def take_tokens(n):
                                v.wait_ge(s_tn, n)
                                nc.vector.tensor_copy(xgT[:, :, :], px[:, :].rearrange("p (k n) -> p k n", n=P)).then_inc(s_xT, 1)

                            v.sem_inc(s_ye, 1)
                            take_tokens(1)
                            with v.Fori(0, total(v)) as s:
                                if layer == 3:
                                    for half in range(2):
                                        v.wait_ge(s_act, s * 2 + half + 1)
                                        v.wait_ge(s_h, s * 4 + 2 * half + 2)
                                        nc.vector.tensor_tensor(hT[:, 4 * half:4 * half + 4, :].rearrange("p c n -> p (c n)"), sg[:, half, :], ph3[half][:, :], ALU.mult).then_inc(s_hT, 1)
                                take_tokens(s + 2)
                                v.wait_ge(s_y, s + 2)
                                v.wait_ge(s_yf, s + 1)
                                nc.vector.tensor_copy(y[:, :], py[:, :]).then_inc(s_ye, 1)

                    with nc.Block() as block:
                        @block.gpsimd
                        def _(pool):
                            for n in range(top * B):
                                c, b = n % top, n // top
                                if n >= 4:
                                    pool.wait_ge(s_up, n - 3)
                                pool.indirect_dma_start(yg[:, n % 4, :], None, rows_out,
                                                        bass.IndirectOffsetOnAxis(ap=pos[:, c, b:b + 1], axis=0)).then_inc(s_yg[n % 4], 16)

                        @block.vector
                        def _(v):
                            for n in range(top * B):
                                c, b = n % top, n // top
                                v.wait_ge(s_yg[n % 4], 16 * (n // 4 + 1))
                                if c:
                                    v.wait_ge(s_up, n)
                                nc.vector.scalar_tensor_tensor(out=x[:, b, :], in0=yg[:, n % 4, :], scalar=coef[:, c, b:b + 1], in1=x[:, b, :],
                                                               op0=ALU.mult, op1=ALU.add).then_inc(s_up, 1)

        def additive(tag):
            FB = 16
            UB = P // FB * DK
            POOLS = (1,4,6,9,12,14)
            VECS = [i for i in range(UB) if i not in POOLS]
            RP, RV = 3, 5
            NEG = -1e30

            def place(i):
                return (1, POOLS.index(i)) if i in POOLS else (0, VECS.index(i))

            whole = ExitStack()
            with whole:
                S = lambda n: sem(n + tag, whole)
                T = lambda n, shape, dt=F32: sb(n + tag, shape, dt, whole)
                featT, txtT = T("featT", [P, DK, B * P]), T("txtT", [P, DK, B * P])
                Ws, W = T("Ws", [P, DK, D]), T("W", [P, DK, D])
                vrow = T("vrow", [4, P])
                vcol = T("vcol", [P, 4])
                wsel = T("wsel", [P, DK, UB // DK, 32])
                wcb = T("wcb", [P, 2, D])
                bc = T("bc", [P, 2])
                s_w, s_v, s_vt, s_vc = S("weights_loaded"), S("small_loaded"), S("small_turned"), S("small_ready")
                s_z = S("selector_zero")
                s_pj, s_pe = S("projected"), S("projection_evacuated")

                st = ExitStack()
                with st:
                    with nc.Block() as block:
                        norm_transposed(block, st, tag)

                        @block.sync
                        def _(sp):
                            row = lambda a: a.rearrange("(c p) a -> (a c) p", p=P)
                            sp.dma_start(W[:, :, :], t["L2_xattn_W"].rearrange("(k p) n -> p k n", p=P)).then_inc(s_w, 16)
                            sp.dma_start(Ws[:, :, :], t["L2_xattn_Ws"].rearrange("(k p) n -> p k n", p=P)).then_inc(s_w, 16)
                            sp.dma_start(vrow[0:2, :], row(t["L2_xattn_w"])).then_inc(s_v, 16)
                            sp.dma_start(vrow[2:4, :], t["L2_xattn_b"].rearrange("a (c p) -> (a c) p", p=P)).then_inc(s_v, 16)
                            sp.dma_start(wcb[:, 0, :], t["L2_xattn_Wcw"].to_broadcast([P, D])).then_inc(s_v, 16)
                            sp.dma_start(wcb[:, 1, :], t["L2_xattn_Wcb"].to_broadcast([P, D])).then_inc(s_v, 16)
                            one = lambda a: a.rearrange("(a n) -> a n", a=1).to_broadcast([P, 1])
                            sp.dma_start(bc[:, 0:1], one(t["L2_xattn_bcw"])).then_inc(s_v, 16)
                            sp.dma_start(bc[:, 1:2], one(t["L2_xattn_bcb"])).then_inc(s_v, 16)

                st = ExitStack()
                with st:
                    pv = st.enter_context(nc.psum_tensor("pv" + tag, [P, 512], F32))
                    pp = [st.enter_context(nc.psum_tensor(f"pp{i}{tag}", [P, 512], F32)) for i in range(4)]
                    with nc.Block() as block:
                        @block.tensor
                        def _(pe):
                            pe.wait_ge(s_v, 16 * 6)
                            pe.transpose(pv[:, 0:4], vrow[:, :], ident[0:4, 0:4]).then_inc(s_vt, 1)
                            pe.wait_ge(s_w, 32)
                            with pe.Fori(0, NG) as g:
                                for i, (w, src) in enumerate(((W, xnT), (Ws, ctxT))):
                                    for c in range(DK):
                                        pe.wait_ge(s_pe, g * 4 + (2 * i + c + 1))
                                        for k in range(DK):
                                            m = pe.matmul(pp[2 * i + c][:, :], w[:, k, c * P:(c + 1) * P], src[:, k, ds(g * GT, GT)], start=(k == 0), stop=(k == DK - 1))
                                        m.then_inc(s_pj, 1)

                        @block.vector
                        def _(v):
                            nc.vector.memset(wsel[:, :, :, :], 0.0).then_inc(s_z, 1)
                            v.wait_ge(s_vt, 1)
                            nc.vector.tensor_copy(vcol[:, :], pv[:, 0:4]).then_inc(s_vc, 1)
                            v.wait_ge(s_z, 1)
                            v.wait_ge(s_vc, 1)
                            for c in range(DK):
                                for u in range(UB // DK):
                                    m = nc.vector.tensor_copy(wsel[:, c, u, u:u + 1], vcol[:, c:c + 1])
                            m.then_inc(s_vc, 1)

                        @block.scalar
                        def _(act):
                            act.sem_inc(s_pe, 4)
                            act.wait_ge(s_vc, 2)
                            with act.Fori(0, NG) as g:
                                for i, dst in enumerate((featT, txtT)):
                                    for c in range(DK):
                                        act.wait_ge(s_pj, g * 4 + (2 * i + c + 1))
                                        d = dst[:, c, ds(g * GT, GT)]
                                        if i == 0:
                                            act.activation(d, pp[c][:, :], ACT.Identity, bias=vcol[:, 2 + c:3 + c]).then_inc(s_pe, 1)
                                        else:
                                            act.activation(d, pp[2 + c][:, :], ACT.Copy).then_inc(s_pe, 1)

                st = ExitStack()
                with st:
                    R = lambda n: sem(n + tag, st)
                    U = lambda n, shape, dt=F32: sb(n + tag, shape, dt, st)
                    flat = [w[:, :, :].rearrange("p k n -> p (k n)") for w in (wq, wk, wv, wo)] + [xnT[:, k, :] for k in range(DK)]
                    room = [f.rearrange("p (f k) -> p f k", k=P) for f in flat]
                    room += [U(f"th{i}", [P, FB, P])[:, :, :] for i in range(RV + RP - len(room))]
                    th = [room[:RV], room[RV:]]
                    ring = (RV, RP)

                    def buf(i):
                        who, n = place(i)
                        return th[who][n % ring[who]]

                    def split(ap):
                        return ap.rearrange("p (j i) k -> p j i k", i=4)

                    def feat(c, b, u):
                        f = featT[:, c, ds(b * P, P)].rearrange("p (j f) -> p j f", j=4)[:, :, 4 * u:4 * u + 4]
                        return f.unsqueeze(3).to_broadcast([P, 4, 4, P])

                    def spread(text):
                        return text.unsqueeze(1).unsqueeze(1).to_broadcast([P, 4, 4, P])

                    cx = U("cx", [P, D])
                    rv, rho = U("rv", [P, 512]), U("rho", [P, P])
                    qm = U("qm", [P, P], I32)
                    qn = U("qn", [P, P])
                    rs, pr, pT = U("rs", [P, P]), U("pr", [P, P]), U("pT", [P, P])
                    nmx, sm = U("nmx", [P, 1]), U("sm", [P, 1])
                    dot, rsm, pre, ws = U("dot", [P, 2]), U("rsm", [P, 1]), U("pre", [P, 2]), U("ws", [P, 2])
                    sc2 = U("sc2", [P, 2])
                    junk = U("junk", [P, 2, D])
                    upd = U("upd", [P, 2, D])
                    pbk = lambda n: st.enter_context(nc.psum_tensor(n + tag, [P, 512], F32))
                    prho, pt2, ptx = pbk("prho"), pbk("pt2"), pbk("ptx")
                    ptxt = st.enter_context(nc.psum_tensor("ptxt" + tag, [P, 1024], F32))
                    s_sum = [R("vector_sums_ready"), R("gpsimd_sums_ready")]
                    s_th = R("tanh_ready")
                    s_use = [R("vector_unit_used"), R("gpsimd_unit_used")]
                    s_txt = R("text_projected")
                    s_rv, s_rho, s_qm, s_qn, s_rs = R("rho_evacuated"), R("rho_sorted"), R("mask_loaded"), R("mask_read"), R("rho_masked")
                    s_nm, s_p, s_t2, s_pT = R("nmax_ready"), R("probs_ready"), R("probs_turned"), R("probsT_ready")
                    s_cx, s_tx, s_d, s_pre, s_ws, s_up = R("text_loaded"), R("text_mixed"), R("dot_step"), R("pre_ready"), R("ws_ready"), R("tile_step")

                    V_AT = {4: 0, 8: 1, 11: 2, 14: 3}
                    P_AT = {5: 0, 8: 1}
                    A_AT = {0: 0, 5: 1, 11: 2}

                    with nc.Block() as block:
                        @block.sync
                        def _(sp):
                            cd = t["ctx_1024"]
                            with sp.Fori(0, B) as b:
                                sp.wait_ge(s_qn, b + 1)
                                sp.dma_start(qm[:, :], t["mask_BxS2_ik0"][ds(b, 1), :].to_broadcast([P, P])).then_inc(s_qm, 16)
                                sp.wait_ge(s_tx, b + 1)
                                sp.dma_start(cx[:, :], cd[ds(b, 1)].rearrange("a s d -> (a s) d")).then_inc(s_cx, 16)
                                sp.wait_ge(s_rv, b + 1)
                                for j in range(4):
                                    sp.dma_start(rho[32 * j:32 * j + 32, :], rv[32 * j:32 * j + UB // DK, :].rearrange("u (i k) -> u i k", i=4)).then_inc(s_rho, 16)

                        @block.vector
                        def _(v):
                            V = nc.vector

                            def post(b, part):
                                if part == 0:
                                    v.wait_ge(s_qm, b * 16 + 16)
                                    V.tensor_scalar(qn[:, :], qm[:, :], -1.0, 1.0, ALU.mult, ALU.add).then_inc(s_qn, 1)
                                    v.wait_ge(s_qn, b + 2)
                                    v.wait_ge(s_rho, b * 64 + 64)
                                    V.scalar_tensor_tensor(out=rs[:, :], in0=qn[:, :], scalar=NEG, in1=rho[:, :], op0=ALU.mult, op1=ALU.add).then_inc(s_rs, 1)
                                    v.wait_ge(s_rs, b + 1)
                                    V.tensor_reduce(nmx[:, :], rs[:, :], AX.X, ALU.max, negate=True).then_inc(s_nm, 1)
                                elif part == 1:
                                    v.wait_ge(s_t2, b + 1)
                                    V.tensor_copy(pT[:, :], pt2[:, 0:P]).then_inc(s_pT, 1)
                                elif part == 2:
                                    v.wait_ge(s_tx, b + 2)
                                    for i in range(2):
                                        V.tensor_tensor_reduce(junk[:, i, :], ptx[:, 0:D], wcb[:, i, :], 1.0, 0.0, ALU.mult, ALU.add, dot[:, i:i + 1]).then_inc(s_d, 1)
                                    V.reciprocal(rsm[:, :], sm[:, :]).then_inc(s_d, 1)
                                    v.wait_ge(s_d, b * 4 + 3)
                                    V.tensor_scalar(sc2[:, :], dot[:, :], rsm[:, 0:1], None, ALU.mult).then_inc(s_d, 1)
                                    v.wait_ge(s_d, b * 4 + 4)
                                    V.tensor_tensor(pre[:, :], sc2[:, :], bc[:, :], ALU.add).then_inc(s_pre, 1)
                                else:
                                    v.wait_ge(s_ws, b + 1)
                                    xb = x[:, ds(b, 1), :].rearrange("p a c -> p (a c)")
                                    V.tensor_scalar(upd[:, 0, :], xb, mean[:, ds(b, 1)], rstd[:, ds(b, 1)], ALU.subtract, ALU.mult).then_inc(s_up, 1)
                                    v.wait_ge(s_up, b * 3 + 1)
                                    V.tensor_scalar(upd[:, 1, :], upd[:, 0, :], ws[:, 0:1], ws[:, 1:2], ALU.mult, ALU.add).then_inc(s_up, 1)
                                    v.wait_ge(s_up, b * 3 + 2)
                                    V.scalar_tensor_tensor(out=xb, in0=upd[:, 1, :], scalar=gate[:, 2:3], in1=xb, op0=ALU.mult, op1=ALU.add).then_inc(s_up, 1)

                            def batch(b, before):
                                v.wait_ge(s_txt, b + 1)
                                for i in range(UB):
                                    u, c = i // DK, i % DK
                                    who, n = place(i)
                                    if who == 0:
                                        v.wait_ge(s_use[0], b * len(VECS) + (n + 1))
                                        V.tensor_tensor(split(buf(i)), feat(c, b, u), spread(ptxt[:, ds(b % 2 * 512 + c * P, P)]), ALU.add).then_inc(s_sum[0], 1)
                                    if before is not None and i in V_AT:
                                        post(before, V_AT[i])

                            v.sem_inc(s_qn, 1)
                            batch(0, None)
                            with v.Fori(1, B) as b:
                                batch(b, b - 1)
                            for part in range(4):
                                post(B - 1, part)

                        @block.gpsimd
                        def _(pool):
                            with pool.Fori(0, B) as b:
                                for n, i in enumerate(POOLS):
                                    u, c = i // DK, i % DK
                                    pool.wait_ge(s_use[1], b * len(POOLS) + (n + 1))
                                    pool.tensor_tensor(split(buf(i)), feat(c, b, u), spread(txtT[:, c, ds(b * P, P)]), ALU.add).then_inc(s_sum[1], 1)

                        @block.scalar
                        def _(act):
                            def post(b, part):
                                if part == 0:
                                    who = place(UB - 1)[0]
                                    act.wait_ge(s_use[who], b * (len(POOLS) if who else len(VECS)) + (len(POOLS) + RP if who else len(VECS) + RV))
                                    act.activation(rv[:, :], prho[:, :], ACT.Copy).then_inc(s_rv, 1)
                                elif part == 1:
                                    act.wait_ge(s_nm, b + 1)
                                    act.activation(pr[:, :], rs[:, :], ACT.Exp, bias=nmx[:, 0:1], accum_out=sm[:, 0:1]).then_inc(s_p, 1)
                                else:
                                    act.wait_ge(s_pre, b + 1)
                                    act.activation(ws[:, :], pre[:, :], ACT.Tanh).then_inc(s_ws, 1)

                            def batch(b, before):
                                for i in range(UB):
                                    who, n = place(i)
                                    act.wait_ge(s_sum[who], b * (len(POOLS) if who else len(VECS)) + (n + 1))
                                    act.activation(buf(i), buf(i), ACT.Tanh).then_inc(s_th, 1)
                                    if before is not None and i in A_AT:
                                        post(before, A_AT[i])

                            batch(0, None)
                            with act.Fori(1, B) as b:
                                batch(b, b - 1)
                            for part in range(3):
                                post(B - 1, part)

                        @block.tensor
                        def _(pe):
                            pe.sem_inc(s_use[0], RV)
                            pe.sem_inc(s_use[1], RP)
                            pe.sem_inc(s_tx, 1)

                            def text(b):
                                for c in range(DK):
                                    for k in range(DK):
                                        m = pe.matmul(ptxt[:, ds(b % 2 * 512 + c * P, P)], Ws[:, k, c * P:(c + 1) * P], ctxT[:, k, ds(b * P, P)],
                                                      start=(k == 0), stop=(k == DK - 1))
                                m.then_inc(s_txt, 1)

                            def post(b, part):
                                if part == 0:
                                    pe.wait_ge(s_p, b + 1)
                                    pe.transpose(pt2[:, 0:P], pr[:, :], ident[:, :]).then_inc(s_t2, 1)
                                else:
                                    pe.wait_ge(s_pT, b + 1)
                                    pe.wait_ge(s_cx, b * 16 + 16)
                                    pe.matmul(ptx[:, 0:D], pT[:, :], cx[:, :], start=True, stop=True).then_inc(s_tx, 1)

                            def batch(b, before, last=False):
                                if before is not None:
                                    pe.wait_ge(s_rv, b)
                                for i in range(UB):
                                    u, c = i // DK, i % DK
                                    pe.wait_ge(s_th, b * UB + (i + 1))
                                    for j in range(4):
                                        m = pe.matmul(prho[32 * j:32 * j + 32, :], wsel[:, c, u, :], buf(i)[:, 4 * j:4 * j + 4, :],
                                                      start=(i == 0), stop=(i == UB - 1))
                                    m.then_inc(s_use[place(i)[0]], 1)
                                    if i == 2 and not last:
                                        text(b + 1)
                                    if before is not None and i in P_AT:
                                        post(before, P_AT[i])

                            text(0)
                            batch(0, None)
                            with pe.Fori(1, B - 1) as b:
                                batch(b, b - 1)
                            batch(B - 1, B - 2, last=True)
                            for part in range(2):
                                post(B - 1, part)

        def store():
            with nc.Block() as block:
                @block.sync
                def _(sp):
                    sp.dma_start(out.rearrange("b s d -> s b d"), x[:, :, :]).then_inc(s_out, 16)
                    sp.wait_ge(s_out, 16)

        setup()
        with nc.Block() as block:
            @block.vector
            def _(v):
                v.wait_ge(s_x, 16)

            @block.tensor
            def _(pe):
                pe.wait_ge(s_w0, 64)
        if 0 in layers:
            attention(0, "_a0")
            semaphores_cleared()
        if 1 in layers:
            bitlinear(0, "_f0")
            semaphores_cleared()
        if 2 in layers:
            attention(1, "_a1")
            semaphores_cleared()
        if 3 in layers:
            experts(1, "_f1")
            semaphores_cleared()
        if 4 in layers:
            additive("_a2")
            semaphores_cleared()
        if 5 in layers:
            bitlinear(2, "_f2")
            semaphores_cleared()
        if 6 in layers:
            if 5 not in layers:
                with nc.Block() as block:
                    @block.sync
                    def _(sp):
                        weights3(sp)
            attention(3, "_a3")
            semaphores_cleared()
        if 7 in layers:
            experts(3, "_f3")
        store()


_SKIP = ("mask_BxS_ff1",)


def kernel(**inputs):
    import numpy as _np
    import concourse.bacc as _bacc
    from concourse.bass_utils import run_bass_kernel_spmd as _run

    nc = _bacc.Bacc("TRN2", target_bir_lowering=False, num_devices=1)
    arrays, aps = {}, {}
    for name, value in inputs.items():
        if name in _SKIP:
            continue
        a = _np.ascontiguousarray(value)
        arrays[f"in_{name}"] = a
        aps[name] = nc.dram_tensor(f"in_{name}", a.shape, mybir.dt.from_np(a.dtype), kind="ExternalInput").ap()
    out = nc.dram_tensor("out", (B, P, D), F32, kind="ExternalOutput").ap()
    build(nc, aps, out)
    r = _run(nc, [arrays], core_ids=[0])
    return r.results[0]["out"]
```

```python
from contextlib import ExitStack

import concourse.bass as bass
from concourse import mybir

ALU = mybir.AluOpType
ACT = mybir.ActivationFunctionType
AX = mybir.AxisListType
F32 = mybir.dt.float32
BF16 = mybir.dt.bfloat16
I32 = mybir.dt.int32

P = 128
B = 16
D = 256
DK = D // P
G = 4
NG = B // G
GT = G * P
H = 16
E = 8
F = 1024
FC = F // P
LN_EPS = 1e-5
ROUND = 12582912.0
BIG = 1e9


def ds(i, n):
    return bass.ds(i, n)


def build(nc, t, out):
    outer = ExitStack()
    with outer:
        passing = []

        def sem(name, stack=outer):
            h = nc.alloc_semaphore(name=name)
            if stack is not outer:
                passing.append(h)
            return h

        def semaphores_cleared():
            nc.clear_and_free_semaphores(list(passing))
            passing.clear()
            nc.all_engine_barrier()

        def sb(name, shape, dt=F32, stack=outer):
            return stack.enter_context(nc.sbuf_tensor(name, shape, dt))

        def banks(stack, names):
            return {n: stack.enter_context(nc.psum_tensor(n, [P, 512], F32)) for n in names}

        x = sb("x", [P, B, D])
        xnT = sb("xnT", [P, DK, B * P])
        ctxT = sb("ctxT", [P, DK, B * P])
        ident = sb("ident", [P, P])
        identb = sb("identb", [P, P], BF16)
        ones = sb("ones", [P, 512])
        gate = sb("gate", [P, 8])
        nhalf = sb("nhalf", [P, B])
        stats = sb("stats", [P, B, 6])
        mom = sb("mom", [P, 5, B])
        mean = sb("mean", [P, B])
        veps = sb("veps", [P, B])
        rstd = sb("rstd", [P, B])
        cols = sb("cols", [P, 100])
        wq = sb("wq", [P, DK, 1024])
        wk = sb("wk", [P, DK, 1024])
        wv = sb("wv", [P, DK, 1024])
        wo = sb("wo", [P, 8, D])
        wq1 = sb("wq1", [P, DK, 512])
        wk1 = sb("wk1", [P, DK, 512])
        wv1 = sb("wv1", [P, DK, D])
        wo1 = sb("wo1", [P, 4, D])
        rows1 = sb("rows1", [2, 2, 512])
        mrow = sb("mrow", [2, B * P])
        tern0 = sb("tern0", [P, DK, D], BF16)
        tern1 = sb("tern1", [P, DK, F], BF16)
        tern2 = sb("tern2", [P, FC, D], BF16)
        wscale = sb("wscale", [P, 4])

        zero = sb("zero", [P, D])
        slots_of = {1: B + E - 1, 3: 2 * B + E - 1}
        rows_of = {l: (nc.dram_tensor(f"rows_in_f{l}", ((n + 1) * P, D), F32, kind="Internal").ap(),
                       nc.dram_tensor(f"rows_out_f{l}", (n * P, D), F32, kind="Internal").ap()) for l, n in slots_of.items()}
        s_zero = {l: sem(f"rows_zeroed_f{l}") for l in slots_of}

        def zero_rows(sp, layer):
            for rows, n in zip(rows_of[layer], (slots_of[layer] + 1, slots_of[layer])):
                sp.dma_start(rows.rearrange("(n p) d -> p n d", p=P), zero[:, :].unsqueeze(1).to_broadcast([P, n, D])).then_inc(s_zero[layer], 16)

        s_x = sem("x_loaded")
        s_w0 = sem("w0_loaded")
        s_w3 = sem("w3_loaded")
        s_out = sem("out_stored")

        def take_stats(b):
            nc.vector.bn_stats(stats[:, ds(b, 1), :].rearrange("p a c -> p (a c)"), x[:, ds(b, 1), :].rearrange("p a c -> p (a c)"))

        def setup():
            st = ExitStack()
            with st:
                S = lambda n: sem(n, st)
                ctx_in = sb("ctx_in", [P, 2, G, D], F32, st)
                brow = sb("brow", [96, P], F32, st)
                win = sb("win", [P, 4, DK, D], F32, st)
                wop = sb("wop", [P, DK, 512], F32, st)
                packed = sb("packed", [64, D], I32, st)
                code = sb("code", [64, 4, D], I32, st)
                ternp = sb("ternp", [64, 4, D], BF16, st)
                mint = sb("mint", [2, B * P], I32, st)
                g_in = sb("g_in", [P, 8], F32, st)
                ps = banks(st, [f"set{i}" for i in range(6)])
                pf = [ps[f"set{i}"] for i in range(6)]
                pb = [st.enter_context(nc.psum_tensor(f"setb{i}", [P, 1024], BF16)) for i in range(2)]
                s_ctx = [S("ctx_even_loaded"), S("ctx_odd_loaded")]
                s_ctxT, s_ctxE = S("ctx_turned"), S("ctx_evacuated")
                s_small, s_win, s_packed, s_pad = S("small_loaded"), S("w1x_loaded"), S("packed_loaded"), S("pads_zero")
                s_id, s_dve, s_turn, s_evac = S("ident_ready"), S("dve_step"), S("weight_turned"), S("weight_evacuated")
                s_rows, s_wop = S("rows_loaded"), S("wo1_padded")
                s_g = S("g_step")
                s_q = S("ternary_ready")

                with nc.Block() as block:
                    @block.sync
                    def _(sp):
                        cv = t["ctx_1024"].rearrange("(g a) s d -> g s a d", a=G)
                        sp.dma_start(ctx_in[:, 0, :, :], cv[0]).then_inc(s_ctx[0], 16)
                        sp.dma_start(ctx_in[:, 1, :, :], cv[1]).then_inc(s_ctx[1], 16)
                        sp.dma_start(x[:, :, :], t["x"].rearrange("b s d -> s b d")).then_inc(s_x, 16)
                        for n in range(2, NG):
                            sp.wait_ge(s_ctxT, 2 * (n - 2) + 2)
                            sp.dma_start(ctx_in[:, n % 2, :, :], cv[n]).then_inc(s_ctx[n % 2], 16)
                        sp.dma_start(wq[:, :, :], t["L0_xattn_Wq"].rearrange("(k p) n -> p k n", p=P)).then_inc(s_w0, 16)
                        sp.dma_start(wk[:, :, :], t["L0_xattn_Wk"].rearrange("(k p) n -> p k n", p=P)).then_inc(s_w0, 16)
                        sp.dma_start(wv[:, :, :], t["L0_xattn_Wv"].rearrange("(k p) n -> p k n", p=P)).then_inc(s_w0, 16)
                        sp.dma_start(wo[:, :, :], t["L0_xattn_Wo"].rearrange("(k p) n -> p k n", p=P)).then_inc(s_w0, 16)

                    @block.gpsimd
                    def _(pool):
                        pool.memset(ident[:, :], 0.0).then_inc(s_id, 1)
                        pool.memset(ones[:, :], 1.0).then_inc(s_id, 1)
                        pool.wait_ge(s_id, 2)
                        pool.affine_select(out=ident[:, :], in_=ident[:, :], compare_op=ALU.not_equal, fill=1.0,
                                           base=0, pattern=[[-1, P]], channel_multiplier=1).then_inc(s_id, 1)
                        pool.wait_ge(s_id, 3)
                        pool.tensor_copy(identb[:, :], ident[:, :]).then_inc(s_id, 1)
                        pool.memset(nhalf[:, :], -0.5).then_inc(s_id, 1)
                        pool.memset(zero[:, :], 0.0)
                        pool.memset(wq1[:, :, :], 0.0).then_inc(s_pad, 1)
                        pool.memset(wk1[:, :, :], 0.0).then_inc(s_pad, 1)
                        pool.memset(rows1[:, :, :], 0.0).then_inc(s_pad, 1)
                        pool.memset(wop[:, :, :], 0.0).then_inc(s_pad, 1)
                        pool.wait_ge(s_pad, 4)
                        r1 = rows1[:, :, :].rearrange("r a (h c) -> r a h c", c=32)
                        pool.memset(r1[0:1, 0, :, 16], 1.0).then_inc(s_pad, 1)
                        pool.memset(r1[0:1, 1, :, 16], 4.0 * BIG).then_inc(s_pad, 1)
                        pool.wait_ge(s_win, 64)
                        pool.tensor_copy(wop[:, :, :].rearrange("p o (h c) -> p o h c", c=32)[:, :, :, 0:16],
                                         win[:, 3, :, :].rearrange("p o (h c) -> p o h c", c=16)).then_inc(s_wop, 1)

                    @block.scalar
                    def _(act):
                        row = lambda a: a.rearrange("(c p) -> c p", p=P)
                        act.dma_start(brow[0:8, :], row(t["L0_xattn_bq"])).then_inc(s_small, 16)
                        act.dma_start(brow[8:16, :], row(t["L0_xattn_bk"])).then_inc(s_small, 16)
                        act.dma_start(brow[16:24, :], row(t["L3_xattn_wq_b"])).then_inc(s_small, 16)
                        act.dma_start(brow[24:32, :], row(t["L3_xattn_wk_b"])).then_inc(s_small, 16)
                        act.dma_start(brow[32:96, :], t["L1_ffn_b1"].rearrange("e (c p) -> (e c) p", p=P)).then_inc(s_small, 16)
                        act.dma_start(g_in[:, 0:4], t["g_xattn"].rearrange("(a n) -> a n", a=1).to_broadcast([P, 4])).then_inc(s_small, 16)
                        act.dma_start(g_in[:, 4:8], t["g_ffn"].rearrange("(a n) -> a n", a=1).to_broadcast([P, 4])).then_inc(s_small, 16)
                        act.dma_start(mint[:, :], t["mask_Bx1x1xS2_ik0"].rearrange("b i j s -> (i j) (b s)").to_broadcast([2, B * P])).then_inc(s_small, 16)
                        for n, w in enumerate(("Wq", "Wk", "Wv", "Wo")):
                            act.dma_start(win[:, n, :, :], t["L1_xattn_" + w].rearrange("(k p) n -> p k n", p=P)).then_inc(s_win, 16)
                        act.dma_start(packed[:, :], t["L0_ffn_packed_weight"].rearrange("(p n) -> p n", n=D)).then_inc(s_packed, 16)
                        act.wait_ge(s_pad, 6)
                        r1 = rows1[:, :, :].rearrange("r a (h c) -> r a h c", c=32)
                        act.dma_start(r1[0:1, 0, :, 0:16], t["L1_xattn_bq"].rearrange("(a h c) -> a h c", a=1, c=16)).then_inc(s_rows, 16)
                        act.dma_start(r1[1:2, 1, :, 0:16], t["L1_xattn_bk"].rearrange("(a h c) -> a h c", a=1, c=16)).then_inc(s_rows, 16)
                        act.wait_ge(s_small, 16 * 8)
                        act.activation(gate[:, :], g_in[:, :], ACT.Tanh).then_inc(s_g, 1)
                        for n in range(NG):
                            for k in range(DK):
                                act.wait_ge(s_ctxT, 2 * n + k + 1)
                                act.activation(ctxT[:, k, n * GT:(n + 1) * GT], pf[(2 * n + k) % 4][:, :], ACT.Copy).then_inc(s_ctxE, 1)
                        act.wait_ge(s_rows, 32)

                    jobs = []
                    for n, w in enumerate((wq1, wk1)):
                        for k in range(DK):
                            jobs.append(("f", [win[:, n, o, k * P:(k + 1) * P] for o in range(DK)],
                                         w[:, k, :].rearrange("p (h c) -> p h c", c=32)[:, :, 0:16],
                                         lambda ap: ap[:, 0:256].rearrange("p (h c) -> p h c", c=16), "win"))
                    for k in range(DK):
                        jobs.append(("f", [win[:, 2, o, k * P:(k + 1) * P] for o in range(DK)],
                                     wv1[:, k, :], lambda ap: ap[:, 0:256], "win"))
                    for k in range(4):
                        jobs.append(("f", [wop[:, o, k * P:(k + 1) * P] for o in range(DK)],
                                     wo1[:, k, :], lambda ap: ap[:, 0:256], "wop"))
                    jobs.append(("f", [brow[:, :]], cols[:, 0:96], lambda ap: ap[:, 0:96], "rows"))
                    jobs.append(("f", [rows1[0:1, 0, c * P:(c + 1) * P] for c in range(4)], cols[:, 96:100], lambda ap: ap[:, 0:4], "rows1"))
                    for k in range(DK):
                        jobs.append(("b", [ternp[:, s, k * P:(k + 1) * P] for s in range(4)],
                                     tern0[:, k, :], lambda ap: ap[:, 0:256], "tern"))
                    READY = {"win": (s_win, 64), "wop": (s_wop, 1), "rows": (s_small, 128), "rows1": (s_rows, 32), "tern": (s_q, 4)}

                    @block.tensor
                    def _(pe):
                        pe.wait_ge(s_id, 5)
                        for n in range(NG):
                            pe.wait_ge(s_ctx[n % 2], 16 * (n // 2 + 1))
                            for k in range(DK):
                                if n >= 2:
                                    pe.wait_ge(s_ctxE, 2 * (n - 2) + k + 1)
                                for a in range(G):
                                    m = pe.transpose(pf[(2 * n + k) % 4][:, a * P:(a + 1) * P], ctx_in[:, n % 2, a, k * P:(k + 1) * P], ident[:, :])
                                m.then_inc(s_ctxT, 1)

                        def turn(n, kind, srcs, what):
                            pe.wait_ge(*READY[what])
                            if n >= 2:
                                pe.wait_ge(s_evac, n - 1)
                            bank = (pf[4:6] if kind == "f" else pb)[n % 2]
                            at = 0
                            for src in srcs:
                                rows, width = src.shape[0], src.shape[1]
                                m = pe.transpose(bank[0:width, at:at + rows], src, (ident if kind == "f" else identb)[0:rows, 0:rows])
                                at += rows
                            m.then_inc(s_turn, 1)

                        for n, (kind, srcs, _, _, what) in enumerate(jobs):
                            turn(n, kind, srcs, what)

                    @block.vector
                    def _(v):
                        v.wait_ge(s_x, 16)
                        for b in range(B):
                            take_stats(b)
                        v.wait_ge(s_packed, 16)
                        for s in range(4):
                            nc.vector.tensor_scalar(code[:, s, :], packed[:, :], 2 * s, 3, ALU.logical_shift_right, ALU.bitwise_and).then_inc(s_dve, 1)
                        for s in range(4):
                            v.wait_ge(s_dve, s + 1)
                            nc.vector.tensor_scalar(ternp[:, s, :], code[:, s, :], -1.0, None, ALU.add).then_inc(s_q, 1)
                        v.wait_ge(s_small, 128)
                        v.wait_ge(s_id, 5)
                        nc.vector.tensor_scalar(mrow[:, :], mint[:, :], 0.0, ident[0:2, 0:1], ALU.not_equal, ALU.subtract).then_inc(s_dve, 1)
                        v.wait_ge(s_pad, 6)

                        def evac(n):
                            kind, _, dst, view, _ = jobs[n]
                            v.wait_ge(s_turn, n + 1)
                            bank = (pf[4:6] if kind == "f" else pb)[n % 2]
                            nc.vector.tensor_copy(dst, view(bank)).then_inc(s_evac, 1)

                        for n in range(len(jobs)):
                            evac(n)

        def load_ternary(sp, s_w12):
            for w, name in ((wq, "W1"), (wk, "W2")):
                src = t["L2_ffn_" + name].rearrange("(k p) n -> p k n", p=P)
                sp.dma_start(w[:, :, :].rearrange("p a b -> p (a b)").rearrange("p (k n) -> p k n", n=src.shape[2]), src).then_inc(s_w12, 16)

        def ternary_weights(st, tag, s_w12):
            S = lambda n: sem(n + tag, st)
            absw = sb("absw" + tag, [P, 2], F32, st)
            q1 = sb("q1" + tag, [P, FC, D], BF16, st)
            q2 = sb("q2" + tag, [P, DK, F], BF16, st)
            psum = st.enter_context(nc.psum_tensor("psum" + tag, [P, 2], F32))
            pb = [st.enter_context(nc.psum_tensor(f"setb{i}{tag}", [P, 1024], BF16)) for i in range(2)]
            s_sum, s_dve, s_q = S("abs_summed"), S("ternary_step"), S("ternary_ready")
            s_turn, s_evac = S("ternary_turned"), S("ternary_evacuated")
            flat = [w[:, :, :].rearrange("p k n -> p (k n)") for w in (wq, wk)]
            codes = [q1[:, :, :].rearrange("p k n -> p (k n)"), q2[:, :, :].rearrange("p k n -> p (k n)")]
            jobs = [(0, [q1[:, 4 * half + o, k * P:(k + 1) * P] for o in range(4)], tern1[:, k, half * 512:(half + 1) * 512])
                    for k in range(DK) for half in range(2)]
            jobs += [(1, [q2[:, o, k * P:(k + 1) * P] for o in range(DK)], tern2[:, k, :]) for k in range(FC)]

            def sums(pe):
                pe.wait_ge(s_sum, 2)
                pe.matmul(psum[:, :], ones[:, 0:P], absw[:, :], start=True, stop=True).then_inc(s_sum, 1)

            def turns(pe):
                for n, (m, tiles, _) in enumerate(jobs):
                    pe.wait_ge(s_q, m + 1)
                    if n >= 2:
                        pe.wait_ge(s_evac, n - 1)
                    for i, tile in enumerate(tiles):
                        ins = pe.transpose(pb[n % 2][:, i * P:(i + 1) * P], tile, identb[:, :])
                    ins.then_inc(s_turn, 1)

            def vector(v):
                v.wait_ge(s_w12, 32)
                for n in range(2):
                    nc.vector.tensor_reduce(absw[:, n:n + 1], flat[n], AX.X, ALU.add, apply_absolute_value=True).then_inc(s_sum, 1)
                v.wait_ge(s_sum, 3)
                nc.vector.tensor_scalar(wscale[:, 0:2], psum[:, :], 1.0 / (D * F), 1e-5, ALU.mult, ALU.max).then_inc(s_dve, 1)
                v.wait_ge(s_dve, 1)
                nc.vector.reciprocal(wscale[:, 2:4], wscale[:, 0:2]).then_inc(s_dve, 1)
                v.wait_ge(s_dve, 2)
                for n in range(2):
                    nc.vector.tensor_scalar(flat[n], flat[n], wscale[:, 2 + n:3 + n], ROUND, ALU.mult, ALU.add).then_inc(s_dve, 1)
                for n in range(2):
                    v.wait_ge(s_dve, 3 + n)
                    nc.vector.tensor_scalar(flat[n], flat[n], ROUND, -1.0, ALU.subtract, ALU.max).then_inc(s_dve, 1)
                for n in range(2):
                    v.wait_ge(s_dve, 5 + n)
                    nc.vector.tensor_scalar(codes[n], flat[n], 1.0, None, ALU.min).then_inc(s_q, 1)
                for n, (_, tiles, dst) in enumerate(jobs):
                    v.wait_ge(s_turn, n + 1)
                    nc.vector.tensor_copy(dst, pb[n % 2][:, 0:len(tiles) * P]).then_inc(s_evac, 1)

            return sums, turns, vector

        def weights3(sp):
            for w, name in ((wk, "wk_w"), (wq, "wq_w"), (wv, "wv_w"), (wo, "wo_w")):
                sp.dma_start(w[:, :, :], t["L3_xattn_" + name].rearrange("(k p) n -> p k n", p=P)).then_inc(s_w3, 16)

        def moments_vector(v, s_mo, s_step):
            me, ve, mo, vo = (stats[:, :, i] for i in (1, 2, 4, 5))
            nc.vector.tensor_tensor(mom[:, 0, :], me, mo, ALU.add).then_inc(s_step, 1)
            nc.vector.tensor_tensor(mom[:, 1, :], me, mo, ALU.subtract).then_inc(s_step, 1)
            nc.vector.tensor_tensor(mom[:, 2, :], ve, vo, ALU.add).then_inc(s_step, 1)
            v.wait_ge(s_step, 1)
            nc.vector.tensor_scalar(mean[:, :], mom[:, 0, :], 0.5, None, ALU.mult).then_inc(s_step, 1)
            v.wait_ge(s_step, 2)
            nc.vector.scalar_tensor_tensor(out=mom[:, 3, :], in0=mom[:, 1, :], scalar=0.25, in1=mom[:, 1, :],
                                           op0=ALU.mult, op1=ALU.mult).then_inc(s_step, 1)
            v.wait_ge(s_step, 3)
            nc.vector.tensor_scalar(mom[:, 4, :], mom[:, 2, :], 1.0 / D, LN_EPS, ALU.mult, ALU.add).then_inc(s_step, 1)
            v.wait_ge(s_step, 6)
            nc.vector.tensor_tensor(veps[:, :], mom[:, 4, :], mom[:, 3, :], ALU.add).then_inc(s_mo, 1)

        def root_pool(pool, s_mo, s_rs):
            pool.wait_ge(s_mo, 1)
            pool.tensor_tensor(rstd[:, :], veps[:, :], nhalf[:, :], ALU.pow).then_inc(s_rs, 1)

        def norm_transposed(block, st, tag, keep=None):
            S = lambda n: sem(n + tag, st)
            xn = keep if keep is not None else sb("xn" + tag, [P, 2 * G, D], F32, st)
            ring = xn.shape[1]
            ps = banks(st, [f"xt{i}" + tag for i in range(4)])
            pt = [ps[f"xt{i}" + tag] for i in range(4)]
            s_mo, s_step, s_rs = S("moments_done"), S("moment_step"), S("rstd_done")
            s_xn, s_turn = S("xn_ready"), S("xn_turned")
            s_ev = [S("first_chunk_evacuated"), S("second_chunk_evacuated")]

            @block.gpsimd
            def _(pool):
                root_pool(pool, s_mo, s_rs)

            @block.vector
            def _(v):
                def norm(n):
                    if n * G >= ring:
                        v.wait_ge(s_turn, DK * (n - 1))
                    for b in range(n * G, (n + 1) * G):
                        m = nc.vector.tensor_scalar(xn[:, b % ring, :], x[:, b, :], mean[:, b:b + 1], rstd[:, b:b + 1], ALU.subtract, ALU.mult)
                    m.then_inc(s_xn, 1)

                moments_vector(v, s_mo, s_step)
                v.wait_ge(s_rs, 1)
                norm(0)
                for n in range(NG):
                    if n + 1 < NG:
                        norm(n + 1)
                    v.wait_ge(s_turn, DK * n + 2)
                    nc.vector.tensor_copy(xnT[:, 1, n * GT:(n + 1) * GT], pt[2 * (n % 2) + 1][:, :]).then_inc(s_ev[1], 1)

            @block.tensor
            def _(pe):
                for n in range(NG):
                    pe.wait_ge(s_xn, n + 1)
                    for k in range(DK):
                        if n >= 2:
                            pe.wait_ge(s_ev[k], n - 1)
                        for a in range(G):
                            m = pe.transpose(pt[2 * (n % 2) + k][:, a * P:(a + 1) * P], xn[:, (n * G + a) % ring, k * P:(k + 1) * P], ident[:, :])
                        m.then_inc(s_turn, 1)

            @block.scalar
            def _(act):
                for n in range(NG):
                    act.wait_ge(s_turn, DK * n + 1)
                    act.activation(xnT[:, 0, n * GT:(n + 1) * GT], pt[2 * (n % 2)][:, :], ACT.Copy).then_inc(s_ev[0], 1)

        def attention(layer, tag):
            HP, DV, KT = {0: (64, 64, 1), 1: (32, 16, 1), 3: (64, 64, 2)}[layer]
            HC = P // HP
            NC = H // HC
            HU = 4 // KT
            CU = HU // HC
            U = H // HU
            N = G * U
            OB = NC // 4
            UO = U // OB
            VH = (H * DV + 511) // 512
            VW = H * DV // VH
            qscale = {0: 0.125, 1: 0.25, 3: 0.125}[layer]
            Wq, Wk, Wv, Wo = (wq1, wk1, wv1, wo1) if layer == 1 else (wq, wk, wv, wo)
            bcol = {0: 0, 1: 96, 3: 16}[layer]
            st = ExitStack()
            with st:
                S = lambda n: sem(n + tag, st)
                qT = sb("qT" + tag, [P, NC, GT], F32, st)
                kd = sb("kd" + tag, [P, NC, HC, GT], F32, st)
                cg = sb("cg" + tag, [P, DK, GT], F32, st)
                vv = sb("vv" + tag, [P, 2, H, HP], F32, st)
                prob = sb("prob" + tag, [P, 4, 512], F32, st)
                probT = sb("probT" + tag, [P, 2, 512], F32, st)
                nmax = sb("nmax" + tag, [P, 2, HU], F32, st)
                sums = sb("sums" + tag, [P, 4, HU], F32, st)
                rinv = sb("rinv" + tag, [P, 2, HU], F32, st)
                oT = sb("oT" + tag, [P, 2, NC, P], F32, st)
                bv = sb("bv" + tag, [P, H * DV], F32, st)
                bo = sb("bo" + tag, [P, D], F32, st)
                biased = sb("biased" + tag, [P, D], F32, st)
                bqs = sb("bqs" + tag, [P, 8], F32, st)
                ps = banks(st, [n + tag for n in ("pp0", "pp1", "ps0", "ps1", "pt0", "pt1", "po", "pw")])
                pp = [ps["pp0" + tag], ps["pp1" + tag]]
                psc = [ps["ps0" + tag], ps["ps1" + tag]]
                ptr = [ps["pt0" + tag], ps["pt1" + tag]]
                po, pw = ps["po" + tag], ps["pw" + tag]
                s_bias, s_bq, s_pads = S("bias_loaded"), S("bq_scaled"), S("pads_cleared")
                s_cg, s_up = S("group_context_ready"), S("tokens_updated")
                s_mo, s_step, s_rs = S("moments_done"), S("moment_step"), S("rstd_done")
                s_xn, s_xt, s_xe = S("xn_ready"), S("xn_turned"), S("xn_evacuated")
                xgT = xnT[:, :, 0:GT]
                xn = xnT[:, 0, GT:GT + G * D].rearrange("p (a d) -> p a d", d=D)
                s_p, s_pf = S("proj_ready"), S("proj_evacuated")
                s_w, s_wf = S("work_ready"), S("work_evacuated")
                s_s, s_nm, s_e = S("scores_ready"), S("nmax_ready"), S("probs_ready")
                s_r, s_x = S("rinv_ready"), S("probs_scaled")
                s_t, s_tf = S("probs_turned"), S("turned_evacuated")
                s_pv, s_of = S("values_summed"), S("out_evacuated")
                pre = "L%d_xattn_" % layer
                bv_d, bo_d = (t[pre + "wv_b"], t[pre + "wo_b"]) if layer == 3 else (t[pre + "bv"], t[pre + "bo"])
                NP = 2 * NC
                TAIL = range(N + 2 if layer == 1 else N, N + 5)
                NW = G * (VH + 1)
                NO = G * OB

                after = {n: [] for n in range(N + 5)}
                for half in range(VH):
                    after[half].append((half, 0))
                for a in range(1, G):
                    after[a * U - U + 3].append((0, a))
                    if VH == 2:
                        after[a * U - U + 5].append((1, a))
                for a in range(G):
                    after[a * U + U + 4].append(("out", a))
                order = [use for n in range(N + 5) for use in after[n]]
                wv_last = order.index((VH - 1, G - 1))

                if layer == 1:
                    msk = sb("msk", [P, GT], I32, st)
                    val = sb("val", [P, GT], F32, st)
                    cm = sb("cm", [P, DK, GT], F32, st)
                    s_msk, s_val, s_cm = S("mask_loaded"), S("valid_ready"), S("masked_ready")
                if layer == 3:
                    md3 = [w[:, :, :].rearrange("p k n -> p (k n)").rearrange("p (c n) -> p c n", n=P) for w in (wq1, wk1)]
                    mv = wo1[:, :, :].rearrange("p k n -> p (k n)").rearrange("p (h d) -> p h d", d=HP)
                    s_mem, s_memT, s_memE = S("memory_loaded"), S("memory_turned"), S("memory_keys_ready")
                    mk_in = vv[:, 1, :, :].rearrange("p h d -> p (h d)")

                def tiles(bank):
                    return bank.rearrange("p (h t k) -> p h t k", h=HU, t=KT)

                with nc.Block() as block:
                    @block.sync
                    def _(sp):
                        sp.dma_start(bv[:, :], bv_d.rearrange("(a n) -> a n", a=1).to_broadcast([P, H * DV])).then_inc(s_bias, 16)
                        sp.dma_start(bo[:, :], bo_d.rearrange("(a n) -> a n", a=1).to_broadcast([P, D])).then_inc(s_bias, 16)
                        if layer == 3:
                            sp.dma_start(mk_in, t["L3_xattn_mk"][0]).then_inc(s_mem, 16)
                            sp.dma_start(mv.rearrange("p h d -> p (h d)"), t["L3_xattn_mv"][0]).then_inc(s_mem, 16)
                        if layer == 1:
                            md = t["mask_Bx1x1xS2_ik0"].rearrange("b i j s -> (i j) (b s)")
                            with sp.Fori(0, NG) as g:
                                sp.wait_ge(s_val, g + 1)
                                sp.dma_start(msk[:, :], md[:, ds(g * GT, GT)].to_broadcast([P, GT])).then_inc(s_msk, 16)
                        if layer in slots_of:
                            zero_rows(sp, layer)

                    @block.gpsimd
                    def _(pool):
                        for c in range(NC):
                            pool.memset(kd[:, c, :, :], 0.0).then_inc(s_pads, 1)
                            if c == 1:
                                root_pool(pool, s_mo, s_rs)
                        if layer == 1:
                            pool.memset(vv[:, :, :, :], 0.0).then_inc(s_pads, 1)
                        if layer == 3:
                            for j in range(HC):
                                pool.memset(md3[j], 0.0).then_inc(s_pads, 1)
                        pool.sem_inc(s_x, 2)

                        def group(g, first):
                            if not first:
                                pool.wait_ge(s_w, (g - 1) * NW + wv_last + 1)
                            pool.tensor_copy(cg[:, :, :], ctxT[:, :, ds(g * GT, GT)]).then_inc(s_cg, 1)
                            for n in range(N):
                                pool.wait_ge(s_r, g * N + n + 1)
                                pb = prob[:, n % 4, :].rearrange("p (h k) -> p h k", h=HU)
                                pool.tensor_tensor(pb, pb, rinv[:, n % 2, :].unsqueeze(2).to_broadcast([P, HU, KT * P]), ALU.mult).then_inc(s_x, 1)
                        group(0, True)
                        with pool.Fori(1, NG) as g:
                            group(g, False)

                    @block.tensor
                    def _(pe):
                        pe.sem_inc(s_t, 4)
                        if layer == 3:
                            pe.wait_ge(s_w3, 64)
                        pe.wait_ge(s_bias, 32)
                        def project(g, i):
                            c, isk = i % NC, i < NC
                            if c == 0 and not isk:
                                pe.wait_ge(s_xn, g * G + G)
                                pe.wait_ge(s_e, g * N + 2)
                                for k in range(DK):
                                    for a in range(G):
                                        m = pe.transpose(psc[k][:, a * P:(a + 1) * P], xn[:, a, k * P:(k + 1) * P], ident[:, :])
                                    m.then_inc(s_xt, 1)
                                pe.wait_ge(s_xe, g * DK + DK)
                            pe.wait_ge(s_pf, g * NP + i + 1)
                            W = Wk if isk else Wq
                            masked = isk and layer == 1
                            for k in range(DK):
                                if isk and layer == 1:
                                    if c == 0 and k == 0:
                                        pe.wait_ge(s_cm, g * DK + DK)
                                    src = cm[:, k, :]
                                elif isk:
                                    src = ctxT[:, k, ds(g * GT, GT)]
                                else:
                                    src = xgT[:, k, :]
                                m = pe.matmul(pp[i % 2][:, :], W[:, k, c * P:(c + 1) * P], src,
                                              start=(k == 0), stop=(k == DK - 1 and not masked))
                            if masked:
                                m = pe.matmul(pp[i % 2][:, :], rows1[0:2, 1, c * P:(c + 1) * P], mrow[0:2, ds(g * GT, GT)], start=False, stop=True)
                            m.then_inc(s_p, 1)

                        def group(g, last):
                            pe.wait_ge(s_cg, g + 1)
                            w = [0]

                            def work(kind, a):
                                if kind != "out":
                                    pe.wait_ge(s_wf, g * NW + w[0] + 1)
                                    for k in range(DK):
                                        m = pe.matmul(pw[:, 0:VW], cg[:, k, a * P:(a + 1) * P], Wv[:, k, kind * VW:(kind + 1) * VW],
                                                      start=(k == 0), stop=(k == DK - 1))
                                    m.then_inc(s_w, 1)
                                    w[0] += 1
                                else:
                                    pe.wait_ge(s_of, g * NO + (a + 1) * OB + 1)
                                    pe.wait_ge(s_wf, g * NW + w[0] + 1)
                                    for c in range(NC):
                                        m = pe.matmul(pw[:, 0:D], oT[:, a % 2, c, :], Wo[:, c, :], start=(c == 0), stop=(c == NC - 1))
                                    m.then_inc(s_w, 1)
                                    w[0] += 1

                            pe.wait_ge(s_pf, g * NP + NP + 2)
                            for n in range(N + 5):
                                if n < N:
                                    a, u = n // U, n % U
                                    pe.wait_ge(s_e, g * N + n + 1)
                                    for i in range(CU):
                                        c = u * CU + i
                                        queries = qT[:, c, a * P:(a + 1) * P]
                                        scores = tiles(psc[n % 2][:, :])[:, i * HC:(i + 1) * HC]
                                        m = pe.matmul(scores[:, :, 0, :], queries, kd[:, c, :, a * P:(a + 1) * P], start=True, stop=True)
                                        if layer == 3:
                                            for j in range(HC):
                                                m = pe.matmul(scores[:, j, 1, :], queries, md3[j][:, c, :], start=True, stop=True)
                                    m.then_inc(s_s, 1)
                                if 2 <= n <= N + 1:
                                    m1 = n - 2
                                    pe.wait_ge(s_x, g * N + m1 + 3)
                                    pe.wait_ge(s_tf, g * N + m1 + 1)
                                    for i in range(4):
                                        m = pe.transpose(ptr[m1 % 2][:, i * P:(i + 1) * P], prob[:, m1 % 4, i * P:(i + 1) * P], ident[:, :])
                                    m.then_inc(s_t, 1)
                                if 3 <= n <= N + 2:
                                    m2 = n - 3
                                    a, u = m2 // U, m2 % U
                                    pe.wait_ge(s_tf, g * N + m2 + 3)
                                    if u == 0:
                                        pe.wait_ge(s_wf, g * NW + w[0] + 1)
                                    if u % UO == 0:
                                        pe.wait_ge(s_of, g * NO + m2 // UO + 1)
                                    for i in range(HU):
                                        h = u * HU + i
                                        p0, at = HP * (h % HC), (h // HC) % 4 * P
                                        for kt in range(KT):
                                            vals = mv[:, h, :] if kt else vv[:, a % 2, h, :]
                                            m = pe.matmul(po[p0:p0 + HP, at:at + P], vals, tiles(probT[:, m2 % 2, :])[:, i, kt, :],
                                                          start=(kt == 0), stop=(kt == KT - 1))
                                    m.then_inc(s_pv, 1)
                                for kind, a in after[n]:
                                    work(kind, a)
                                if n in TAIL and not last:
                                    project(g + 1, n - TAIL[0])
                            assert w[0] == NW
                            if not last:
                                for i in range(len(TAIL), NP):
                                    project(g + 1, i)

                        for i in range(NP):
                            project(0, i)
                        if layer == 3:
                            pe.wait_ge(s_mem, 32)
                            for half in range(2):
                                for c in range(4):
                                    m = pe.transpose(ptr[half][:, c * P:(c + 1) * P], mk_in[:, (4 * half + c) * P:(4 * half + c + 1) * P], ident[:, :])
                                m.then_inc(s_memT, 1)
                            pe.wait_ge(s_memE, 4)
                        with pe.Fori(0, NG - 1) as g:
                            group(g, False)
                        group(NG - 1, True)

                    @block.scalar
                    def _(act):
                        act.sem_inc(s_pf, 2)
                        act.sem_inc(s_e, 2)
                        act.activation(bqs[:, 0:NC], cols[:, bcol:bcol + NC], ACT.Copy, scale=qscale).then_inc(s_bq, 1)
                        act.wait_ge(s_bq, 1)

                        def evacuate(g, first):
                            for i in range(NP):
                                c, isk = i % NC, i < NC
                                act.wait_ge(s_p, g * NP + i + 1)
                                src = pp[i % 2]
                                if not isk:
                                    m = act.activation(qT[:, c, :], src[:, :], ACT.Identity, bias=bqs[:, c:c + 1], scale=qscale)
                                else:
                                    if first:
                                        act.wait_ge(s_pads, c + 1)
                                    for j in range(HC):
                                        own = slice(HP * j, HP * (j + 1))
                                        if layer == 1:
                                            m = act.activation(kd[own, c, j, :], src[own, :], ACT.Copy)
                                        else:
                                            m = act.activation(kd[own, c, j, :], src[own, :], ACT.Identity, bias=cols[own, bcol + 8 + c:bcol + 9 + c])
                                m.then_inc(s_pf, 1)

                        def group(g):
                            for n in range(N):
                                act.wait_ge(s_nm, g * N + n + 1)
                                act.wait_ge(s_t, g * N + n + 1)
                                for i in range(HU):
                                    m = act.activation(prob[:, n % 4, i * KT * P:(i + 1) * KT * P], psc[n % 2][:, i * KT * P:(i + 1) * KT * P],
                                                       ACT.Exp, bias=nmax[:, n % 2, i:i + 1], accum_out=sums[:, n % 4, i:i + 1])
                                m.then_inc(s_e, 1)

                        evacuate(0, True)
                        with act.Fori(0, NG - 1) as g:
                            group(g)
                            evacuate(g + 1, False)
                        group(NG - 1)

                    @block.vector
                    def _(v):
                        v.sem_inc(s_wf, 1)
                        v.sem_inc(s_tf, 2)
                        v.sem_inc(s_of, 1)
                        if layer == 1:
                            v.sem_inc(s_val, 1)
                        moments_vector(v, s_mo, s_step)
                        v.wait_ge(s_bias, 32)
                        v.wait_ge(s_rs, 1)
                        def sources(g):
                            if layer == 1:
                                v.wait_ge(s_msk, (g + 1) * 16)
                                nc.vector.tensor_scalar(val[:, :], msk[:, :], 0.0, None, ALU.not_equal).then_inc(s_val, 1)
                                v.wait_ge(s_val, g + 2)
                                for k in range(DK):
                                    nc.vector.tensor_tensor(cm[:, k, :], ctxT[:, k, ds(g * GT, GT)], val[:, :], ALU.mult).then_inc(s_cm, 1)
                            for a in range(G):
                                b = g * G + a
                                nc.vector.tensor_scalar(xn[:, a, :], x[:, ds(b, 1), :].rearrange("p a c -> p (a c)"),
                                                        mean[:, ds(b, 1)], rstd[:, ds(b, 1)], ALU.subtract, ALU.mult).then_inc(s_xn, 1)

                        def turned_tokens(g):
                            for k in range(DK):
                                v.wait_ge(s_xt, g * DK + (k + 1))
                                nc.vector.tensor_copy(xgT[:, k, :], psc[k][:, :]).then_inc(s_xe, 1)

                        def group(g, last):
                            w = [0]

                            def work(kind, a):
                                v.wait_ge(s_w, g * NW + w[0] + 1)
                                if kind != "out":
                                    hh = H // VH
                                    as_heads = lambda ap: ap.rearrange("p (h d) -> p h d", d=DV)
                                    nc.vector.tensor_tensor(vv[:, a % 2, kind * hh:(kind + 1) * hh, 0:DV], as_heads(pw[:, 0:VW]),
                                                            as_heads(bv[:, kind * VW:(kind + 1) * VW]), ALU.add).then_inc(s_wf, 1)
                                    w[0] += 1
                                else:
                                    xb = x[:, ds(g * G + a, 1), :].rearrange("p a c -> p (a c)")
                                    nc.vector.tensor_tensor(biased[:, :], pw[:, 0:D], bo[:, :], ALU.add).then_inc(s_wf, 1)
                                    w[0] += 1
                                    v.wait_ge(s_wf, g * NW + w[0] + 1)
                                    nc.vector.scalar_tensor_tensor(out=xb, in0=biased[:, :], scalar=gate[:, layer:layer + 1], in1=xb,
                                                                   op0=ALU.mult, op1=ALU.add).then_inc(s_up, 1)
                                    v.wait_ge(s_up, g * G + (a + 1))
                                    take_stats(g * G + a)

                            for n in range(N + 5):
                                if 1 <= n <= N:
                                    m0 = n - 1
                                    v.wait_ge(s_e, g * N + m0 + 3)
                                    v.wait_ge(s_x, g * N + m0 + 1)
                                    nc.vector.reciprocal(rinv[:, m0 % 2, :], sums[:, m0 % 4, :]).then_inc(s_r, 1)
                                if n < N:
                                    v.wait_ge(s_s, g * N + n + 1)
                                    v.wait_ge(s_e, g * N + n + 1)
                                    nc.vector.tensor_reduce(nmax[:, n % 2, :], psc[n % 2][:, :].rearrange("p (h k) -> p h k", h=HU),
                                                            AX.X, ALU.max, negate=True).then_inc(s_nm, 1)
                                if 2 <= n <= N + 1:
                                    m1 = n - 2
                                    v.wait_ge(s_t, g * N + m1 + 5)
                                    if m1 >= 2:
                                        v.wait_ge(s_pv, g * N + m1 - 1)
                                    nc.vector.tensor_copy(probT[:, m1 % 2, :], ptr[m1 % 2][:, :]).then_inc(s_tf, 1)
                                if 3 <= n <= N + 2 and (n - 3) % UO == UO - 1:
                                    m2 = n - 3
                                    a, ob = m2 // U, m2 % U // UO
                                    v.wait_ge(s_pv, g * N + m2 + 1)
                                    nc.vector.tensor_copy(oT[:, a % 2, 4 * ob:4 * ob + 4, :], po[:, :].rearrange("p (c n) -> p c n", n=P)).then_inc(s_of, 1)
                                for kind, a in after[n]:
                                    work(kind, a)
                                if n == N + 1 and not last:
                                    sources(g + 1)
                            if not last:
                                turned_tokens(g + 1)

                        sources(0)
                        turned_tokens(0)
                        if layer == 1:
                            v.wait_ge(s_pads, NC + 1)
                        if layer == 3:
                            v.wait_ge(s_pads, NC + HC)
                            for half in range(2):
                                v.wait_ge(s_memT, half + 1)
                                for j in range(HC):
                                    own = slice(HP * j, HP * (j + 1))
                                    nc.vector.tensor_copy(md3[j][own, 4 * half:4 * half + 4, :], ptr[half][own, :].rearrange("p (c n) -> p c n", n=P)).then_inc(s_memE, 1)
                        with v.Fori(0, NG - 1) as g:
                            group(g, False)
                        group(NG - 1, True)

        def bitlinear(layer, tag):
            two = layer == 2
            R = 8
            W1, N1 = (tern1, F) if two else (tern0, D)
            xnv = xnT[:, :, :].rearrange("p k n -> p (k n)").rearrange("p (b d) -> p b d", d=D)
            gcol = gate[:, 4 + layer:5 + layer]
            st = ExitStack()
            with st:
                S = lambda n: sem(n + tag, st)
                am = sb("am" + tag, [P, B], F32, st)
                am1 = sb("am1" + tag, [P, B], F32, st)
                up = sb("up" + tag, [P, B], F32, st)
                upr = sb("upr" + tag, [P, B], F32, st)
                down = sb("down" + tag, [P, B], F32, st)
                wsc = sb("wsc" + tag, [P, 2], F32, st)
                bias = sb("bias" + tag, [P, D], F32, st)
                gbias = sb("gbias" + tag, [P, D], F32, st)
                tmp = sb("tmp" + tag, [P, 2, D], F32, st)
                q = sb("q" + tag, [P, 2, D], BF16, st)
                qT = sb("qT" + tag, [P, 2, DK, P], BF16, st)
                s_mo, s_step, s_rs = S("moments_done"), S("moment_step"), S("rstd_done")
                s_b, s_n, s_am, s_x2 = S("bias_loaded"), S("xn_ready"), S("absmax_ready"), S("bias_added")
                s_d = S("dve_step")
                s_q, s_t, s_e = S("codes_ready"), S("codes_turned"), S("codes_evacuated")
                s_m, s_y = S("sums_ready"), S("tokens_done")
                pt = [st.enter_context(nc.psum_tensor(f"pt{i}{tag}", [P, 1024], BF16)) for i in range(2)]
                NY = 4 if two else 3
                if two:
                    b1 = sb("b1" + tag, [P, F], F32, st)
                    h = sb("h" + tag, [P, 2, F], F32, st)
                    tmp2 = sb("tmp2" + tag, [P, F], F32, st)
                    q2 = sb("q2" + tag, [P, 2, F], BF16, st)
                    q2T = sb("q2T" + tag, [P, 2, FC, P], BF16, st)
                    am2 = sb("am2" + tag, [P, 2, 5], F32, st)
                    ph = [st.enter_context(nc.psum_tensor(f"ph{i}{tag}", [P, 512], F32)) for i in range(2)]
                    pt2 = st.enter_context(nc.psum_tensor("pt2" + tag, [P, 1024], BF16))
                    s_h, s_gl, s_q2 = S("hidden_ready"), S("gelu_done"), S("codes2_ready")
                    s_m1, s_t2, s_e2 = S("sums1_ready"), S("codes2_turned"), S("codes2_evacuated")
                py = [st.enter_context(nc.psum_tensor(f"py{i}{tag}", [P, D], F32)) for i in range(2)]
                KD = (2 + 7) * R if two else 2 * R

                with nc.Block() as block:
                    @block.sync
                    def _(sp):
                        row = lambda a: a.rearrange("(a n) -> a n", a=1)
                        sp.dma_start(bias[:, :], row(t["L2_ffn_b2" if two else "L0_ffn_bias"]).to_broadcast([P, D])).then_inc(s_b, 16)
                        if two:
                            sp.dma_start(b1[:, :], row(t["L2_ffn_b1"]).to_broadcast([P, F])).then_inc(s_b, 16)
                            weights3(sp)
                        else:
                            sp.dma_start(wsc[:, 0:1], row(t["L0_ffn_weight_scale"]).to_broadcast([P, 1])).then_inc(s_b, 16)

                    @block.gpsimd
                    def _(pool):
                        root_pool(pool, s_mo, s_rs)
                        pool.wait_ge(s_n, B)
                        pool.wait_ge(s_b, 33)
                        pool.tensor_tensor(x[:, :, :], x[:, :, :], gbias[:, :].unsqueeze(1).to_broadcast([P, B, D]), ALU.add).then_inc(s_x2, 1)

                    @block.vector
                    def _(v):
                        moments_vector(v, s_mo, s_step)
                        v.wait_ge(s_b, 32)
                        nc.vector.tensor_scalar(gbias[:, :], bias[:, :], gcol, None, ALU.mult).then_inc(s_b, 1)
                        wlast = wscale[:, 1:2] if two else wsc[:, 0:1]
                        nc.vector.tensor_scalar(wsc[:, 1:2], wlast, gcol, 1.0 / 127.0, ALU.mult, ALU.mult).then_inc(s_step, 1)
                        v.wait_ge(s_step, 7)
                        v.wait_ge(s_rs, 1)
                        with v.Fori(0, NG) as g:
                            for a in range(G):
                                b = g * G + a
                                nc.vector.tensor_scalar(xnv[:, ds(b, 1), :].rearrange("p a c -> p (a c)"), x[:, ds(b, 1), :].rearrange("p a c -> p (a c)"),
                                                        mean[:, ds(b, 1)], rstd[:, ds(b, 1)], ALU.subtract, ALU.mult).then_inc(s_n, 1)
                            v.wait_ge(s_n, g * G + G)
                            nc.vector.tensor_reduce(am[:, ds(g * G, G)], xnv[:, ds(g * G, G), :], AX.X, ALU.max, apply_absolute_value=True).then_inc(s_am, 1)
                        v.wait_ge(s_am, NG)
                        nc.vector.tensor_scalar(am1[:, :], am[:, :], 1e-5, None, ALU.max).then_inc(s_am, 1)
                        v.wait_ge(s_am, NG + 1)
                        nc.vector.reciprocal(upr[:, :], am1[:, :]).then_inc(s_am, 1)
                        if two:
                            nc.vector.tensor_scalar(down[:, :], am1[:, :], wscale[:, 0:1], 1.0 / 127.0, ALU.mult, ALU.mult).then_inc(s_am, 1)
                        else:
                            nc.vector.tensor_scalar(down[:, :], am1[:, :], wsc[:, 1:2], None, ALU.mult).then_inc(s_am, 1)
                        v.wait_ge(s_am, NG + 2)
                        nc.vector.tensor_scalar(up[:, :], upr[:, :], 127.0, None, ALU.mult).then_inc(s_am, 1)
                        v.wait_ge(s_am, NG + 4)

                        if two:
                            v.sem_inc(s_h, 1)
                        with v.Fori(0, B // R) as g:
                            done = [0]

                            def step(ins):
                                ins.then_inc(s_d, 1)
                                done[0] += 1
                                v.wait_ge(s_d, g * KD + done[0])

                            def codes(dst, src, scratch, scale, s_ready):
                                step(nc.vector.tensor_scalar(scratch, src, scale, ROUND, ALU.mult, ALU.add))
                                step(nc.vector.tensor_scalar(scratch, scratch, ROUND, -128.0, ALU.subtract, ALU.max))
                                nc.vector.tensor_scalar(dst, scratch, 127.0, None, ALU.min).then_inc(s_ready, 1)

                            for n in range(R + NY - 1):
                                if n < R:
                                    b = g * R + n
                                    v.wait_ge(s_t, b + 1)
                                    codes(q[:, n % 2, :], xnv[:, ds(b, 1), :].rearrange("p a c -> p (a c)"), tmp[:, n % 2, :], up[:, ds(b, 1)], s_q)
                                if two and 2 <= n <= R + 1:
                                    a = n - 2
                                    b = g * R + a
                                    v.wait_ge(s_gl, b + 1)
                                    sc = am2[:, a % 2, :]
                                    hh = h[:, a % 2, :]
                                    step(nc.vector.tensor_reduce(sc[:, 0:1], hh, AX.X, ALU.max, apply_absolute_value=True))
                                    step(nc.vector.tensor_scalar(sc[:, 1:2], sc[:, 0:1], 1e-5, None, ALU.max))
                                    step(nc.vector.reciprocal(sc[:, 2:3], sc[:, 1:2]))
                                    step(nc.vector.tensor_scalar(sc[:, 3:4], sc[:, 2:3], 127.0, None, ALU.mult))
                                    step(nc.vector.tensor_scalar(sc[:, 4:5], sc[:, 1:2], wsc[:, 1:2], None, ALU.mult))
                                    v.wait_ge(s_t2, b + 1)
                                    codes(q2[:, a % 2, :], hh, tmp2[:, :], sc[:, 3:4], s_q2)
                                    v.wait_ge(s_q2, b + 1)
                                if two and 1 <= n <= R:
                                    a = n - 1
                                    b = g * R + a
                                    v.wait_ge(s_m1, b + 3)
                                    for half in range(2):
                                        c = slice(half * 512, half * 512 + 512)
                                        nc.vector.scalar_tensor_tensor(out=h[:, a % 2, c], in0=ph[half][:, :], scalar=down[:, ds(b, 1)], in1=b1[:, c],
                                                                       op0=ALU.mult, op1=ALU.add).then_inc(s_h, 1)
                                if NY - 1 <= n:
                                    a = n - NY + 1
                                    b = g * R + a
                                    v.wait_ge(s_m, b + 3)
                                    if a == 0:
                                        v.wait_ge(s_x2, 1)
                                    xb = x[:, ds(b, 1), :].rearrange("p a c -> p (a c)")
                                    nc.vector.scalar_tensor_tensor(out=xb, in0=py[a % 2][:, :], scalar=am2[:, a % 2, 4:5] if two else down[:, ds(b, 1)], in1=xb,
                                                                   op0=ALU.mult, op1=ALU.add).then_inc(s_y, 1)
                                    v.wait_ge(s_y, b + 3)
                                    take_stats(b)
                            assert done[0] == KD

                    @block.tensor
                    def _(pe):
                        pe.sem_inc(s_t, 2)
                        pe.sem_inc(s_m, 2)
                        if two:
                            pe.sem_inc(s_t2, 2)
                            pe.sem_inc(s_m1, 2)
                        with pe.Fori(0, B // R) as g:
                            for n in range(R + NY - 1):
                                if 1 <= n <= R:
                                    a = n - 1
                                    b = g * R + a
                                    pe.wait_ge(s_e, b + 3)
                                    if two:
                                        pe.wait_ge(s_h, 2 * b + 1)
                                        for half in range(2):
                                            for k in range(DK):
                                                m = pe.matmul(ph[half][:, :], qT[:, a % 2, k, :], W1[:, k, half * 512:half * 512 + 512], start=(k == 0), stop=(k == DK - 1))
                                        m.then_inc(s_m1, 1)
                                    else:
                                        pe.wait_ge(s_y, b + 1)
                                        for k in range(DK):
                                            m = pe.matmul(py[a % 2][:, :], qT[:, a % 2, k, :], W1[:, k, :], start=(k == 0), stop=(k == DK - 1))
                                        m.then_inc(s_m, 1)
                                if n < R:
                                    b = g * R + n
                                    pe.wait_ge(s_q, b + 1)
                                    pe.wait_ge(s_e, b + 1)
                                    for k in range(DK):
                                        m = pe.transpose(pt[n % 2][:, k * P:(k + 1) * P], q[:, n % 2, k * P:(k + 1) * P], identb[:, :])
                                    m.then_inc(s_t, 1)
                                if two and 2 <= n <= R + 1:
                                    a = n - 2
                                    b = g * R + a
                                    pe.wait_ge(s_q2, b + 1)
                                    pe.wait_ge(s_e2, b + 1)
                                    for c in range(FC):
                                        m = pe.transpose(pt2[:, c * P:(c + 1) * P], q2[:, a % 2, c * P:(c + 1) * P], identb[:, :])
                                    m.then_inc(s_t2, 1)
                                if two and 3 <= n:
                                    a = n - 3
                                    b = g * R + a
                                    pe.wait_ge(s_e2, b + 2)
                                    pe.wait_ge(s_y, b + 1)
                                    for c in range(FC):
                                        m = pe.matmul(py[a % 2][:, :], q2T[:, a % 2, c, :], tern2[:, c, :], start=(c == 0), stop=(c == FC - 1))
                                    m.then_inc(s_m, 1)

                    @block.scalar
                    def _(act):
                        act.sem_inc(s_e, 2)
                        act.sem_inc(s_y, 2)
                        if two:
                            act.sem_inc(s_e2, 1)
                        with act.Fori(0, B // R) as g:
                            for n in range(R + 2):
                                if n < R:
                                    b = g * R + n
                                    act.wait_ge(s_t, b + 3)
                                    act.wait_ge(s_m1 if two else s_m, b + 1)
                                    act.activation(qT[:, n % 2, :, :], pt[n % 2][:, 0:D].rearrange("p (k n) -> p k n", n=P), ACT.Copy).then_inc(s_e, 1)
                                if two and 1 <= n <= R:
                                    a = n - 1
                                    b = g * R + a
                                    act.wait_ge(s_h, 2 * b + 3)
                                    act.activation(h[:, a % 2, :], h[:, a % 2, :], ACT.Gelu).then_inc(s_gl, 1)
                                if two and 2 <= n:
                                    a = n - 2
                                    b = g * R + a
                                    act.wait_ge(s_t2, b + 3)
                                    act.wait_ge(s_m, b + 1)
                                    act.activation(q2T[:, a % 2, :, :], pt2[:, :].rearrange("p (k n) -> p k n", n=P), ACT.Copy).then_inc(s_e2, 1)

        def experts(layer, tag):
            top = 2 if layer == 3 else 1
            SLOTS = slots_of[layer]
            pre = "L%d_ffn_" % layer
            gcol = gate[:, 4 + layer:5 + layer]
            rows_in, rows_out = rows_of[layer]
            whole = ExitStack()
            with whole:
                S = lambda n: sem(n + tag, whole)
                xtok = sb("xtok" + tag, [P, B, D], F32, whole)
                pos = sb("pos" + tag, [P, top, B], mybir.dt.uint32, whole)
                coef = sb("coef" + tag, [P, top, B], F32, whole)
                first = sb("first" + tag, [P, 16], I32, whole)
                gw = sb("gw" + tag, [P, DK, E], F32, whole)
                if layer == 1:
                    wred, wg = sb("wred", [P, DK, 16], F32, whole), sb("wg", [E, 16], F32, whole)
                s_gw = S("gate_weights_loaded")
                s_w = [S("weights_even_loaded"), S("weights_odd_loaded")]
                w1 = sb("w1" + tag, [P, 2, DK, F], F32, whole)
                w3 = sb("w3" + tag, [P, 2, DK, F], F32, whole) if layer == 3 else None
                w2 = sb("w2" + tag, [P, 2, FC, D], F32, whole)
                w1d = t[pre + "w1"].rearrange("e (k p) n -> e p k n", p=P)
                w2d = t[pre + "w2"].rearrange("e (c p) n -> e p c n", p=P)
                w3d = t[pre + "w3"].rearrange("e (k p) n -> e p k n", p=P) if layer == 3 else None
                NW = 3 if layer == 3 else 2

                def load_weights(eng, e, j):
                    def of(d):
                        return d[ds(e, 1)].rearrange("a p k n -> (a p) k n")
                    eng.dma_start(w1[:, j, :, :], of(w1d)).then_inc(s_w[j], 16)
                    eng.dma_start(w2[:, j, :, :], of(w2d)).then_inc(s_w[j], 16)
                    if layer == 3:
                        eng.dma_start(w3[:, j, :, :], of(w3d)).then_inc(s_w[j], 16)

                st = ExitStack()
                with st:
                    with nc.Block() as block:
                        norm_transposed(block, st, tag, xtok)

                        @block.sync
                        def _(sp):
                            if layer == 1:
                                sp.dma_start(wred[:, :, :], t[pre + "w_red"].rearrange("(k p) n -> p k n", p=P)).then_inc(s_gw, 16)
                                sp.dma_start(wg[:, :], t[pre + "wg"]).then_inc(s_gw, 16)
                            else:
                                sp.dma_start(gw[:, :, :], t[pre + "gate_w"].rearrange("(k p) n -> p k n", p=P)).then_inc(s_gw, 16)
                            load_weights(sp, 0, 0)
                            sp.wait_ge(s_zero[layer], 32)

                st = ExitStack()
                with st:
                    R = lambda n: sem(n + tag, st)
                    T = lambda n, shape, dt=F32: sb(n + tag, shape, dt, st)
                    lgT = T("lgT", [E, B * P])
                    lg = T("lg", [P, B, E])
                    pr = T("pr", [P, B, E])
                    prs = T("prs", [P, top, B, E])
                    oh = T("oh", [P, top, B, E])
                    eq = T("eq", [P, B, E])
                    tok = T("tok", [P, 8, B])
                    pref = T("pref", [P, E])
                    low = T("low", [P, P])
                    chosen = T("chosen", [P, B, E])
                    cnt = T("cnt", [P, E, B])
                    run = T("run", [P, E, B])
                    full = T("full", [P, B, E])
                    ends = T("ends", [P, E + 1])
                    slot = T("slot", [P, 6, E])
                    firstf = T("firstf", [P, 16])
                    pos_f = T("pos_f", [P, top, B])
                    pl = [st.enter_context(nc.psum_tensor(f"pl{i}{tag}", [P, 512], F32)) for i in range(4)]
                    s_c, s_l, s_le, s_lt, s_d, s_mx, s_ex, s_oh, s_rk, s_pos, s_sc = (
                        R(n) for n in ("constants_ready", "logits_turned_ready", "logits_evacuated", "logits_ready",
                                       "dve_step", "max_subtracted", "exp_done", "choices_ready", "ranks_ready", "rows_known", "tokens_scattered"))
                    if layer == 1:
                        wredT = T("wredT", [16, DK, P])
                        wgn = T("wgn", [E, 16])
                        wgs = T("wgs", [E, 8])
                        sq = T("sq", [E, 16])
                        wgT = T("wgT", [16, E])
                        s_g1, s_g2, s_g3 = R("gate_parts_turned"), R("gate_parts_ready"), R("norm_root")

                    with nc.Block() as block:
                        @block.gpsimd
                        def _(pool):
                            pool.iota(pref[:, :], pattern=[[-1, E]], base=E, channel_multiplier=0, allow_small_or_imprecise_dtypes=True).then_inc(s_c, 1)
                            pool.affine_select(out=low[:, :], in_=ones[:, 0:P], compare_op=ALU.is_gt, fill=0.0, base=0,
                                               pattern=[[1, P]], channel_multiplier=-1).then_inc(s_c, 1)
                            pool.memset(ends[:, :], 0.0).then_inc(s_c, 1)
                            pool.memset(firstf[:, :], 0.0).then_inc(s_c, 1)
                            if layer == 1:
                                pool.wait_ge(s_g3, 1)
                                pool.tensor_tensor(wgs[:, 1:2], wgs[:, 0:1], wgs[:, 7:8], ALU.pow).then_inc(s_g3, 1)
                            pool.wait_ge(s_pos, 1)
                            for c in range(top):
                                for b in range(B):
                                    pool.indirect_dma_start(rows_in, bass.IndirectOffsetOnAxis(ap=pos[:, c, b:b + 1], axis=0),
                                                            xtok[:, b, :], None).then_inc(s_sc, 16)
                            pool.wait_ge(s_sc, 16 * top * B)

                        @block.tensor
                        def _(pe):
                            pe.wait_ge(s_c, 4)
                            if layer == 1:
                                pe.wait_ge(s_gw, 32)
                                for k in range(DK):
                                    pe.transpose(pl[0][0:16, k * P:(k + 1) * P], wred[:, k, :], ident[:, :])
                                pe.wait_ge(s_g3, 3)
                                pe.transpose(pl[1][0:16, 0:E], wgn[:, :], ident[0:E, 0:E]).then_inc(s_g1, 1)
                                pe.wait_ge(s_g2, 2)
                                for k in range(DK):
                                    m = pe.matmul(pl[2 + k][:, 0:E], wredT[:, k, :], wgT[:, :], start=True, stop=True)
                                m.then_inc(s_g1, 1)
                                pe.wait_ge(s_g2, 4)
                            else:
                                pe.wait_ge(s_gw, 16)
                            for g in range(NG):
                                if g >= 2:
                                    pe.wait_ge(s_le, g - 1)
                                for k in range(DK):
                                    m = pe.matmul(pl[g % 2][0:E, :], gw[:, k, :], xnT[:, k, g * GT:(g + 1) * GT], start=(k == 0), stop=(k == DK - 1))
                                m.then_inc(s_l, 1)
                            pe.wait_ge(s_le, NG)
                            for b in range(B):
                                m = pe.transpose(pl[2][:, b * E:(b + 1) * E], lgT[:, b * P:(b + 1) * P], ident[0:E, 0:E])
                            m.then_inc(s_lt, 1)
                            pe.wait_ge(s_oh, 1)
                            ch = chosen[:, :, :].rearrange("p b e -> p (b e)")
                            pe.matmul(pl[0][:, 0:P], low[:, :], ch, start=True, stop=True)
                            pe.matmul(pl[1][:, 0:P], ones[:, 0:P], ch, start=True, stop=True).then_inc(s_rk, 1)

                        @block.scalar
                        def _(act):
                            act.wait_ge(s_mx, 1)
                            act.activation(pr[:, :, :], lg[:, :, :], ACT.Exp).then_inc(s_ex, 1)

                        @block.vector
                        def _(v):
                            n = [0]

                            def step(ins):
                                ins.then_inc(s_d, 1)
                                n[0] += 1
                                v.wait_ge(s_d, n[0])

                            V = nc.vector
                            v.wait_ge(s_c, 4)
                            if layer == 1:
                                v.wait_ge(s_gw, 32)
                                step(V.tensor_tensor(sq[:, :], wg[:, :], wg[:, :], ALU.mult))
                                step(V.memset(wgs[:, 7:8], 0.5))
                                V.tensor_reduce(wgs[:, 0:1], sq[:, :], AX.X, ALU.add).then_inc(s_g3, 1)
                                v.wait_ge(s_g3, 2)
                                step(V.tensor_scalar(wgs[:, 2:3], wgs[:, 1:2], 1e-4, None, ALU.max))
                                step(V.reciprocal(wgs[:, 3:4], wgs[:, 2:3]))
                                V.tensor_scalar(wgn[:, :], wg[:, :], wgs[:, 3:4], None, ALU.mult).then_inc(s_g3, 1)
                                v.wait_ge(s_g1, 1)
                                V.tensor_copy(wredT[:, :, :], pl[0][0:16, 0:D].rearrange("p (k n) -> p k n", n=P)).then_inc(s_g2, 1)
                                V.tensor_copy(wgT[:, :], pl[1][0:16, 0:E]).then_inc(s_g2, 1)
                                v.wait_ge(s_g1, 2)
                                for k in range(DK):
                                    V.tensor_copy(gw[:, k, :], pl[2 + k][:, 0:E]).then_inc(s_g2, 1)
                            for g in range(NG):
                                v.wait_ge(s_l, g + 1)
                                V.tensor_copy(lgT[:, g * GT:(g + 1) * GT], pl[g % 2][0:E, :]).then_inc(s_le, 1)
                            v.wait_ge(s_lt, 1)

                            def per_token(ap):
                                return ap.unsqueeze(2).to_broadcast([P, B, E])

                            pl3 = pl[2][:, 0:B * E].rearrange("p (b e) -> p b e", e=E)
                            step(V.tensor_reduce(tok[:, 0, :], pl3, AX.X, ALU.max))
                            V.tensor_tensor(lg[:, :, :], pl3, per_token(tok[:, 0, :]), ALU.subtract).then_inc(s_mx, 1)
                            v.wait_ge(s_ex, 1)
                            step(V.tensor_reduce(tok[:, 1, :], pr[:, :, :], AX.X, ALU.add))
                            step(V.reciprocal(tok[:, 2, :], tok[:, 1, :]))
                            step(V.tensor_tensor(prs[:, 0, :, :], pr[:, :, :], per_token(tok[:, 2, :]), ALU.mult))
                            prefb = pref[:, :].unsqueeze(1).to_broadcast([P, B, E])
                            for c in range(top):
                                best, code = tok[:, 3 + c, :], tok[:, 5 + c, :]
                                if c:
                                    step(V.scalar_tensor_tensor(out=prs[:, 1, :, :], in0=oh[:, 0, :, :], scalar=-4.0, in1=prs[:, 0, :, :], op0=ALU.mult, op1=ALU.add))
                                step(V.tensor_reduce(best, prs[:, c, :, :], AX.X, ALU.max))
                                step(V.tensor_tensor(eq[:, :, :], prs[:, c, :, :], per_token(best), ALU.is_equal))
                                step(V.tensor_tensor(eq[:, :, :], eq[:, :, :], prefb, ALU.mult))
                                step(V.tensor_reduce(code, eq[:, :, :], AX.X, ALU.max))
                                step(V.tensor_tensor(oh[:, c, :, :], eq[:, :, :], per_token(code), ALU.is_equal))
                            if top == 2:
                                V.tensor_tensor(chosen[:, :, :], oh[:, 0, :, :], oh[:, 1, :, :], ALU.add).then_inc(s_oh, 1)
                                step(V.tensor_tensor(tok[:, 7, :], tok[:, 3, :], tok[:, 4, :], ALU.add))
                                step(V.reciprocal(tok[:, 0, :], tok[:, 7, :]))
                                for c in range(top):
                                    step(V.scalar_tensor_tensor(out=coef[:, c, :], in0=tok[:, 3 + c, :], scalar=gcol, in1=tok[:, 0, :], op0=ALU.mult, op1=ALU.mult))
                            else:
                                V.tensor_copy(chosen[:, :, :], oh[:, 0, :, :]).then_inc(s_oh, 1)
                                step(V.tensor_scalar(coef[:, 0, :], tok[:, 3, :], gcol, None, ALU.mult))
                            v.wait_ge(s_rk, 1)
                            counts = pl[1][:, 0:P].rearrange("p (b e) -> p e b", e=E)
                            step(V.tensor_copy(cnt[:, :, :], counts))
                            step(V.tensor_tensor_scan(run[:, :, :].rearrange("p e b -> p (e b)"), ones[:, 0:P], cnt[:, :, :].rearrange("p e b -> p (e b)"), 0.0, ALU.mult, ALU.add))
                            step(V.tensor_copy(ends[:, 1:E + 1], run[:, :, B - 1]))
                            step(V.tensor_tensor(slot[:, 0, :], ends[:, 1:E + 1], ends[:, 0:E], ALU.subtract))
                            step(V.tensor_scalar(slot[:, 1, :], slot[:, 0, :], 1.0 / P, 0.5 - 0.5 / P, ALU.mult, ALU.add))
                            step(V.tensor_scalar(slot[:, 2, :], slot[:, 1, :], ROUND, ROUND, ALU.add, ALU.subtract))
                            step(V.tensor_scalar(slot[:, 3, :], slot[:, 2, :], 1.0, None, ALU.max))
                            step(V.tensor_tensor_scan(firstf[:, 2:E + 2], ones[:, 0:E], slot[:, 3, :], 0.0, ALU.mult, ALU.add))
                            step(V.tensor_copy(first[:, :], firstf[:, :]))
                            step(V.scalar_tensor_tensor(out=slot[:, 4, :], in0=firstf[:, 1:E + 1], scalar=float(P), in1=ends[:, 0:E], op0=ALU.mult, op1=ALU.subtract))
                            step(V.tensor_tensor(run[:, :, :], run[:, :, :], cnt[:, :, :], ALU.subtract))
                            step(V.tensor_tensor(full[:, :, :], pl[0][:, 0:P].rearrange("p (b e) -> p b e", e=E), run[:, :, :].rearrange("p e b -> p b e"), ALU.add))
                            step(V.tensor_tensor(full[:, :, :], full[:, :, :], slot[:, 4, :].unsqueeze(1).to_broadcast([P, B, E]), ALU.add))
                            for c in range(top):
                                step(V.tensor_tensor(oh[:, c, :, :], oh[:, c, :, :], full[:, :, :], ALU.mult))
                                step(V.tensor_reduce(pos_f[:, c, :], oh[:, c, :, :], AX.X, ALU.add))
                            V.tensor_copy(pos[:, :, :], pos_f[:, :, :]).then_inc(s_pos, 1)

                st = ExitStack()
                with st:
                    R = lambda n: sem(n + tag, st)
                    T = lambda n, shape, dt=F32: sb(n + tag, shape, dt, st)
                    xg = T("xg", [P, D])
                    xgT = T("xgT", [P, DK, P])
                    hT = T("hT", [P, FC, P])
                    y = T("y", [P, D])
                    b1e = T("b1e", [P, 2, FC]) if layer == 1 else None
                    b2 = T("b2", [1, E, D]) if layer == 1 else None
                    b2e = T("b2e", [1, 2, D]) if layer == 1 else None
                    sg = T("sg", [P, 2, 512]) if layer == 3 else None
                    yg = T("yg", [P, 4, D])
                    pb = lambda n, w: st.enter_context(nc.psum_tensor(n + tag, [P, w], F32))
                    ph = [pb(f"ph{i}", 512) for i in range(2)]
                    ph3 = [pb(f"ph3{i}", 512) for i in range(2)] if layer == 3 else None
                    px, py = pb("px", D), pb("py", D)
                    s_xg, s_tn, s_xT = R("tokens_loaded"), R("tokens_turned"), R("turned_evacuated")
                    s_h, s_act, s_hT = R("hidden_sums"), R("activated"), R("hidden_ready")
                    s_y, s_ye, s_st, s_yf = R("slot_done"), R("y_evacuated"), R("y_stored"), R("y_free")
                    s_b, s_be = R("bias2_loaded"), R("bias_ready")
                    s_yg = [R(f"gathered{i}") for i in range(4)]
                    s_up = R("tokens_updated")

                    def slot_range(eng, e):
                        a = eng.value_load(first[0:1, ds(e + 1, 1)], min_val=0, max_val=SLOTS - 1)
                        b = eng.value_load(first[0:1, ds(e + 2, 1)], min_val=1, max_val=SLOTS)
                        return a, b

                    def total(eng):
                        return eng.value_load(first[0:1, E + 1:E + 2], min_val=E, max_val=SLOTS)

                    with nc.Block() as block:
                        @block.sync
                        def _(sp):
                            if layer == 1:
                                sp.dma_start(b2[:, :, :], t[pre + "b2"].rearrange("(a e) n -> a e n", a=1)).then_inc(s_b, 16)

                        @block.gpsimd
                        def _(pool):
                            pool.sem_inc(s_yf, 1)
                            pool.dma_start(xg[:, :], rows_in[0:P, :]).then_inc(s_xg, 16)
                            pool.wait_ge(s_tn, 1)
                            pool.dma_start(xg[:, :], rows_in[P:2 * P, :]).then_inc(s_xg, 16)
                            slots = total(pool)
                            with pool.Fori(1, slots) as s:
                                pool.wait_ge(s_tn, s + 1)
                                pool.dma_start(xg[:, :], rows_in[ds((s + 1) * P, P), :]).then_inc(s_xg, 16)
                                pool.wait_ge(s_ye, s + 1)
                                pool.dma_start(rows_out[ds((s - 1) * P, P), :], y[:, :]).then_inc(s_st, 16)
                                pool.wait_ge(s_st, s * 16)
                                pool.sem_inc(s_yf, 1)
                            pool.wait_ge(s_ye, slots + 1)
                            pool.dma_start(rows_out[ds((slots - 1) * P, P), :], y[:, :]).then_inc(s_st, 16)
                            pool.wait_ge(s_st, slots * 16)

                        @block.tensor
                        def _(pe):
                            def turn():
                                for k in range(DK):
                                    m = pe.transpose(px[:, k * P:(k + 1) * P], xg[:, k * P:(k + 1) * P], ident[:, :])
                                m.then_inc(s_tn, 1)

                            pe.sem_inc(s_y, 1)
                            pe.wait_ge(s_xg, 16)
                            turn()

                            def expert(r, j):
                                a, b = slot_range(pe, r * 2 + j)
                                with pe.Fori(a, b) as s:
                                    pe.wait_ge(s_w[j], (r + 1) * (16 * NW))
                                    if layer == 1:
                                        pe.wait_ge(s_be, r * 2 + j + 1)
                                    pe.wait_ge(s_xT, s + 1)
                                    for half in range(2):
                                        for w, bank in ((w1, ph), (w3, ph3))[:layer // 2 + 1]:
                                            for c in range(4):
                                                f = (4 * half + c) * P
                                                for k in range(DK):
                                                    m = pe.matmul(bank[half][:, c * P:(c + 1) * P], w[:, j, k, f:f + P], xgT[:, k, :], start=(k == 0), stop=(k == DK - 1))
                                            m.then_inc(s_h, 1)
                                    pe.wait_ge(s_xg, s * 16 + 32)
                                    turn()
                                    pe.wait_ge(s_ye, s + 1)
                                    for c in range(FC):
                                        if c % 4 == 0:
                                            pe.wait_ge(s_hT, s * 2 + c // 4 + 1)
                                        m = pe.matmul(py[:, :], hT[:, c, :], w2[:, j, c, :], start=(c == 0), stop=(c == FC - 1 and layer == 3))
                                    if layer == 1:
                                        m = pe.matmul(py[:, :], ones[0:1, 0:P], b2e[0:1, j, :], start=False, stop=True)
                                    m.then_inc(s_y, 1)

                            with pe.Fori(0, E // 2) as r:
                                for j in range(2):
                                    expert(r, j)

                        @block.scalar
                        def _(act):
                            if layer == 1:
                                act.wait_ge(s_b, 16)

                            def expert(r, j, load):
                                a, b = slot_range(act, r * 2 + j)
                                act.wait_ge(s_y, a + 1)
                                if load:
                                    load_weights(act, r * 2 + j + 1, 1 - j)
                                if layer == 1:
                                    act.activation(b1e[:, j, :], cols[:, ds(r * 16 + (32 + FC * j), FC)], ACT.Copy).then_inc(s_b, 1)
                                    act.activation(b2e[:, j, :], b2[0:1, ds(r * 2 + j, 1), :].rearrange("a e n -> a (e n)"), ACT.Copy).then_inc(s_be, 1)
                                    act.wait_ge(s_b, r * 2 + (j + 17))
                                with act.Fori(a, b) as s:
                                    for half in range(2):
                                        if layer == 1:
                                            act.wait_ge(s_h, s * 2 + half + 1)
                                            for c in range(4):
                                                m = act.activation(hT[:, 4 * half + c, :], ph[half][:, c * P:(c + 1) * P], ACT.Gelu, bias=b1e[:, j, 4 * half + c:4 * half + c + 1])
                                            m.then_inc(s_hT, 1)
                                        else:
                                            act.wait_ge(s_h, s * 4 + 2 * half + 1)
                                            act.activation(sg[:, half, :], ph[half][:, :], ACT.Silu).then_inc(s_act, 1)

                            with act.Fori(0, E // 2 - 1) as r:
                                for j in range(2):
                                    expert(r, j, True)
                            for j in range(2):
                                expert(E // 2 - 1, j, j == 0)

                        @block.vector
                        def _(v):
                            def take_tokens(n):
                                v.wait_ge(s_tn, n)
                                nc.vector.tensor_copy(xgT[:, :, :], px[:, :].rearrange("p (k n) -> p k n", n=P)).then_inc(s_xT, 1)

                            v.sem_inc(s_ye, 1)
                            take_tokens(1)
                            with v.Fori(0, total(v)) as s:
                                if layer == 3:
                                    for half in range(2):
                                        v.wait_ge(s_act, s * 2 + half + 1)
                                        v.wait_ge(s_h, s * 4 + 2 * half + 2)
                                        nc.vector.tensor_tensor(hT[:, 4 * half:4 * half + 4, :].rearrange("p c n -> p (c n)"), sg[:, half, :], ph3[half][:, :], ALU.mult).then_inc(s_hT, 1)
                                take_tokens(s + 2)
                                v.wait_ge(s_y, s + 2)
                                v.wait_ge(s_yf, s + 1)
                                nc.vector.tensor_copy(y[:, :], py[:, :]).then_inc(s_ye, 1)

                    with nc.Block() as block:
                        @block.sync
                        def _(sp):
                            if layer == 3:
                                for b in range(B):
                                    sp.wait_ge(s_up, top * (b + 1))
                                    sp.dma_start(out[b], x[:, b, :]).then_inc(s_out, 16)
                                sp.wait_ge(s_out, 16 * B)

                        @block.gpsimd
                        def _(pool):
                            for n in range(top * B):
                                c, b = n % top, n // top
                                if n >= 4:
                                    pool.wait_ge(s_up, n - 3)
                                pool.indirect_dma_start(yg[:, n % 4, :], None, rows_out,
                                                        bass.IndirectOffsetOnAxis(ap=pos[:, c, b:b + 1], axis=0)).then_inc(s_yg[n % 4], 16)

                        @block.vector
                        def _(v):
                            for n in range(top * B):
                                c, b = n % top, n // top
                                v.wait_ge(s_yg[n % 4], 16 * (n // 4 + 1))
                                if c:
                                    v.wait_ge(s_up, n)
                                nc.vector.scalar_tensor_tensor(out=x[:, b, :], in0=yg[:, n % 4, :], scalar=coef[:, c, b:b + 1], in1=x[:, b, :],
                                                               op0=ALU.mult, op1=ALU.add).then_inc(s_up, 1)
                                if c == top - 1 and layer == 1:
                                    v.wait_ge(s_up, n + 1)
                                    take_stats(b)

        def additive(tag):
            FB = 16
            UB = P // FB * DK
            POOLS = (1, 4, 6, 9, 12, 14)
            VECS = [i for i in range(UB) if i not in POOLS]
            RP, RV = 3, 5
            NEG = -1e30

            def place(i):
                return (1, POOLS.index(i)) if i in POOLS else (0, VECS.index(i))

            whole = ExitStack()
            with whole:
                S = lambda n: sem(n + tag, whole)
                T = lambda n, shape, dt=F32: sb(n + tag, shape, dt, whole)
                featT = T("featT", [P, DK, B * P])
                Ws, W = T("Ws", [P, DK, D]), T("W", [P, DK, D])
                vrow = T("vrow", [4, P])
                vcol = T("vcol", [P, 4])
                wsel = T("wsel", [P, DK, UB // DK, 32])
                wcb = T("wcb", [P, 2, D])
                bc = T("bc", [P, 2])
                s_w, s_v, s_vt, s_vc = S("weights_loaded"), S("small_loaded"), S("small_turned"), S("small_ready")
                s_z, s_w12 = S("selector_zero"), S("ternary_sources_loaded")
                s_pj, s_pe = S("projected"), S("projection_evacuated")

                st = ExitStack()
                with st:
                    with nc.Block() as block:
                        norm_transposed(block, st, tag)

                        @block.sync
                        def _(sp):
                            row = lambda a: a.rearrange("(c p) a -> (a c) p", p=P)
                            sp.dma_start(W[:, :, :], t["L2_xattn_W"].rearrange("(k p) n -> p k n", p=P)).then_inc(s_w, 16)
                            sp.dma_start(Ws[:, :, :], t["L2_xattn_Ws"].rearrange("(k p) n -> p k n", p=P)).then_inc(s_w, 16)
                            sp.dma_start(vrow[0:2, :], row(t["L2_xattn_w"])).then_inc(s_v, 16)
                            sp.dma_start(vrow[2:4, :], t["L2_xattn_b"].rearrange("a (c p) -> (a c) p", p=P)).then_inc(s_v, 16)
                            sp.dma_start(wcb[:, 0, :], t["L2_xattn_Wcw"].to_broadcast([P, D])).then_inc(s_v, 16)
                            sp.dma_start(wcb[:, 1, :], t["L2_xattn_Wcb"].to_broadcast([P, D])).then_inc(s_v, 16)
                            one = lambda a: a.rearrange("(a n) -> a n", a=1).to_broadcast([P, 1])
                            sp.dma_start(bc[:, 0:1], one(t["L2_xattn_bcw"])).then_inc(s_v, 16)
                            sp.dma_start(bc[:, 1:2], one(t["L2_xattn_bcb"])).then_inc(s_v, 16)
                            load_ternary(sp, s_w12)

                st = ExitStack()
                with st:
                    pv = st.enter_context(nc.psum_tensor("pv" + tag, [P, 512], F32))
                    pp = [st.enter_context(nc.psum_tensor(f"pp{i}{tag}", [P, 512], F32)) for i in range(4)]
                    tern_sums, tern_turns, tern_vector = ternary_weights(st, tag, s_w12)
                    with nc.Block() as block:
                        @block.tensor
                        def _(pe):
                            pe.wait_ge(s_v, 16 * 6)
                            pe.transpose(pv[:, 0:4], vrow[:, :], ident[0:4, 0:4]).then_inc(s_vt, 1)
                            pe.wait_ge(s_w, 32)
                            for g in range(NG):
                                for c in range(DK):
                                    if g >= 2:
                                        pe.wait_ge(s_pe, 2 * (g - 2) + c + 1)
                                    for k in range(DK):
                                        m = pe.matmul(pp[2 * (g % 2) + c][:, :], W[:, k, c * P:(c + 1) * P], xnT[:, k, g * GT:(g + 1) * GT],
                                                      start=(k == 0), stop=(k == DK - 1))
                                    m.then_inc(s_pj, 1)
                                if g == 0:
                                    tern_sums(pe)
                            tern_turns(pe)

                        @block.vector
                        def _(v):
                            nc.vector.memset(wsel[:, :, :, :], 0.0).then_inc(s_z, 1)
                            v.wait_ge(s_vt, 1)
                            nc.vector.tensor_copy(vcol[:, :], pv[:, 0:4]).then_inc(s_vc, 1)
                            v.wait_ge(s_z, 1)
                            v.wait_ge(s_vc, 1)
                            for c in range(DK):
                                for u in range(UB // DK):
                                    m = nc.vector.tensor_copy(wsel[:, c, u, u:u + 1], vcol[:, c:c + 1])
                            m.then_inc(s_vc, 1)
                            tern_vector(v)

                        @block.scalar
                        def _(act):
                            act.wait_ge(s_vc, 2)
                            for g in range(NG):
                                for c in range(DK):
                                    act.wait_ge(s_pj, 2 * g + c + 1)
                                    act.activation(featT[:, c, g * GT:(g + 1) * GT], pp[2 * (g % 2) + c][:, :], ACT.Identity, bias=vcol[:, 2 + c:3 + c]).then_inc(s_pe, 1)

                st = ExitStack()
                with st:
                    R = lambda n: sem(n + tag, st)
                    U = lambda n, shape, dt=F32: sb(n + tag, shape, dt, st)
                    flat = [w[:, :, :].rearrange("p k n -> p (k n)") for w in (wq, wk, wv, wo)] + [xnT[:, k, :] for k in range(DK)]
                    room = [f.rearrange("p (f k) -> p f k", k=P) for f in flat]
                    room += [U(f"th{i}", [P, FB, P])[:, :, :] for i in range(RV + RP - len(room))]
                    th = [room[:RV], room[RV:]]
                    ring = (RV, RP)
                    text_sb = U("text_sb", [P, 2 * DK * P])

                    def buf(i):
                        who, n = place(i)
                        return th[who][n % ring[who]]

                    def split(ap):
                        return ap.rearrange("p (j i) k -> p j i k", i=4)

                    def feat(c, b, u):
                        f = featT[:, c, ds(b * P, P)].rearrange("p (j f) -> p j f", j=4)[:, :, 4 * u:4 * u + 4]
                        return f.unsqueeze(3).to_broadcast([P, 4, 4, P])

                    def spread(text):
                        return text.unsqueeze(1).unsqueeze(1).to_broadcast([P, 4, 4, P])

                    cx = U("cx", [P, D])
                    rv, rho = U("rv", [P, 512]), U("rho", [P, P])
                    qm = U("qm", [P, P], I32)
                    qn = U("qn", [P, P])
                    rs, pr, pT = U("rs", [P, P]), U("pr", [P, P]), U("pT", [P, P])
                    nmx, sm = U("nmx", [P, 1]), U("sm", [P, 1])
                    dot, rsm, pre, ws = U("dot", [P, 2]), U("rsm", [P, 1]), U("pre", [P, 2]), U("ws", [P, 2])
                    sc2 = U("sc2", [P, 2])
                    junk = U("junk", [P, 2, D])
                    upd = U("upd", [P, 2, D])
                    pbk = lambda n: st.enter_context(nc.psum_tensor(n + tag, [P, 512], F32))
                    prho, pt2, ptx = pbk("prho"), pbk("pt2"), pbk("ptx")
                    ptxt = st.enter_context(nc.psum_tensor("ptxt" + tag, [P, 1024], F32))
                    s_sum = [R("vector_sums_ready"), R("gpsimd_sums_ready")]
                    s_th = R("tanh_ready")
                    s_use = [R("vector_unit_used"), R("gpsimd_unit_used")]
                    s_txt, s_tsb = R("text_projected"), R("text_copied")
                    s_rv, s_rho, s_qm, s_qn, s_rs = R("rho_evacuated"), R("rho_sorted"), R("mask_loaded"), R("mask_read"), R("rho_masked")
                    s_nm, s_p, s_t2, s_pT = R("nmax_ready"), R("probs_ready"), R("probs_turned"), R("probsT_ready")
                    s_cx, s_tx, s_d, s_pre, s_ws, s_up = R("text_loaded"), R("text_mixed"), R("dot_step"), R("pre_ready"), R("ws_ready"), R("tile_step")

                    V_AT = {4: 0, 8: 1, 11: 2, 14: 3}
                    P_AT = {5: 0, 8: 1}
                    A_AT = {0: 0, 5: 1, 11: 2}

                    with nc.Block() as block:
                        @block.sync
                        def _(sp):
                            cd = t["ctx_1024"]
                            with sp.Fori(0, B) as b:
                                sp.wait_ge(s_qn, b + 1)
                                sp.dma_start(qm[:, :], t["mask_BxS2_ik0"][ds(b, 1), :].to_broadcast([P, P])).then_inc(s_qm, 16)
                                sp.wait_ge(s_tx, b + 1)
                                sp.dma_start(cx[:, :], cd[ds(b, 1)].rearrange("a s d -> (a s) d")).then_inc(s_cx, 16)
                                sp.wait_ge(s_rv, b + 1)
                                for j in range(4):
                                    sp.dma_start(rho[32 * j:32 * j + 32, :], rv[32 * j:32 * j + UB // DK, :].rearrange("u (i k) -> u i k", i=4)).then_inc(s_rho, 16)

                        @block.vector
                        def _(v):
                            V = nc.vector

                            def post(b, part):
                                if part == 0:
                                    v.wait_ge(s_qm, b * 16 + 16)
                                    V.tensor_scalar(qn[:, :], qm[:, :], -1.0, 1.0, ALU.mult, ALU.add).then_inc(s_qn, 1)
                                    v.wait_ge(s_qn, b + 2)
                                    v.wait_ge(s_rho, b * 64 + 64)
                                    V.scalar_tensor_tensor(out=rs[:, :], in0=qn[:, :], scalar=NEG, in1=rho[:, :], op0=ALU.mult, op1=ALU.add).then_inc(s_rs, 1)
                                    v.wait_ge(s_rs, b + 1)
                                    V.tensor_reduce(nmx[:, :], rs[:, :], AX.X, ALU.max, negate=True).then_inc(s_nm, 1)
                                elif part == 1:
                                    v.wait_ge(s_t2, b + 1)
                                    V.tensor_copy(pT[:, :], pt2[:, 0:P]).then_inc(s_pT, 1)
                                elif part == 2:
                                    v.wait_ge(s_tx, b + 2)
                                    for i in range(2):
                                        V.tensor_tensor_reduce(junk[:, i, :], ptx[:, 0:D], wcb[:, i, :], 1.0, 0.0, ALU.mult, ALU.add, dot[:, i:i + 1]).then_inc(s_d, 1)
                                    V.reciprocal(rsm[:, :], sm[:, :]).then_inc(s_d, 1)
                                    v.wait_ge(s_d, b * 4 + 3)
                                    V.tensor_scalar(sc2[:, :], dot[:, :], rsm[:, 0:1], None, ALU.mult).then_inc(s_d, 1)
                                    v.wait_ge(s_d, b * 4 + 4)
                                    V.tensor_tensor(pre[:, :], sc2[:, :], bc[:, :], ALU.add).then_inc(s_pre, 1)
                                else:
                                    v.wait_ge(s_ws, b + 1)
                                    xb = x[:, ds(b, 1), :].rearrange("p a c -> p (a c)")
                                    V.tensor_scalar(upd[:, 0, :], xb, mean[:, ds(b, 1)], rstd[:, ds(b, 1)], ALU.subtract, ALU.mult).then_inc(s_up, 1)
                                    v.wait_ge(s_up, b * 3 + 1)
                                    V.tensor_scalar(upd[:, 1, :], upd[:, 0, :], ws[:, 0:1], ws[:, 1:2], ALU.mult, ALU.add).then_inc(s_up, 1)
                                    v.wait_ge(s_up, b * 3 + 2)
                                    V.scalar_tensor_tensor(out=xb, in0=upd[:, 1, :], scalar=gate[:, 2:3], in1=xb, op0=ALU.mult, op1=ALU.add).then_inc(s_up, 1)
                                    v.wait_ge(s_up, b * 3 + 3)
                                    take_stats(b)

                            def batch(b, before):
                                v.wait_ge(s_txt, b + 1)
                                V.tensor_copy(text_sb[:, ds(b % 2 * (DK * P), DK * P)], ptxt[:, ds(b % 2 * 512, DK * P)]).then_inc(s_tsb, 1)
                                for i in range(UB):
                                    u, c = i // DK, i % DK
                                    who, n = place(i)
                                    if who == 0:
                                        v.wait_ge(s_use[0], b * len(VECS) + (n + 1))
                                        V.tensor_tensor(split(buf(i)), feat(c, b, u), spread(ptxt[:, ds(b % 2 * 512 + c * P, P)]), ALU.add).then_inc(s_sum[0], 1)
                                    if before is not None and i in V_AT:
                                        post(before, V_AT[i])

                            v.sem_inc(s_qn, 1)
                            batch(0, None)
                            with v.Fori(1, B) as b:
                                batch(b, b - 1)
                            for part in range(4):
                                post(B - 1, part)

                        @block.gpsimd
                        def _(pool):
                            with pool.Fori(0, B) as b:
                                pool.wait_ge(s_tsb, b + 1)
                                for n, i in enumerate(POOLS):
                                    u, c = i // DK, i % DK
                                    pool.wait_ge(s_use[1], b * len(POOLS) + (n + 1))
                                    pool.tensor_tensor(split(buf(i)), feat(c, b, u), spread(text_sb[:, ds(b % 2 * (DK * P) + c * P, P)]), ALU.add).then_inc(s_sum[1], 1)

                        @block.scalar
                        def _(act):
                            def post(b, part):
                                if part == 0:
                                    who = place(UB - 1)[0]
                                    act.wait_ge(s_use[who], b * (len(POOLS) if who else len(VECS)) + (len(POOLS) + RP if who else len(VECS) + RV))
                                    act.activation(rv[:, :], prho[:, :], ACT.Copy).then_inc(s_rv, 1)
                                elif part == 1:
                                    act.wait_ge(s_nm, b + 1)
                                    act.activation(pr[:, :], rs[:, :], ACT.Exp, bias=nmx[:, 0:1], accum_out=sm[:, 0:1]).then_inc(s_p, 1)
                                else:
                                    act.wait_ge(s_pre, b + 1)
                                    act.activation(ws[:, :], pre[:, :], ACT.Tanh).then_inc(s_ws, 1)

                            def batch(b, before):
                                for i in range(UB):
                                    who, n = place(i)
                                    act.wait_ge(s_sum[who], b * (len(POOLS) if who else len(VECS)) + (n + 1))
                                    act.activation(buf(i), buf(i), ACT.Tanh).then_inc(s_th, 1)
                                    if before is not None and i in A_AT:
                                        post(before, A_AT[i])

                            batch(0, None)
                            with act.Fori(1, B) as b:
                                batch(b, b - 1)
                            for part in range(3):
                                post(B - 1, part)

                        @block.tensor
                        def _(pe):
                            pe.sem_inc(s_use[0], RV)
                            pe.sem_inc(s_use[1], RP)
                            pe.sem_inc(s_tx, 1)

                            def text(b):
                                for c in range(DK):
                                    for k in range(DK):
                                        m = pe.matmul(ptxt[:, ds(b % 2 * 512 + c * P, P)], Ws[:, k, c * P:(c + 1) * P], ctxT[:, k, ds(b * P, P)],
                                                      start=(k == 0), stop=(k == DK - 1))
                                m.then_inc(s_txt, 1)

                            def post(b, part):
                                if part == 0:
                                    pe.wait_ge(s_p, b + 1)
                                    pe.transpose(pt2[:, 0:P], pr[:, :], ident[:, :]).then_inc(s_t2, 1)
                                else:
                                    pe.wait_ge(s_pT, b + 1)
                                    pe.wait_ge(s_cx, b * 16 + 16)
                                    pe.matmul(ptx[:, 0:D], pT[:, :], cx[:, :], start=True, stop=True).then_inc(s_tx, 1)

                            def batch(b, before, last=False):
                                if before is not None:
                                    pe.wait_ge(s_rv, b)
                                for i in range(UB):
                                    u, c = i // DK, i % DK
                                    pe.wait_ge(s_th, b * UB + (i + 1))
                                    for j in range(4):
                                        m = pe.matmul(prho[32 * j:32 * j + 32, :], wsel[:, c, u, :], buf(i)[:, 4 * j:4 * j + 4, :],
                                                      start=(i == 0), stop=(i == UB - 1))
                                    m.then_inc(s_use[place(i)[0]], 1)
                                    if i == 2 and not last:
                                        text(b + 1)
                                    if before is not None and i in P_AT:
                                        post(before, P_AT[i])

                            text(0)
                            batch(0, None)
                            with pe.Fori(1, B - 1) as b:
                                batch(b, b - 1)
                            batch(B - 1, B - 2, last=True)
                            for part in range(2):
                                post(B - 1, part)

        setup()
        with nc.Block() as block:
            @block.tensor
            def _(pe):
                pe.wait_ge(s_w0, 64)
        attention(0, "_a0")
        semaphores_cleared()
        bitlinear(0, "_f0")
        semaphores_cleared()
        attention(1, "_a1")
        semaphores_cleared()
        experts(1, "_f1")
        semaphores_cleared()
        additive("_a2")
        semaphores_cleared()
        bitlinear(2, "_f2")
        semaphores_cleared()
        attention(3, "_a3")
        semaphores_cleared()
        experts(3, "_f3")


_SKIP = ("mask_BxS_ff1",)


def kernel(**inputs):
    import numpy as _np
    import concourse.bacc as _bacc
    from concourse.bass_utils import run_bass_kernel_spmd as _run

    nc = _bacc.Bacc("TRN2", target_bir_lowering=False, num_devices=1)
    arrays, aps = {}, {}
    for name, value in inputs.items():
        if name in _SKIP:
            continue
        a = _np.ascontiguousarray(value)
        arrays[f"in_{name}"] = a
        aps[name] = nc.dram_tensor(f"in_{name}", a.shape, mybir.dt.from_np(a.dtype), kind="ExternalInput").ap()
    out = nc.dram_tensor("out", (B, P, D), F32, kind="ExternalOutput").ap()
    build(nc, aps, out)
    r = _run(nc, [arrays], core_ids=[0])
    return r.results[0]["out"]
```
